# Optimizing a Trainium2 kernel written in Bass

```python
import numpy as np
import jax
import jax.numpy as jnp

def _softmax(x, axis=-1):
    return jax.nn.softmax(x, axis=axis)

def _gelu(x):
    return jax.nn.gelu(x, approximate=True)

def _silu(x):
    return jax.nn.silu(x)

def _sigmoid(x):
    return jax.nn.sigmoid(x)

def _layernorm(x, axis=-1, eps=1e-05):
    m = jnp.mean(x, axis=axis, keepdims=True)
    v = jnp.var(x, axis=axis, keepdims=True)
    return (x - m) / jnp.sqrt(v + eps)

def _scatter_add(tgt, idx, src, axis=0):
    return tgt.at[idx].add(src)

def _segment_sum(src, seg, n):
    return jax.ops.segment_sum(src, seg, n)
kernel_name = 'mk_vit_tower_postln_d1_tok_img512_r4_cf10a5'

def setup_inputs(seed: int=0):
    np.random.seed(seed)
    _w = jnp.asarray

    def _rec_inputs():
        import jax
        import jax.numpy as jnp
        _rk = jax.random.key(seed)
        x = -0.000190493 + 0.999948 * jax.random.normal(jax.random.fold_in(_rk, 1), (64, 2, 104, 104), jnp.float32)
        return x
    x = _rec_inputs()

    def _L0_tok_setup():
        import jax, jax.numpy as jnp
        import numpy as np
        HP = 4
        PATCH = 8
        EPS = 1e-07

        def _shifts(x):
            h, w = (x.shape[2], x.shape[3])
            pad2 = ((0, 0), (0, 0))
            left_up = jnp.pad(x[:, :, HP:, :w - HP], pad2 + ((0, HP), (HP, 0)))
            right_up = jnp.pad(x[:, :, HP:, HP:], pad2 + ((0, HP), (0, HP)))
            left_down = jnp.pad(x[:, :, :h - HP, :w - HP], pad2 + ((HP, 0), (HP, 0)))
            right_down = jnp.pad(x[:, :, :h - HP, HP:], pad2 + ((HP, 0), (0, HP)))
            return (left_up, right_up, left_down, right_down)
        key = jax.random.key(seed)
        k1, k2, k3, k4 = jax.random.split(key, 4)
        B, C, S = (128, 2, 104)
        embed_dim = 128
        x = jax.random.normal(k1, (B, C, S, S), dtype=jnp.float32)
        gamma = 1.0 + 0.05 * jax.random.normal(k2, (10, S, S), dtype=jnp.float32)
        beta = 0.05 * jax.random.normal(k3, (10, S, S), dtype=jnp.float32)
        W = 0.02 * jax.random.normal(k4, (embed_dim, 10, PATCH, PATCH), dtype=jnp.float32)
        b = jnp.zeros((embed_dim,), dtype=jnp.float32)
        return {'x': x, 'gamma': gamma, 'beta': beta, 'W': W, 'b': b}
    _L0_tok_all = _L0_tok_setup()
    _L0_tok_in = {k: v for k, v in _L0_tok_all.items() if k in ('gamma', 'beta', 'W', 'b')}
    del _L0_tok_all

    def _L0_attn_setup():
        import jax, jax.numpy as jnp
        import numpy as np
        B, L, C = (2, 256, 128)
        H, P = (8, 4)
        D = C // H
        LN_EPS = 1e-05

        def _layernorm(x, g, b):
            mu = jnp.mean(x, axis=-1, keepdims=True)
            var = jnp.mean((x - mu) ** 2, axis=-1, keepdims=True)
            return (x - mu) * jax.lax.rsqrt(var + LN_EPS) * g + b
        key = jax.random.key(seed)
        ks = jax.random.split(key, 12)
        s = 0.02
        inp = {'features': jax.random.normal(ks[0], (B, L, C), jnp.float32), 'coords': jax.random.normal(ks[1], (B, L, 3), jnp.float32), 'ln_g': jnp.ones((C,), jnp.float32), 'ln_b': jnp.zeros((C,), jnp.float32), 'wq': jax.random.normal(ks[2], (C, C), jnp.float32) * s, 'bq': jnp.zeros((C,), jnp.float32), 'wk': jax.random.normal(ks[3], (C, C), jnp.float32) * s, 'bk': jnp.zeros((C,), jnp.float32), 'wv': jax.random.normal(ks[4], (C, C), jnp.float32) * s, 'bv': jnp.zeros((C,), jnp.float32), 'wqp': jax.random.normal(ks[5], (C, H * P * 3), jnp.float32) * s, 'bqp': jnp.zeros((H * P * 3,), jnp.float32), 'wkp': jax.random.normal(ks[6], (C, H * P * 3), jnp.float32) * s, 'bkp': jnp.zeros((H * P * 3,), jnp.float32), 'wvp': jax.random.normal(ks[7], (C, H * P * 3), jnp.float32) * s, 'bvp': jnp.zeros((H * P * 3,), jnp.float32), 'wo': jax.random.normal(ks[8], (C, C), jnp.float32) * s, 'bo': jnp.zeros((C,), jnp.float32), 'pscale': jnp.full((H,), 1.0 / np.sqrt(P), jnp.float32)}
        return inp
    _L0_attn_all = _L0_attn_setup()
    _L0_attn_in = {k: v for k, v in _L0_attn_all.items() if k in ('coords', 'ln_g', 'ln_b', 'wq', 'bq', 'wk', 'bk', 'wv', 'bv', 'wqp', 'bqp', 'wkp', 'bkp', 'wvp', 'bvp', 'wo', 'bo', 'pscale')}
    del _L0_attn_all

    def _L0_ffn_setup():
        import jax, jax.numpy as jnp
        import numpy as np
        B, T, D = (4, 2048, 128)
        E, F, CAP = (8, 512, 1024)
        key = jax.random.key(seed)
        ks = jax.random.split(key, 6)
        s = 0.02
        return {'x': jax.random.normal(ks[0], (B, T, D), dtype=jnp.float32), 'Wr': jax.random.normal(ks[1], (D, E), dtype=jnp.float32) * s, 'W1': jax.random.normal(ks[2], (E, D, F), dtype=jnp.float32) * s, 'b1': jax.random.normal(ks[3], (E, F), dtype=jnp.float32) * s, 'W2': jax.random.normal(ks[4], (E, F, D), dtype=jnp.float32) * s, 'b2': jax.random.normal(ks[5], (E, D), dtype=jnp.float32) * s}
    _L0_ffn_all = _L0_ffn_setup()
    _L0_ffn_in = {k: v for k, v in _L0_ffn_all.items() if k in ('Wr', 'W1', 'b1', 'W2', 'b2')}
    del _L0_ffn_all
    return {'x': x, 'L0_tok_gamma': _L0_tok_in['gamma'], 'L0_tok_beta': _L0_tok_in['beta'], 'L0_tok_W': _L0_tok_in['W'], 'L0_tok_b': _L0_tok_in['b'], 'L0_attn_coords': _L0_attn_in['coords'], 'L0_attn_ln_g': _L0_attn_in['ln_g'], 'L0_attn_ln_b': _L0_attn_in['ln_b'], 'L0_attn_wq': _L0_attn_in['wq'], 'L0_attn_bq': _L0_attn_in['bq'], 'L0_attn_wk': _L0_attn_in['wk'], 'L0_attn_bk': _L0_attn_in['bk'], 'L0_attn_wv': _L0_attn_in['wv'], 'L0_attn_bv': _L0_attn_in['bv'], 'L0_attn_wqp': _L0_attn_in['wqp'], 'L0_attn_bqp': _L0_attn_in['bqp'], 'L0_attn_wkp': _L0_attn_in['wkp'], 'L0_attn_bkp': _L0_attn_in['bkp'], 'L0_attn_wvp': _L0_attn_in['wvp'], 'L0_attn_bvp': _L0_attn_in['bvp'], 'L0_attn_wo': _L0_attn_in['wo'], 'L0_attn_bo': _L0_attn_in['bo'], 'L0_attn_pscale': _L0_attn_in['pscale'], 'L0_ffn_Wr': _L0_ffn_in['Wr'], 'L0_ffn_W1': _L0_ffn_in['W1'], 'L0_ffn_b1': _L0_ffn_in['b1'], 'L0_ffn_W2': _L0_ffn_in['W2'], 'L0_ffn_b2': _L0_ffn_in['b2']}

def reference(x, L0_tok_gamma, L0_tok_beta, L0_tok_W, L0_tok_b, L0_attn_coords, L0_attn_ln_g, L0_attn_ln_b, L0_attn_wq, L0_attn_bq, L0_attn_wk, L0_attn_bk, L0_attn_wv, L0_attn_bv, L0_attn_wqp, L0_attn_bqp, L0_attn_wkp, L0_attn_bkp, L0_attn_wvp, L0_attn_bvp, L0_attn_wo, L0_attn_bo, L0_attn_pscale, L0_ffn_Wr, L0_ffn_W1, L0_ffn_b1, L0_ffn_W2, L0_ffn_b2):
    import jax
    import jax.numpy as jnp

    def _L0_tok_ref(x, gamma, beta, W, b):
        import jax, jax.numpy as jnp
        import numpy as np
        HP = 4
        PATCH = 8
        EPS = 1e-07

        def _shifts(x):
            h, w = (x.shape[2], x.shape[3])
            pad2 = ((0, 0), (0, 0))
            left_up = jnp.pad(x[:, :, HP:, :w - HP], pad2 + ((0, HP), (HP, 0)))
            right_up = jnp.pad(x[:, :, HP:, HP:], pad2 + ((0, HP), (0, HP)))
            left_down = jnp.pad(x[:, :, :h - HP, :w - HP], pad2 + ((HP, 0), (HP, 0)))
            right_down = jnp.pad(x[:, :, :h - HP, HP:], pad2 + ((HP, 0), (0, HP)))
            return (left_up, right_up, left_down, right_down)
        lu, ru, ld, rd = _shifts(x)
        concat = jnp.concatenate((x, lu, ru, ld, rd), axis=1)
        mean = jnp.mean(concat, axis=(1, 2, 3), keepdims=True)
        var = jnp.var(concat, axis=(1, 2, 3), keepdims=True)
        normed = (concat - mean) * jax.lax.rsqrt(var + EPS)
        normed = normed * gamma[None] + beta[None]
        y = jax.lax.conv_general_dilated(normed, W, window_strides=(PATCH, PATCH), padding='VALID', dimension_numbers=('NCHW', 'OIHW', 'NCHW'))
        y = y + b[None, :, None, None]
        B, E = (y.shape[0], y.shape[1])
        y = y.reshape(B, E, -1).transpose(0, 2, 1)
        return y

    def _L0_attn_ref(features, coords, ln_g, ln_b, wq, bq, wk, bk, wv, bv, wqp, bqp, wkp, bkp, wvp, bvp, wo, bo, pscale):
        import jax, jax.numpy as jnp
        import numpy as np
        B, L, C = (2, 256, 128)
        H, P = (8, 4)
        D = C // H
        LN_EPS = 1e-05

        def _layernorm(x, g, b):
            mu = jnp.mean(x, axis=-1, keepdims=True)
            var = jnp.mean((x - mu) ** 2, axis=-1, keepdims=True)
            return (x - mu) * jax.lax.rsqrt(var + LN_EPS) * g + b
        b, l, c = features.shape
        h = pscale.shape[0]
        d = c // h
        p = wqp.shape[1] // (h * 3)
        x = _layernorm(features, ln_g, ln_b)
        q_s = (x @ wq + bq).reshape(b, l, h, d).transpose(0, 2, 1, 3)
        k_s = (x @ wk + bk).reshape(b, l, h, d).transpose(0, 2, 1, 3)
        v_s = (x @ wv + bv).reshape(b, l, h, d).transpose(0, 2, 1, 3)
        q_p = (x @ wqp + bqp).reshape(b, l, h, p, 3).transpose(0, 2, 1, 3, 4)
        k_p = (x @ wkp + bkp).reshape(b, l, h, p, 3).transpose(0, 2, 1, 3, 4)
        logits_s = jnp.einsum('bhid,bhjd->bhij', q_s, k_s) * d ** (-0.5)
        dot = jnp.einsum('bhipk,bhjpk->bhij', q_p, k_p)
        qsq = jnp.sum(q_p * q_p, axis=(-1, -2))
        ksq = jnp.sum(k_p * k_p, axis=(-1, -2))
        pdist2 = qsq[..., :, None] + ksq[..., None, :] - 2.0 * dot
        logits = logits_s - pdist2 * pscale[None, :, None, None]
        attn = jax.nn.softmax(logits, axis=-1)
        out_s = jnp.einsum('bhij,bhjd->bhid', attn, v_s)
        out_s = out_s.transpose(0, 2, 1, 3).reshape(b, l, c)
        out = out_s @ wo + bo
        return out

    def _L0_ffn_ref(x, Wr, W1, b1, W2, b2):
        import jax, jax.numpy as jnp
        import numpy as np
        B, T, D = (4, 2048, 128)
        E, F, CAP = (8, 512, 1024)
        Bb, Tt, Dd = x.shape
        N = Bb * Tt
        C = min(CAP, N)
        x_flat = x.reshape(N, Dd)
        logits = x_flat @ Wr
        probs = jax.nn.softmax(logits, axis=0)
        vals, idx = jax.lax.top_k(probs.T, C)
        selected = x_flat[idx]
        h = jax.nn.gelu(jnp.einsum('ecd,edf->ecf', selected, W1) + b1[:, None, :], approximate=False)
        out_e = jnp.einsum('ecf,efd->ecd', h, W2) + b2[:, None, :]
        weighted = vals[..., None] * out_e
        output = jnp.zeros_like(x_flat).at[idx.reshape(-1)].add(weighted.reshape(-1, Dd))
        return output.reshape(Bb, Tt, Dd)
    h = _L0_tok_ref(x, L0_tok_gamma, L0_tok_beta, L0_tok_W, L0_tok_b)
    h = _layernorm(h + _L0_attn_ref(h, L0_attn_coords, L0_attn_ln_g, L0_attn_ln_b, L0_attn_wq, L0_attn_bq, L0_attn_wk, L0_attn_bk, L0_attn_wv, L0_attn_bv, L0_attn_wqp, L0_attn_bqp, L0_attn_wkp, L0_attn_bkp, L0_attn_wvp, L0_attn_bvp, L0_attn_wo, L0_attn_bo, L0_attn_pscale), axis=-1)
    h = _layernorm(h + _L0_ffn_ref(h, L0_ffn_Wr, L0_ffn_W1, L0_ffn_b1, L0_ffn_W2, L0_ffn_b2), axis=-1)
    return h

_drawn_inputs = setup_inputs


def setup_inputs(seed=0):
    import zlib

    import numpy as np

    out = dict(_drawn_inputs(seed))
    spreads = {'L0_tok_b': (0.0, 0.1),
     'L0_attn_ln_g': (1.0, 0.6),
     'L0_attn_ln_b': (0.0, 0.8),
     'L0_attn_bq': (0.0, 0.8),
     'L0_attn_bk': (0.0, 2.0),
     'L0_attn_bv': (0.0, 0.1),
     'L0_attn_bqp': (0.0, 0.8),
     'L0_attn_bkp': (0.0, 0.8),
     'L0_attn_bvp': (0.0, 0.1),
     'L0_attn_bo': (0.0, 0.1),
     'L0_attn_pscale': (0.5, 0.6)}
    factors = {'L0_attn_wq': 8.0,
     'L0_attn_wk': 8.0,
     'L0_attn_wqp': 8.0,
     'L0_attn_wkp': 8.0,
     'L0_ffn_Wr': 64.0,
     'L0_ffn_W1': 64.0,
     'L0_ffn_b1': 64.0,
     'L0_ffn_W2': 64.0,
     'L0_ffn_b2': 64.0}
    for name, (base, spread) in spreads.items():
        noise = np.random.default_rng([zlib.crc32(name.encode()), seed]).standard_normal(out[name].shape)
        drawn = base * np.exp(spread * noise) if base else spread * noise
        out[name] = jnp.asarray(drawn.astype(out[name].dtype))
    for name, factor in factors.items():
        out[name] = (out[name] * factor).astype(out[name].dtype)
    return out
```

```python
from contextlib import ExitStack

import numpy as np

import concourse.bass as bass
from concourse import mybir

ALU = mybir.AluOpType
ACT = mybir.ActivationFunctionType
F32 = mybir.dt.float32
U32 = mybir.dt.uint32
AX = mybir.AxisListType

NI, CH, SIDE, SHIFT, PATCH = 64, 2, 104, 4, 8
GRID = SIDE // PATCH
TOK = GRID * GRID
ZG = GRID + 1
ZT = ZG * ZG
XZ = TOK + ZT
VER = 5
KP = CH * PATCH * PATCH
E = 128
HEADS, DH, PP = 8, 16, 12
HT = (TOK + 1) // 2
TP = 2 * HT
NTOK = NI * TOK
UN = 4
NEXP, FF, CAP = 8, 512, 1024
R = 104
TOK_EPS, LN_EPS = 1e-7, 1e-5
NPIX = 10 * SIDE * SIDE
CHUNK = NTOK // 16
UNIT = 512
NBLK = UNIT // 128
KIND = "Internal"


SETUP = 5


def i_par(r, ahead):
    return (r + ahead) % 2


def tower_tokens(nc, ctx, A, h2_dram, lg_dram):

    def sb(name, shape):
        return ctx.enter_context(nc.sbuf_tensor(name, shape, F32))

    def sem(name):
        return ctx.enter_context(nc.semaphore(name))

    xz = sb("xz", [KP, NI * XZ])
    wt = sb("wt", [KP, VER, E])
    gam = sb("gam", [KP, VER, TOK])
    bet = sb("bet", [KP, VER, TOK])
    zwt = sb("zwt", [KP, ZT])
    npix = sb("npix", [KP, KP])
    ones = sb("ones", [KP, KP])
    ident = sb("ident", [KP, KP])
    selm = sb("selm", [KP, KP])
    cst = sb("cst", [KP, 4])
    col = sb("col", [KP, 12])
    tokb, lng, lnb, bv, bo = (col[:, i:i + 1] for i in range(5))
    bq, bk, psc = col[:, 5:7], col[:, 7:9], col[:, 9:11]
    wq = sb("wq", [KP, 2, KP])
    wk = sb("wk", [KP, 2, KP])
    wv = sb("wv", [KP, KP])
    wo = sb("wo", [KP, KP])
    wop = sb("wop", [KP, 2, KP])
    wr = sb("wr", [KP, NEXP])

    gmean = sb("gmean", [KP, TOK])
    gbias = sb("gbias", [KP, TOK])
    qscale = sb("qscale", [KP, 2])
    qbias = sb("qbias", [KP, 2])
    kbias = sb("kbias", [KP, 2])
    qraw = sb("qraw", [KP, 6])
    selk = sb("selk", [KP, 2, KP])
    obias = sb("obias", [KP, 1])
    mhalf = sb("mhalf", [KP, 4])

    zs = sb("zs", [KP, UN, ZT])
    part = sb("part", [KP, 4, 2])
    stat = sb("stat", [KP, 4, 2])
    ivar = sb("ivar", [KP, 4])
    istd = sb("istd", [KP, 4])
    inmr = sb("inmr", [KP, 4])
    tick = sb("tick", [1, 1])
    wrc = sb("wrc", [KP, NEXP])
    vtot = sb("vtot", [KP, 1])
    gx = sb("gx", [KP, 2, VER, TP])
    tb = sb("tb", [KP, TOK])
    yT = sb("yT", [KP, UN, TP])
    st6 = sb("st6", [HT, 2, 6])
    mv = sb("mv", [HT, 2, 2])
    ve = sb("ve", [HT, 2])
    rs = sb("rs", [HT, 2])
    x = sb("x", [HT, 2, E])
    xT = sb("xT", [KP, 2, TP])
    qT = sb("qT", [KP, 2, 2, TP])
    kT = sb("kT", [KP, 2, 2, TP])
    ksq = sb("ksq", [KP, 2, TP])
    q2 = sb("q2", [KP, 2, TP])
    va = sb("va", [HT, 2, 2, HEADS, 32])
    mp = sb("mp", [HT, 2, 2, 2, 4, 32])
    pT = sb("pT", [HT, 2, 4, 2, TP])
    osum = sb("osum", [KP, 2, TP])
    oinv = sb("oinv", [KP, 2, TP])
    oT = sb("oT", [KP, 2, TP])
    sT = sb("sT", [KP, TP])
    st6b = sb("st6b", [HT, 2, 6])
    mvb = sb("mvb", [HT, 2, 2])
    veb = sb("veb", [HT, 2])
    rsb = sb("rsb", [HT, 2])
    h2 = sb("h2", [HT, UN, 2, E])
    lg = sb("lg", [HT, UN, 2, NEXP])

    ring = ctx.enter_context(nc.psum_tensor("ring", [KP, 4, 512], F32))
    bank = [ctx.enter_context(nc.psum_tensor(f"bank{i}", [KP, 512], F32)) for i in range(4, 8)]
    b4, b5, b6, b7 = bank

    s_c = sem("s_consts")
    s_ld = [sem(f"s_loaded{r}") for r in range(UN)]
    s_set = sem("s_setup")
    s_sps = sem("s_setup_psum")
    s_fill = sem("s_filled")
    s_zs = sem("s_zs")
    s_pt = sem("s_part")
    s_stp = sem("s_stat_psum")
    s_st = sem("s_stat")
    s_iv = sem("s_ivar")
    s_is = sem("s_istd")
    s_nm = sem("s_inmr")
    s_gx = sem("s_gx")
    s_cv = sem("s_conv")
    s_tb = sem("s_tb")
    s_y = sem("s_y")
    s_ht = sem("s_h_turned")
    s_hb = sem("s_h_stats")
    s_hr = sem("s_h_rstd")
    s_x = sem("s_x")
    s_xt = sem("s_x_turned")
    s_xT = sem("s_xT")
    s_q = sem("s_q_psum")
    s_qe = sem("s_q")
    s_k = sem("s_k_psum")
    s_sq = sem("s_ksq")
    s_kk = sem("s_k_whole")
    s_ke = sem("s_k")
    s_v = sem("s_v_psum")
    s_ve = sem("s_v")
    s_S = sem("s_scores")
    s_m = sem("s_max")
    s_mt = sem("s_max_turned")
    s_q2 = sem("s_q_less_max")
    s_ST = sem("s_scoresT")
    s_e = sem("s_exp")
    s_pv = sem("s_pv")
    s_os = sem("s_osum")
    s_oi = sem("s_oinv")
    s_on = sem("s_o")
    s_wo = sem("s_wo")
    s_s = sem("s_sum")
    s_sb = sem("s_s_turned")
    s_sn = sem("s_s_stats")
    s_sr = sem("s_s_rstd")
    s_h2 = sem("s_h2")
    s_out = [sem(f"s_stored{r}") for r in range(UN)]

    consts = [(wt, "w"), (gam, "gamma"), (bet, "beta"), (zwt, "zwt"), (npix, "npix"), (ones, "ones"),
              (ident, "ident"), (selm, "selm"), (cst, "cst"), (wr, "wr"), (wq, "wq"), (wk, "wk"), (wv, "wv"),
              (wo, "wo"), (wop, "wop")]
    columns = ("tok_b", "ln_g", "ln_b", "bv", "bo", "bq", "bk", "ps")
    NCONST = len(consts) + len(columns)
    NG = NI // UN

    def w(eng, s, v):
        if isinstance(v, int) and v <= 0:
            return
        eng.wait_ge(s, v)

    def pipeline(eng, body):
        for r in range(UN):
            body(-1, r)
        with eng.Fori(0, NG - 1) as q:
            for r in range(UN):
                body(q, r)
        for r in range(UN):
            body(NG - 1, r)

    def stages(q, r):
        if not isinstance(q, int):
            return True, True, True, True, True
        b = q * UN + r
        return b >= 0, 0 <= b + 1 < NI, 0 <= b + 2 < NI, 0 <= b + 3 < NI, q + 1 < NG

    block = ctx.enter_context(nc.Block())

    @block.sync
    def _(sp):
        at = 0
        for n in columns:
            sp.dma_start(col[:, at:at + A[n].shape[1]], A[n]).then_inc(s_c, 16)
            at += A[n].shape[1]

        def load(q, r):
            w(sp, s_ld[r], q * 16)
            at = (q * UN + r) * XZ
            sp.dma_start(xz[:, bass.ds(at, XZ)], A["xz"][:, bass.ds(at, XZ)]).then_inc(s_ld[r], 16)

        def store(q, r):
            first = (q * UN + r) * TOK
            sp.wait_ge(s_h2, q * UN + r + 1)
            for t, (a, n) in enumerate(((first, HT), (first + HT, HT - 1))):
                sp.dma_start(h2_dram[bass.ds(a, n), :], h2[0:n, r, t, :]).then_inc(s_out[r], 16)
                sp.dma_start(lg_dram[bass.ds(a, n), :], lg[0:n, r, t, :]).then_inc(s_out[r], 16)

        for r in range(UN):
            load(0, r)
        for t, n in consts:
            sp.dma_start(t[:], A[n]).then_inc(s_c, 16)
        for r in range(UN):
            load(1, r)
        with sp.Fori(0, NG - 2) as q:
            for r in range(UN):
                load(q + 2, r)
            for r in range(UN):
                store(q, r)
        for q in (NG - 2, NG - 1):
            for r in range(UN):
                store(q, r)
        for r in range(UN):
            sp.wait_ge(s_out[r], NG * 64)

    @block.gpsimd
    def _(pool):
        for t, v in ((gx[:, :, :, TOK:TP], 0.0), (yT[:, :, TOK:TP], 0.0), (mp[:], 0.0), (va[:, :, :, :, DH:32], 1.0),
                     (mhalf[:], -0.5)):
            nc.gpsimd.memset(t, v).then_inc(s_fill, 1)
        pool.wait_ge(s_fill, 5)
        pool.wait_ge(s_c, 16 * NCONST)

        def gamma(i, q, r):
            pool.wait_ge(s_ld[r], (q + 1) * 16)
            w(pool, s_cv, i - 1)
            o = gx[:, r % 2, :, 0:TOK].rearrange("p v (a b) -> p v a b", b=GRID)
            px = xz[:, bass.ds(i * XZ, TOK)].rearrange("p (a b) -> p a b", b=GRID)
            pz = xz[:, bass.ds(i * XZ + TOK, ZT)].rearrange("p (a b) -> p a b", b=ZG)
            gm = gam[:].rearrange("p v (a b) -> p v a b", b=GRID)
            nc.gpsimd.tensor_tensor(o[:, 0], px, gm[:, 0], ALU.mult)
            for v, (dy, dx) in enumerate(((1, 0), (1, 1), (0, 0), (0, 1))):
                ins = nc.gpsimd.tensor_tensor(o[:, v + 1], pz[:, dy:dy + GRID, dx:dx + GRID], gm[:, v + 1], ALU.mult)
            ins.then_inc(s_gx, 1)

        def body(q, r):
            last, mid, first, more, group = stages(q, r)
            b = q * UN + r
            if first:
                pool.wait_ge(s_hb, 3 * (b + 2) + 3)
                nc.gpsimd.tensor_tensor(rs[:], ve[:], mhalf[0:HT, 0:2], ALU.pow).then_inc(s_hr, 1)
            if more:
                gamma(b + 3, q + (r + 3) // UN, (r + 3) % UN)
            if group and r == 1:
                pool.wait_ge(s_iv, 2 * (q + 2))
                nc.gpsimd.tensor_tensor(istd[:], ivar[:], mhalf[:], ALU.pow).then_inc(s_is, 1)
            if last:
                pool.wait_ge(s_sn, 3 * b + 3)
                nc.gpsimd.tensor_tensor(rsb[:], veb[:], mhalf[0:HT, 0:2], ALU.pow).then_inc(s_sr, 1)

        pipeline(pool, body)

    @block.tensor
    def _(pe):
        mm = nc.tensor.matmul
        pe.wait_ge(s_c, 16 * NCONST)
        for c, t in enumerate((wq[:, 0, :], wq[:, 1, :], wk[:, 0, :], wk[:, 1, :], wv[:])):
            mm(b4[:, c:c + 1], t, lnb, start=True, stop=True)
        for o, t in ((b5, gam), (b6, bet)):
            for v in range(VER):
                mm(o[:, 0:TOK], wt[:, v, :], t[:, v, :], start=(v == 0), stop=(v == VER - 1))
        mm(b7[:, 0:NEXP], ones[:], wr[:], start=True, stop=True).then_inc(s_sps, 1)
        pe.wait_ge(s_set, 3)
        mm(b4[:, 8:9], wo[:], vtot[:], start=True, stop=True).then_inc(s_sps, 1)
        pe.wait_ge(s_set, SETUP)
        pe.wait_ge(s_fill, 5)

        def half(t):
            return slice(t * HT, t * HT + HT)

        def body(q, r):
            last, mid, first, more, group = stages(q, r)
            b = q * UN + r
            i, j, k = b, b + 1, b + 2
            if last:
                pe.wait_ge(s_m, 2 * i + 2)
                w(pe, s_xT, i + 2 if first else NI)
                for G in range(2):
                    for t in range(2):
                        ins = nc.tensor.transpose(b7[:, G * TP + t * HT:G * TP + t * HT + HT],
                                                  mp[:, i_par(r, 0), t, G].rearrange("p g c -> p (g c)"),
                                                  ident[0:HT, 0:HT])
                ins.then_inc(s_mt, 1)
            if first:
                pe.wait_ge(s_gx, k + 1)
                w(pe, s_on, i)
                for v in range(VER):
                    ins = mm(b4[:, 0:TP], wt[:, v, :], gx[:, i_par(r, 2), v, :], start=(v == 0), stop=(v == VER - 1))
                ins.then_inc(s_cv, 1)

            def scoresT(G):
                if G == 0:
                    pe.wait_ge(s_q2, i + 1)
                else:
                    pe.wait_ge(s_e, 2 * i + 1)
                for t in range(2):
                    for g in range(4):
                        p = slice(32 * g, 32 * g + 32)
                        ins = mm(ring[0:HT, g, t * TP:t * TP + TP], kT[p, i_par(r, 0), G, half(t)], q2[p, G, :],
                                 start=True, stop=True)
                ins.then_inc(s_ST, 1)

            def scores(G):
                if G == 0:
                    pe.wait_ge(s_ke, j + 1)
                    w(pe, s_e, 2 * i + 2)
                else:
                    pe.wait_ge(s_m, 2 * j + 1)
                for t in range(2):
                    for g in range(4):
                        p = slice(32 * g, 32 * g + 32)
                        ins = mm(ring[0:HT, g, t * TP:t * TP + TOK], qT[p, i_par(r, 1), G, half(t)],
                                 kT[p, i_par(r, 1), G, 0:TOK], start=True, stop=True)
                ins.then_inc(s_S, 1)

            if last:
                scoresT(0)
            if mid:
                pe.wait_ge(s_xT, j + 1)
                w(pe, s_h2, i)
                for G in range(2):
                    ins = mm(b5[:, G * TP:G * TP + TP], wq[:, G, :], xT[:, i_par(r, 1), :], start=True, stop=True)
                ins.then_inc(s_q, 1)
                w(pe, s_s, i)
                for G in range(2):
                    ins = mm(b6[:, G * TP:G * TP + TP], wk[:, G, :], xT[:, i_par(r, 1), :], start=(G == 0), stop=True,
                             skip_group_check=True)
                ins.then_inc(s_k, 1)
            if first:
                pe.wait_ge(s_y, k + 1)
                w(pe, s_q2, i + 1)
                for t in range(2):
                    ins = nc.tensor.transpose(b7[0:HT, t * E:t * E + E], yT[:, (r + 2) % UN, half(t)], ident[:])
                ins.then_inc(s_ht, 1)
            if mid:
                pe.wait_ge(s_sq, j + 1)
                for G in range(2):
                    ins = mm(b6[:, G * TP:G * TP + TP], selk[:, G, :], ksq[:, G, :], start=False, stop=True,
                             skip_group_check=True)
                ins.then_inc(s_kk, 1)
            if last:
                scoresT(1)
            if mid:
                pe.wait_ge(s_qe, j + 1)
                for t in range(2):
                    ins = mm(b5[0:HT, t * E:t * E + E], xT[:, i_par(r, 1), half(t)], wv[:], start=True, stop=True)
                ins.then_inc(s_v, 1)
            if last:
                pe.wait_ge(s_e, 2 * i + 2)
                w(pe, s_y, k + 1 if first else 0)
                for G in range(2):
                    for t in range(2):
                        n = HT - t
                        for g in range(4):
                            ins = mm(b4[32 * g:32 * g + 32, G * TP:G * TP + TP], va[0:n, i_par(r, 0), t, 4 * G + g, :],
                                     pT[0:n, G, g, t, :], start=(t == 0), stop=(t == 1), skip_group_check=True)
                ins.then_inc(s_pv, 1)
            if mid:
                scores(0)
            if first:
                pe.wait_ge(s_x, k + 1)
                for t in range(2):
                    ins = nc.tensor.transpose(b7[:, half(t)], x[:, t, :], ident[0:HT, 0:HT])
                ins.then_inc(s_xt, 1)
            if last:
                pe.wait_ge(s_on, i + 1)
                w(pe, s_ke, j + 1 if mid else 0)
                for G in range(2):
                    ins = mm(b6[:, 0:TP], wop[:, G, :], oT[:, G, :], start=(G == 0), stop=(G == 1))
                ins.then_inc(s_wo, 1)
            if mid:
                scores(1)
            if last:
                pe.wait_ge(s_s, i + 1)
                w(pe, s_ve, j + 1 if mid else 0)
                for t in range(2):
                    nc.tensor.transpose(b5[0:HT, t * E:t * E + E], sT[:, half(t)], ident[:])
                for t in range(2):
                    ins = mm(b5[0:HT, 2 * E + t * NEXP:2 * E + (t + 1) * NEXP], sT[:, half(t)], wrc[:],
                             start=True, stop=True)
                ins.then_inc(s_sb, 1)
            if group and r == 0:
                pe.wait_ge(s_pt, q + 2)
                mm(b5[:, 300:308], npix[:], part[:].rearrange("p a b -> p (a b)"), start=True, stop=True).then_inc(s_stp, 1)

        pipeline(pe, body)

    @block.scalar
    def _(act):
        act.wait_ge(s_set, SETUP)
        act.wait_ge(s_fill, 5)
        activation = nc.scalar.activation

        def body(q, r):
            last, mid, first, more, group = stages(q, r)
            b = q * UN + r
            i, j, k = b, b + 1, b + 2

            def exponentials(G):
                act.wait_ge(s_ST, 2 * i + G + 1)
                activation(pT[:, G].rearrange("p g t c -> p g (t c)"), ring[0:HT, :, 0:2 * TP], ACT.Exp).then_inc(s_e, 1)

            if last:
                w(act, s_pv, i)
                exponentials(0)
            if mid:
                act.wait_ge(s_q, j + 1)
                for G in range(2):
                    ins = activation(qT[:, i_par(r, 1), G, :], b5[:, G * TP:G * TP + TP], ACT.Identity,
                                     bias=qbias[:, G:G + 1], scale=qscale[:, G:G + 1])
                ins.then_inc(s_qe, 1)
                act.wait_ge(s_k, j + 1)
                w(act, s_kk, j)
                for G in range(2):
                    ins = activation(ksq[:, G, :], b6[:, G * TP:G * TP + TP], ACT.Square, bias=kbias[:, G:G + 1])
                ins.then_inc(s_sq, 1)
            if last:
                exponentials(1)
            if mid:
                act.wait_ge(s_kk, j + 1)
                for G in range(2):
                    ins = activation(kT[:, i_par(r, 1), G, :], b6[:, G * TP:G * TP + TP], ACT.Identity,
                                     bias=kbias[:, G:G + 1])
                ins.then_inc(s_ke, 1)
                act.wait_ge(s_v, j + 1)
                w(act, s_pv, j - 1)
                activation(va[:, i_par(r, 1), :, :, 0:DH],
                           b5[0:HT, 0:2 * E].rearrange("p (t h d) -> p t h d", t=2, d=DH), ACT.Copy).then_inc(s_ve, 1)
            if first:
                act.wait_ge(s_xt, k + 1)
                activation(xT[:, i_par(r, 2), :], b7[:, 0:TP], ACT.Copy).then_inc(s_xT, 1)

        pipeline(act, body)

    @block.vector
    def _(dve):
        V = nc.vector
        dve.wait_ge(s_c, 16 * NCONST)
        V.tensor_scalar(qscale[:], psc, cst[:, 1:2], cst[:, 0:1], ALU.mult, ALU.add)
        for G in range(2):
            V.tensor_scalar(selk[:, G, :], selm[:], psc[:, G:G + 1], -1.0, ALU.mult, ALU.mult)
        dve.wait_ge(s_sps, 1)
        V.tensor_tensor(qraw[:, 0:2], b4[:, 0:2], bq, ALU.add).then_inc(s_set, 1)
        V.tensor_tensor(qraw[:, 2:4], b4[:, 2:4], bk, ALU.add).then_inc(s_set, 1)
        V.tensor_tensor(vtot[:], b4[:, 4:5], bv, ALU.add).then_inc(s_set, 1)
        dve.wait_ge(s_set, 3)
        V.tensor_tensor(qraw[:, 4:6], qraw[:, 0:2], qscale[:], ALU.mult).then_inc(s_set, 1)
        V.tensor_scalar(kbias[:], qraw[:, 2:4], cst[:, 3:4], None, ALU.add)
        V.tensor_copy(gmean[:], b5[:, 0:TOK])
        V.tensor_scalar(gbias[:], b6[:, 0:TOK], tokb, None, ALU.add)
        V.tensor_tensor(wrc[:], wr[:], b7[:, 0:NEXP], ALU.subtract)
        for t in (wq[:, 0, :], wq[:, 1, :], wk[:, 0, :], wk[:, 1, :], wv[:]):
            V.tensor_scalar(t, t, lng, None, ALU.mult)
        dve.wait_ge(s_set, 4)
        V.tensor_scalar(qbias[:], qraw[:, 4:6], cst[:, 2:3], None, ALU.add)
        dve.wait_ge(s_sps, 2)
        V.tensor_tensor(obias[:], b4[:, 8:9], bo, ALU.add).then_inc(s_set, 1)
        dve.wait_ge(s_set, SETUP)
        dve.wait_ge(s_fill, 5)

        def norm_stats(src, six, two, var, s, i):
            for t in range(2):
                ins = V.bn_stats(six[:, t, :], src[0:HT, t * E:t * E + E])
            ins.then_inc(s, 1)
            dve.wait_ge(s, 3 * i + 1)
            V.memset(tick[:], 0.0)
            for t in range(2):
                ins = V.bn_aggr(two[:, t, :], six[:, t, :])
            ins.then_inc(s, 1)
            dve.wait_ge(s, 3 * i + 2)
            V.tensor_scalar(var[:], two[:, :, 1], LN_EPS, None, ALU.add).then_inc(s, 1)

        def body(q, r):
            last, mid, first, more, group = stages(q, r)
            b = q * UN + r
            i, j, k = b, b + 1, b + 2
            if last:
                dve.wait_ge(s_mt, i + 1)
                V.tensor_tensor(q2[:].rearrange("p g c -> p (g c)"), qT[:, i_par(r, 0)].rearrange("p g c -> p (g c)"),
                                b7[:, 0:2 * TP], ALU.add).then_inc(s_q2, 1)
            if first:
                c = (r + 2) % UN
                dve.wait_ge(s_nm, q + (2 if r >= 2 else 1))
                V.scalar_tensor_tensor(tb[:], gmean[:], inmr[:, c:c + 1], gbias[:], ALU.mult, ALU.add).then_inc(s_tb, 1)
                dve.wait_ge(s_cv, k + 1)
                dve.wait_ge(s_tb, k + 1)
                V.scalar_tensor_tensor(yT[:, c, 0:TOK], b4[:, 0:TOK], istd[:, c:c + 1], tb[:], ALU.mult,
                                       ALU.add).then_inc(s_y, 1)
            if group and r == 1:
                dve.wait_ge(s_st, q + 2)
                V.tensor_tensor(ivar[:], stat[:, :, 0], stat[:, :, 0], ALU.mult).then_inc(s_iv, 1)
                dve.wait_ge(s_iv, 2 * (q + 1) + 1)
                V.scalar_tensor_tensor(ivar[:], stat[:, :, 1], TOK_EPS, ivar[:], ALU.add, ALU.subtract).then_inc(s_iv, 1)
            if first:
                dve.wait_ge(s_ht, k + 1)
                norm_stats(b7, st6, mv, ve, s_hb, k)
            if group and r == 0:
                at = (q + 1) * (UN * XZ)
                for n in range(UN):
                    dve.wait_ge(s_ld[n], (q + 2) * 16)
                z = [xz[:, bass.ds(at + n * XZ + TOK, ZT)] for n in range(UN)]
                for n in range(UN):
                    ins = V.scalar_tensor_tensor(zs[:, n, :], z[n], 1.0, zwt[:], ALU.mult, ALU.mult,
                                                 accum_out=part[:, n, 0:1])
                ins.then_inc(s_zs, 1)
                dve.wait_ge(s_zs, q + 2)
                for n in range(UN):
                    ins = V.scalar_tensor_tensor(zs[:, n, :], zs[:, n, :], 1.0, z[n], ALU.mult, ALU.mult,
                                                 accum_out=part[:, n, 1:2])
                ins.then_inc(s_pt, 1)
            if first:
                dve.wait_ge(s_hr, k + 1)
                w(dve, s_xt, k)
                for t in range(2):
                    ins = V.tensor_scalar(x[:, t, :], b7[0:HT, t * E:t * E + E], mv[:, t, 0:1], rs[:, t:t + 1],
                                          ALU.subtract, ALU.mult)
                ins.then_inc(s_x, 1)
            if group and r == 1:
                dve.wait_ge(s_is, q + 2)
                V.scalar_tensor_tensor(inmr[:], stat[:, :, 0], -1.0, istd[:], ALU.mult, ALU.mult).then_inc(s_nm, 1)
            if last:
                dve.wait_ge(s_pv, i + 1)
                V.memset(tick[:], 0.0)
                o = b4[:, 0:2 * TP]
                flat = [t[:].rearrange("p g c -> p (g c)") for t in (osum, oinv, oT)]
                V.stream_shuffle(flat[0], o, [DH + c % DH for c in range(32)]).then_inc(s_os, 1)
                dve.wait_ge(s_os, i + 1)
                V.reciprocal(flat[1], flat[0]).then_inc(s_oi, 1)
                dve.wait_ge(s_oi, i + 1)
                w(dve, s_wo, i)
                V.tensor_tensor(flat[2], o, flat[1], ALU.mult).then_inc(s_on, 1)

            def maxima(G):
                dve.wait_ge(s_S, 2 * j + G + 1)
                w(dve, s_mt, j - 1)
                V.tensor_reduce(mp[:, i_par(r, 1), :, G, :, 29].rearrange("p t g -> p g t"),
                                ring[0:HT, :, 0:2 * TP].rearrange("p g (t c) -> p g t c", t=2)[:, :, :, 0:TOK],
                                AX.X, ALU.max, negate=True).then_inc(s_m, 1)

            if mid:
                maxima(0)
            if last:
                dve.wait_ge(s_wo, i + 1)
                w(dve, s_sb, i)
                V.scalar_tensor_tensor(sT[:], b6[:, 0:TP], obias[:, 0:1], yT[:, r, :], ALU.add,
                                       ALU.add).then_inc(s_s, 1)
            if mid:
                maxima(1)
            if group and r == 0:
                dve.wait_ge(s_stp, q + 2)
                V.tensor_copy(stat[:].rearrange("p a b -> p (a b)"), b5[:, 300:308]).then_inc(s_st, 1)
            if last:
                dve.wait_ge(s_sb, i + 1)
                norm_stats(b5, st6b, mvb, veb, s_sn, i)
                dve.wait_ge(s_sr, i + 1)
                w(dve, s_out[r], q * 64)
                V.tensor_tensor(lg[:, r], b5[0:HT, 2 * E:2 * E + 2 * NEXP].rearrange("p (t e) -> p t e", t=2),
                                rsb[:].unsqueeze(2).to_broadcast([HT, 2, NEXP]), ALU.mult)
                for t in range(2):
                    ins = V.tensor_scalar(h2[:, r, t, :], b5[0:HT, t * E:t * E + E], mvb[:, t, 0:1], rsb[:, t:t + 1],
                                          ALU.subtract, ALU.mult)
                ins.then_inc(s_h2, 1)

        pipeline(dve, body)


def experts(nc, ctx, A, h2_dram, lg_dram, e_dram, t_dram, acc_dram, out):

    def sb(name, shape, dt=F32):
        return ctx.enter_context(nc.sbuf_tensor(name, shape, dt))

    def sem(name):
        return ctx.enter_context(nc.semaphore(name))

    W3 = NEXP * R
    TAB = 2 * R + 1
    NB = CAP // 128
    BITS = 30
    CT = 13
    NCH = R // CT
    ON_ACT = 8

    ident = sb("ident2", [128, 128])
    ones = sb("ones2", [R, R])
    tri = sb("tri", [R, R])
    blk = sb("blk", [128, 128])
    reset = sb("reset", [R, W3])
    slots = sb("slots", [R, CAP])
    slot1 = sb("slot1", [128, NB])
    iota = sb("iota", [128, R])
    rowbase = sb("rowbase", [R, 1])
    bits = sb("bits", [128, BITS], U32)
    b1 = sb("b1", [128, NEXP * 4])
    b2 = sb("b2", [128, NEXP * E])

    lrow = sb("lrow", [R, W3])
    pr = sb("pr", [R, NEXP, R])
    mx = sb("mx", [R, NEXP])
    gm = sb("gm", [NEXP, 1])
    dg = sb("dg", [NEXP, NEXP])
    mb = sb("mb", [R, NEXP])
    tot = sb("tot", [R, NEXP])
    rtot = sb("rtot", [R, NEXP])
    pe_ = sb("pe_", [128, CHUNK])
    ge = sb("ge", [128, CHUNK])
    cnt = sb("cnt", [128, 1])
    cand = sb("cand", [128, 1])
    pick = sb("pick", [128, 1])
    thr = sb("thr", [128, 1])
    tb = sb("thr_rows", [R, NEXP])
    gt = sb("gt", [R, NEXP, R])
    eq = sb("eq", [R, NEXP, R])
    run = sb("run", [R, NEXP, R])
    ng = sb("ng", [R, NEXP])
    te = sb("te", [R, NEXP])
    room = sb("room", [R, NEXP])
    start = sb("start", [R, NEXP])
    end = sb("end", [R, NEXP])
    tab = sb("tab", [R, NEXP * TAB])
    oh0 = sb("oh0", [R, CAP])
    oh = sb("oh", [R, CAP])
    tabs = sb("tabs", [128, NB, TAB])
    jk = sb("jk", [128, NB, R])
    loc = sb("loc", [128, NB])
    wgt = sb("wgt", [128, 2, NB])
    idx = sb("idx", [128, 2, NB], U32)
    xg = sb("xg", [128, 2, NB, E])
    xgT = sb("xgT", [128, 2, UNIT])
    w1 = sb("w1", [128, 2, FF])
    w2 = sb("w2", [128, 2, 4, E])
    hT = sb("hT", [128, 2, 4, UNIT])
    yb = sb("yb", [128, NBLK, E])
    yw = sb("yw", [128, 2, NBLK, E])
    fin = sb("fin", [R, 3, CT, E])
    fout = sb("fout", [R, 2, CT, E])
    f6 = sb("f6", [R, CT, 6])
    fmv = sb("fmv", [R, 2, CT, 2])
    fve = sb("fve", [R, CT])
    frs = sb("frs", [R, 2, CT])
    fnm = sb("fnm", [R, 2, CT])
    half = sb("half", [128, CT])
    b1e = sb("b1e", [128, 2, 4])

    def pb(name):
        return ctx.enter_context(nc.psum_tensor(name, [128, 512], F32))

    bI = [pb("bI0"), pb("bI1")]
    bX = pb("bX")
    bH = [pb("bH0"), pb("bH1"), pb("bH2")]
    bO = [pb("bO0"), pb("bO1")]

    s_c = sem("s2_consts")
    s_l = sem("s_logits")
    s_copy = sem("s_acc_copied")
    s_half = sem("s_half")
    s_d = sem("s_dve")
    s_pe = sem("s_routing_psum")
    s_sh = sem("s_shifted")
    s_ex = sem("s_exp2")
    s_est = sem("s_exp_stored")
    s_eld = sem("s_exp_loaded")
    s_cnt = sem("s_count")
    s_sum = sem("s_count_sum")
    s_cand = sem("s_cand")
    s_pick = sem("s_pick")
    s_thr = sem("s_thr")
    s_tst = sem("s_thr_stored")
    s_tld = sem("s_thr_loaded")
    s_tab = sem("s_table")
    s_o0 = sem("s_onehot_half")
    s_oh = sem("s_onehot")
    s_ix = sem("s_index_psum")
    s_ie = sem("s_index_copied")
    s_loc = sem("s_loc")
    s_idx = sem("s_idx")
    s_g = [[sem(f"s_gathered{p}{u}") for u in range(2)] for p in range(2)]
    s_w = [sem(f"s_weights{p}") for p in range(2)]
    s_xp = sem("s_xg_turned")
    s_xe = sem("s_xgT")
    s_h = sem("s_h_psum")
    s_held = sem("s_held")
    s_b1 = sem("s_b1")
    s_ge = sem("s_gelu")
    s_o = sem("s_o_psum")
    s_yb = sem("s_y_biased")
    s_yw = sem("s_y_weighted")
    s_sc = [sem(f"s_scattered{p}") for p in range(2)]
    s_fl = [sem(f"s_fin_loaded{n}") for n in range(3)]
    s_f6 = sem("s_fin_stats")
    s_fr = sem("s_fin_rstd")
    s_fn = sem("s_fin_nmr")
    s_fa = sem("s_fin_act")
    s_fv = sem("s_fin_dve")
    s_fs = [sem(f"s_fin_stored{n}") for n in range(2)]

    consts = [(ident, "ident"), (ones, "ones1"), (tri, "tri"), (blk, "blk"), (reset, "reset"), (slots, "slots"),
              (slot1, "slot1"), (iota, "iota"), (rowbase, "rowbase"), (bits, "bits"), (b1, "b1"), (b2, "b2")]

    def w(eng, s, v):
        if isinstance(v, int) and v <= 0:
            return
        eng.wait_ge(s, v)

    def pipeline(eng, body):
        body(-1, 1)
        for p in range(2):
            body(0, p)
        with eng.Fori(1, NEXP // 2 - 1) as q:
            for p in range(2):
                body(q, p)
        for p in range(2):
            body(NEXP // 2 - 1, p)

    def stages(q, p):
        if not isinstance(q, int):
            return True, True
        e = 2 * q + p
        return e >= 0, e + 1 < NEXP

    def rows(d):
        return d.rearrange("(p t) e -> p t e", p=R)

    block = ctx.enter_context(nc.Block())

    @block.sync
    def _(sp):
        sp.dma_start(lrow[:], lg_dram.rearrange("(p t) e -> p (t e)", p=R)).then_inc(s_l, 16)
        for t, n in consts:
            sp.dma_start(t[:], A[n]).then_inc(s_c, 16)

        def weights(q, p):
            e = 2 * q + p
            w(sp, s_o, 2 * (e - 1))
            sp.dma_start(w1[:, p, :], A["W1"][bass.ds(e, 1)].rearrange("e d f -> d (e f)")).then_inc(s_w[p], 16)
            sp.dma_start(w2[:, p], A["W2"][bass.ds(e, 1)].rearrange("e (c f) d -> f (e c) d", c=4)).then_inc(s_w[p], 16)

        weights(0, 0)
        weights(0, 1)
        sp.wait_ge(s_ex, 1)
        sp.dma_start(e_dram.rearrange("e (p t) -> p e t", p=R), pr[:]).then_inc(s_est, 16)
        sp.wait_ge(s_est, 16)
        sp.dma_start(pe_[:], e_dram.rearrange("e (c m) -> (e c) m", c=16)).then_inc(s_eld, 16)
        sp.dma_start(acc_dram, h2_dram).then_inc(s_copy, 16)
        sp.wait_ge(s_thr, BITS + 1)
        sp.dma_start(t_dram.rearrange("o e -> e o"), thr[0:128:16, :]).then_inc(s_tst, 16)
        sp.wait_ge(s_tst, 16)
        sp.dma_start(tb[:], t_dram.to_broadcast([R, NEXP])).then_inc(s_tld, 16)
        with sp.Fori(1, NEXP // 2) as q:
            for p in range(2):
                weights(q, p)
        for p in range(2):
            sp.wait_ge(s_sc[p], 16 * NBLK * NEXP)

        def store(n):
            sp.wait_ge(s_fa, n + 1)
            sp.wait_ge(s_fv, n + 1)
            sp.dma_start(rows(out)[:, n * CT:(n + 1) * CT, :], fout[:, n % 2]).then_inc(s_fs[n % 2], 16)

        for n in range(NCH):
            if n >= 3:
                sp.wait_ge(s_fa, n - 2)
                sp.wait_ge(s_fv, n - 2)
            sp.dma_start(fin[:, n % 3], rows(acc_dram)[:, n * CT:(n + 1) * CT, :]).then_inc(s_fl[n % 3], 16)
            if n >= 2:
                store(n - 2)
        store(NCH - 2)
        store(NCH - 1)
        for n in range(2):
            sp.wait_ge(s_fs[n], 16 * (NCH // 2))

    @block.gpsimd
    def _(pool):
        nc.gpsimd.memset(half[:], -0.5).then_inc(s_half, 1)
        pool.wait_ge(s_copy, 16)
        pool.wait_ge(s_half, 1)

        def held():
            pool.sem_inc(s_held, 1)

        def body(q, p):
            ffn, index = stages(q, p)
            e = 2 * q + p
            n = 1 - p
            if index:
                pool.wait_ge(s_idx, e + 2)
                w(pool, s_xp, 2 * e)
                held()
                for k in range(NB):
                    nc.gpsimd.indirect_dma_start(
                        out=xg[:, n, k, :], out_offset=None, in_=h2_dram,
                        in_offset=bass.IndirectOffsetOnAxis(ap=idx[:, n, k:k + 1], axis=0),
                    ).then_inc(s_g[n][k // NBLK], 16)
            if ffn:
                for u in range(2):
                    pool.wait_ge(s_yw, 2 * e + u + 1)
                    if u == 0:
                        for v in range(2):
                            w(pool, s_sc[v], 16 * NBLK * e)
                    held()
                    for k in range(NBLK):
                        nc.gpsimd.indirect_dma_start(
                            out=acc_dram, in_=yw[:, u, k, :], in_offset=None,
                            out_offset=bass.IndirectOffsetOnAxis(ap=idx[:, p, u * NBLK + k:u * NBLK + k + 1], axis=0),
                            compute_op=ALU.add,
                        ).then_inc(s_sc[u], 16)

        pipeline(pool, body)
        for n in range(NCH):
            pool.wait_ge(s_f6, 3 * n + 3)
            nc.gpsimd.tensor_tensor(frs[:, n % 2, :], fve[:], half[0:R, :], ALU.pow).then_inc(s_fr, 1)

    @block.tensor
    def _(pe):
        mm = nc.tensor.matmul
        pe.wait_ge(s_c, 16 * len(consts))
        pe.wait_ge(s_d, D_MAX)
        nc.tensor.transpose(bX[0:NEXP, 0:R], mx[:], ident[0:R, 0:R]).then_inc(s_pe, 1)
        pe.wait_ge(s_d, D_DIAG)
        mm(bX[0:R, 0:NEXP], ones[0:NEXP, :], dg[:], start=True, stop=True).then_inc(s_pe, 1)
        pe.wait_ge(s_d, D_TOT)
        mm(bX[0:R, 0:NEXP], ones[:], tot[:], start=True, stop=True).then_inc(s_pe, 1)
        with pe.Fori(0, BITS) as i:
            pe.wait_ge(s_cnt, i + 1)
            mm(bI[0][:, 0:1], blk[:], cnt[:], start=True, stop=True).then_inc(s_sum, 1)
        pe.wait_ge(s_d, D_TIES)
        mm(bX[0:R, 0:NEXP], ones[:], ng[:], start=True, stop=False)
        mm(bX[0:R, 0:NEXP], tri[:], te[:], start=False, stop=True).then_inc(s_pe, 1)
        pe.wait_ge(s_d, D_SEL)
        mm(bX[0:R, 0:NEXP], tri[:], te[:], start=True, stop=True).then_inc(s_pe, 1)
        pe.wait_ge(s_tab, 1)

        def body(q, p):
            ffn, index = stages(q, p)
            e = 2 * q + p

            def tables(k):
                if k == 0:
                    pe.wait_ge(s_oh, e + 2)
                w(pe, s_ie, 4 * (e + 1) + k - 1)
                for c in range(2):
                    at = (2 * k + c) * 128
                    ins = mm(bI[k % 2][:, c * TAB:(c + 1) * TAB], oh[:, at:at + 128], tab[:, bass.ds((e + 1) * TAB, TAB)],
                             start=True, stop=True)
                ins.then_inc(s_ix, 1)

            def layers(u):
                n = 2 * e + u
                pe.wait_ge(s_g[p][u], (q + 1) * 16 * NBLK)
                w(pe, s_xe, n)
                for k in range(NBLK):
                    ins = nc.tensor.transpose(bX[:, k * 128:(k + 1) * 128], xg[:, p, u * NBLK + k, :], ident[:])
                ins.then_inc(s_xp, 1)
                if u == 0:
                    pe.wait_ge(s_w[p], (q + 1) * 32)
                pe.wait_ge(s_xe, n + 1)
                for f in range(4):
                    if f % 3 == 0:
                        w(pe, s_ge, 4 * n + f // 3)
                    mm(bH[f % 3][:], w1[:, p, f * 128:(f + 1) * 128], xgT[:, u, :], start=True, stop=True).then_inc(s_h, 1)
                pe.wait_ge(s_ge, 4 * n + 4)
                w(pe, s_yb, n - 1)
                for k in range(NBLK):
                    for f in range(4):
                        ins = mm(bO[u][:, k * E:(k + 1) * E], hT[:, u, f, k * 128:(k + 1) * 128], w2[:, p, f, :],
                                 start=(f == 0), stop=(f == 3))
                ins.then_inc(s_o, 1)

            if ffn:
                layers(0)
            if index:
                for k in range(NB // 2):
                    tables(k)
            if ffn:
                layers(1)

        pipeline(pe, body)

    @block.scalar
    def _(act):
        activation = nc.scalar.activation
        act.wait_ge(s_sh, 1)
        activation(pr[:], pr[:], ACT.Exp).then_inc(s_ex, 1)
        act.wait_ge(s_c, 16 * len(consts))

        def body(q, p):
            ffn, index = stages(q, p)
            e = 2 * q + p

            def gelus(u):
                n = 2 * e + u
                if u == 0:
                    activation(b1e[:, p, :], b1[:, bass.ds(e * 4, 4)], ACT.Copy).then_inc(s_b1, 1)
                    act.wait_ge(s_b1, e + 1)
                for f in range(4):
                    act.wait_ge(s_h, 4 * n + f + 1)
                    if f == 0:
                        w(act, s_o, n - 1)
                    activation(hT[:, u, f, :], bH[f % 3][:], ACT.Gelu,
                               bias=b1e[:, p, f:f + 1]).then_inc(s_ge, 1)

            if ffn:
                gelus(0)
            if index:
                for k in range(NB // 2):
                    act.wait_ge(s_ix, 4 * (e + 1) + k + 1)
                    if k == 0:
                        w(act, s_idx, e + 1)
                    activation(tabs[:, 2 * k:2 * k + 2, :].rearrange("p k c -> p (k c)"), bI[k % 2][:, 0:2 * TAB],
                               ACT.Copy).then_inc(s_ie, 1)
            if ffn:
                gelus(1)

        pipeline(act, body)
        for n in range(NCH):
            act.wait_ge(s_fn, n + 1)
            if n >= 2:
                act.wait_ge(s_fs[n % 2], 16 * (n // 2))
            for t in range(ON_ACT):
                ins = activation(fout[:, n % 2, t, :], fin[:, n % 3, t, :], ACT.Identity, bias=fnm[:, n % 2, t:t + 1],
                                 scale=frs[:, n % 2, t:t + 1])
            ins.then_inc(s_fa, 1)

    @block.vector
    def _(dve):
        V = nc.vector
        done = [0]

        def link(ins):
            done[0] += 1
            ins.then_inc(s_d, 1)
            dve.wait_ge(s_d, done[0])

        def over(t):
            return t[:].unsqueeze(2).to_broadcast([R, NEXP, R])

        def flat(t):
            return t[:].rearrange("p e t -> p (e t)")

        dve.wait_ge(s_l, 16)
        link(V.tensor_copy(pr[:], lrow[:].rearrange("p (t e) -> p e t", e=NEXP)))
        link(V.tensor_reduce(mx[:], pr[:], AX.X, ALU.max))
        assert done[0] == D_MAX
        dve.wait_ge(s_pe, 1)
        link(V.tensor_reduce(gm[:], bX[0:NEXP, 0:R], AX.X, ALU.max))
        dve.wait_ge(s_c, 16 * len(consts))
        link(V.tensor_scalar(dg[:], ident[0:NEXP, 0:NEXP], gm[:, 0:1], None, ALU.mult))
        assert done[0] == D_DIAG
        dve.wait_ge(s_pe, 2)
        link(V.tensor_copy(mb[:], bX[0:R, 0:NEXP]))
        V.tensor_tensor(pr[:], pr[:], over(mb), ALU.subtract).then_inc(s_sh, 1)
        dve.wait_ge(s_ex, 1)
        link(V.tensor_reduce(tot[:], pr[:], AX.X, ALU.add))
        assert done[0] == D_TOT
        dve.wait_ge(s_pe, 3)
        link(V.reciprocal(rtot[:], bX[0:R, 0:NEXP]))
        link(V.tensor_tensor(tab[:].rearrange("p (e c) -> p e c", c=TAB)[:, :, R:2 * R], pr[:], over(rtot), ALU.mult))
        V.tensor_copy(tab[:].rearrange("p (e c) -> p e c", c=TAB)[:, :, 2 * R],
                      rowbase[:, 0:1].to_broadcast([R, NEXP]))

        V.memset(thr[:], 0.0).then_inc(s_thr, 1)
        dve.wait_ge(s_eld, 16)
        with dve.Fori(0, BITS) as i:
            dve.wait_ge(s_thr, i + 1)
            V.tensor_tensor(cand[:].bitcast(U32), thr[:].bitcast(U32), bits[:, bass.ds(i, 1)],
                            ALU.bitwise_or).then_inc(s_cand, 1)
            dve.wait_ge(s_cand, i + 1)
            V.tensor_scalar(ge[:], pe_[:], cand[:, 0:1], 0.0, ALU.is_ge, ALU.add, accum_out=cnt[:]).then_inc(s_cnt, 1)
            dve.wait_ge(s_sum, i + 1)
            V.scalar_tensor_tensor(pick[:], bI[0][:, 0:1], CAP - 0.5, cand[:], ALU.is_ge, ALU.mult).then_inc(s_pick, 1)
            dve.wait_ge(s_pick, i + 1)
            V.tensor_tensor(thr[:], thr[:], pick[:], ALU.max).then_inc(s_thr, 1)

        dve.wait_ge(s_tld, 16)
        V.tensor_tensor(gt[:], pr[:], over(tb), ALU.is_gt)
        link(V.tensor_tensor(eq[:], pr[:], over(tb), ALU.is_equal))
        V.tensor_reduce(ng[:], gt[:], AX.X, ALU.add)
        link(V.tensor_tensor_scan(flat(run), reset[:], flat(eq), 0.0, ALU.mult, ALU.add))
        link(V.tensor_copy(te[:], run[:, :, R - 1]))
        assert done[0] == D_TIES
        dve.wait_ge(s_pe, 4)
        link(V.tensor_scalar(room[:], bX[0:R, 0:NEXP], -1.0, float(CAP), ALU.mult, ALU.add))
        link(V.tensor_tensor(run[:], run[:], over(room), ALU.is_le))
        link(V.tensor_tensor(run[:], run[:], eq[:], ALU.mult))
        link(V.tensor_tensor(gt[:], gt[:], run[:], ALU.add))
        link(V.tensor_tensor_scan(flat(run), reset[:], flat(gt), 0.0, ALU.mult, ALU.add))
        link(V.tensor_copy(te[:], run[:, :, R - 1]))
        assert done[0] == D_SEL
        dve.wait_ge(s_pe, 5)
        link(V.tensor_copy(start[:], bX[0:R, 0:NEXP]))
        V.tensor_tensor(end[:], start[:], te[:], ALU.add)
        link(V.tensor_tensor(run[:], run[:], over(start), ALU.add))
        V.tensor_tensor(tab[:].rearrange("p (e c) -> p e c", c=TAB)[:, :, 0:R], run[:], gt[:], ALU.mult).then_inc(s_tab, 1)
        dve.wait_ge(s_tab, 1)

        def body(q, p):
            ffn, index = stages(q, p)
            e = 2 * q + p
            n = 1 - p

            def onehot():
                w(dve, s_ix, 4 * (e + 1))
                V.tensor_scalar(oh0[:], slots[:], start[:, bass.ds(e + 1, 1)], None, ALU.is_ge).then_inc(s_o0, 1)
                dve.wait_ge(s_o0, e + 2)
                V.scalar_tensor_tensor(oh[:], slots[:], end[:, bass.ds(e + 1, 1)], oh0[:], ALU.is_lt,
                                       ALU.mult).then_inc(s_oh, 1)

            def numbers():
                for k in range(NB):
                    if k % 2 == 0:
                        dve.wait_ge(s_ie, 4 * (e + 1) + k // 2 + 1)
                    if k == 0:
                        for v in range(2):
                            w(dve, s_sc[v], 16 * NBLK * e)
                        w(dve, s_idx, e + 1)
                    V.scalar_tensor_tensor(jk[:, k, :], tabs[:, k, 0:R], slot1[:, k:k + 1], iota[:], ALU.is_equal,
                                           ALU.mult, accum_out=loc[:, k:k + 1])
                    ins = V.scalar_tensor_tensor(tabs[:, k, R:2 * R], tabs[:, k, 0:R], slot1[:, k:k + 1],
                                                 tabs[:, k, R:2 * R], ALU.is_equal, ALU.mult,
                                                 accum_out=wgt[:, n, k:k + 1])
                ins.then_inc(s_loc, 1)
                dve.wait_ge(s_loc, e + 2)
                V.tensor_tensor(idx[:, n, :], loc[:], tabs[:, :, 2 * R], ALU.add).then_inc(s_idx, 1)

            def turned(u):
                m = 2 * e + u
                dve.wait_ge(s_xp, m + 1)
                w(dve, s_h, 4 * (m - 1))
                V.tensor_copy(xgT[:, u, :], bX[:]).then_inc(s_xe, 1)

            def weighted(u):
                m = 2 * e + u
                dve.wait_ge(s_o, m + 1)
                w(dve, s_yw, m)
                V.tensor_tensor(yb[:], bO[u][:].rearrange("p (k c) -> p k c", c=E),
                                b2[:, bass.ds(e * E, E)].unsqueeze(1).to_broadcast([128, NBLK, E]),
                                ALU.add).then_inc(s_yb, 1)
                dve.wait_ge(s_yb, m + 1)
                w(dve, s_sc[u], 16 * NBLK * e)
                V.tensor_tensor(yw[:, u], yb[:], wgt[:, p, u * NBLK:(u + 1) * NBLK].unsqueeze(2).to_broadcast([128, NBLK, E]),
                                ALU.mult).then_inc(s_yw, 1)

            if index:
                onehot()
            if ffn:
                turned(0)
                weighted(0)
            if index:
                numbers()
            if ffn:
                turned(1)
                weighted(1)

        pipeline(dve, body)
        for n in range(NCH):
            dve.wait_ge(s_fl[n % 3], 16 * (n // 3 + 1))
            if n >= 2:
                dve.wait_ge(s_fa, n - 1)
            for t in range(CT):
                ins = V.bn_stats(f6[:, t, :], fin[:, n % 3, t, :])
            ins.then_inc(s_f6, 1)
            dve.wait_ge(s_f6, 3 * n + 1)
            for t in range(CT):
                ins = V.bn_aggr(fmv[:, n % 2, t, :], f6[:, t, :])
            ins.then_inc(s_f6, 1)
            dve.wait_ge(s_f6, 3 * n + 2)
            V.tensor_scalar(fve[:], fmv[:, n % 2, :, 1], LN_EPS, None, ALU.add).then_inc(s_f6, 1)
            dve.wait_ge(s_fr, n + 1)
            V.scalar_tensor_tensor(fnm[:, n % 2, :], fmv[:, n % 2, :, 0], -1.0, frs[:, n % 2, :], ALU.mult,
                                   ALU.mult).then_inc(s_fn, 1)
            if n >= 2:
                dve.wait_ge(s_fs[n % 2], 16 * (n // 2))
            for t in range(ON_ACT, CT):
                ins = V.tensor_scalar(fout[:, n % 2, t, :], fin[:, n % 3, t, :], fmv[:, n % 2, t, 0:1],
                                      frs[:, n % 2, t:t + 1], ALU.subtract, ALU.mult)
            ins.then_inc(s_fv, 1)


D_MAX, D_DIAG, D_TOT, D_TIES, D_SEL = 2, 4, 6, 11, 17


def program(nc, A, out):
    h2_dram = nc.dram_tensor("h2_rows", [NTOK, E], F32, kind=A["kind"]).ap()
    lg_dram = nc.dram_tensor("logit_rows", [NTOK, NEXP], F32, kind=A["kind"]).ap()
    e_dram = nc.dram_tensor("exp_rows", [NEXP, NTOK], F32, kind="Internal").ap()
    t_dram = nc.dram_tensor("thresholds", [1, NEXP], F32, kind="Internal").ap()
    acc_dram = nc.dram_tensor("acc_rows", [NTOK, E], F32, kind=A["kind"]).ap()
    with ExitStack() as ctx:
        tower_tokens(nc, ctx, A, h2_dram, lg_dram)
    with ExitStack() as ctx:
        experts(nc, ctx, A, h2_dram, lg_dram, e_dram, t_dram, acc_dram, out)


def layouts(i):
    f = {k: np.asarray(v) for k, v in i.items()}
    x = f["x"]
    plain = x.reshape(NI, CH, GRID, PATCH, GRID, PATCH).transpose(1, 3, 5, 0, 2, 4).reshape(KP, NI, TOK)
    pad = np.pad(x, ((0, 0), (0, 0), (SHIFT, SHIFT), (SHIFT, SHIFT)))
    shifted = pad.reshape(NI, CH, ZG, PATCH, ZG, PATCH).transpose(1, 3, 5, 0, 2, 4).reshape(KP, NI, ZT)

    def patches(g):
        return g.reshape(VER, CH, GRID, PATCH, GRID, PATCH).transpose(1, 3, 5, 0, 2, 4).reshape(KP, VER, TOK)

    def heads(scalar, point):
        o = np.zeros(scalar.shape[:-1] + (HEADS, 32), scalar.dtype)
        o[..., 0:DH] = scalar.reshape(scalar.shape[:-1] + (HEADS, DH))
        o[..., DH:DH + PP] = point.reshape(point.shape[:-1] + (HEADS, PP))
        return o.reshape(scalar.shape[:-1] + (2, KP))

    def column(v):
        return v.reshape(-1, 1)

    wo = f["L0_attn_wo"]
    wop = np.zeros((HEADS, 32, E), wo.dtype)
    wop[:, 0:DH] = wo.reshape(HEADS, DH, E)
    edge = np.full(ZG, 2.0)
    edge[[0, -1]] = 1.0
    row = np.arange(KP) % 32
    cst = np.stack([0.25 * (row < DH), 2.0 * ((row >= DH) & (row < DH + PP)), row == 28, row == 29], 1)
    selm = np.zeros((KP, KP))
    for p in range(KP):
        if DH <= row[p] < DH + PP:
            selm[p, p - row[p] + 28] = 1.0
    c = lambda a: np.ascontiguousarray(a, np.float32)
    return {
        "xz": np.concatenate([plain, shifted], 2).reshape(KP, NI * XZ),
        "w": np.ascontiguousarray(f["L0_tok_W"].reshape(E, VER, KP).transpose(2, 1, 0)),
        "gamma": patches(f["L0_tok_gamma"]), "beta": patches(f["L0_tok_beta"]),
        "zwt": c(np.broadcast_to((1.0 + np.outer(edge, edge)).reshape(1, ZT), (KP, ZT))),
        "npix": c(np.full((KP, KP), 1.0 / NPIX)), "ones": c(np.full((KP, KP), 1.0 / E)),
        "ident": c(np.eye(KP)), "selm": c(selm), "cst": c(cst), "wr": f["L0_ffn_Wr"],
        "tok_b": column(f["L0_tok_b"]), "ln_g": column(f["L0_attn_ln_g"]), "ln_b": column(f["L0_attn_ln_b"]),
        "bv": column(f["L0_attn_bv"]), "bo": column(f["L0_attn_bo"]),
        "bq": heads(f["L0_attn_bq"], f["L0_attn_bqp"]).T, "bk": heads(f["L0_attn_bk"], f["L0_attn_bkp"]).T,
        "ps": np.repeat(f["L0_attn_pscale"].reshape(2, 4).T, 32, 0),
        "wq": heads(f["L0_attn_wq"], f["L0_attn_wqp"]), "wk": heads(f["L0_attn_wk"], f["L0_attn_wkp"]),
        "wv": f["L0_attn_wv"], "wo": wo,
        "wop": wop.reshape(2, KP, E).transpose(1, 0, 2),
        "ones1": c(np.ones((R, R))), "tri": c(np.triu(np.ones((R, R)), 1)),
        "blk": c(np.kron(np.eye(NEXP), np.ones((16, 16)))),
        "reset": c(np.broadcast_to((np.arange(NEXP * R) % R != 0)[None], (R, NEXP * R))),
        "slots": c(np.broadcast_to(np.arange(CAP)[None], (R, CAP))),
        "slot1": c(1 + np.arange(128)[:, None] + 128 * np.arange(CAP // 128)[None]),
        "iota": c(np.broadcast_to(np.arange(R)[None], (128, R))),
        "rowbase": c(R * np.arange(R)[:, None]),
        "bits": np.broadcast_to((1 << np.arange(29, -1, -1, dtype=np.uint32))[None], (128, 30)),
        "b1": f["L0_ffn_b1"].reshape(NEXP * 4, 128).T,
        "b2": np.broadcast_to(f["L0_ffn_b2"].reshape(1, NEXP * E), (128, NEXP * E)),
        "W1": f["L0_ffn_W1"], "W2": f["L0_ffn_W2"],
    }


def kernel(**inputs):
    import concourse.bacc as _bacc
    from concourse.bass_utils import run_bass_kernel_spmd as _run

    nc = _bacc.Bacc("TRN2", target_bir_lowering=False, num_devices=1)
    arrays, A = {}, {"kind": KIND}
    for name, a in layouts(inputs).items():
        a = np.ascontiguousarray(a)
        arrays[f"in_{name}"] = a
        A[name] = nc.dram_tensor(f"in_{name}", a.shape, mybir.dt.from_np(a.dtype), kind="ExternalInput").ap()
    out = nc.dram_tensor("out_tokens", [NTOK, E], F32, kind="ExternalOutput").ap()
    program(nc, A, out)
    r = _run(nc, [arrays], core_ids=[0])
    return r.results[0]["out_tokens"].reshape(NI, TOK, E)
```

```python
from contextlib import ExitStack

import numpy as np

import concourse.bass as bass
from concourse import mybir

ALU = mybir.AluOpType
ACT = mybir.ActivationFunctionType
F32 = mybir.dt.float32
U32 = mybir.dt.uint32
AX = mybir.AxisListType

NI, CH, SIDE, SHIFT, PATCH = 64, 2, 104, 4, 8
GRID = SIDE // PATCH
TOK = GRID * GRID
ZG = GRID + 1
ZT = ZG * ZG
XZ = TOK + ZT
VER = 5
KP = CH * PATCH * PATCH
E = 128
HEADS, DH, PP = 8, 16, 12
HT = (TOK + 1) // 2
TP = 2 * HT
NTOK = NI * TOK
UN = 4
NEXP, FF, CAP = 8, 512, 1024
R = 104
TOK_EPS, LN_EPS = 1e-7, 1e-5
NPIX = 10 * SIDE * SIDE
CHUNK = NTOK // 16
UNIT = 512
NBLK = UNIT // 128
KIND = "Internal"


SETUP = 7
FILLS = 6


def i_par(r, ahead):
    return (r + ahead) % 2


def i_ring(r, ahead):
    return (r + ahead) % UN


def tower_tokens(nc, ctx, A, h2_dram, lg_dram):

    def sb(name, shape):
        return ctx.enter_context(nc.sbuf_tensor(name, shape, F32))

    def sem(name):
        return ctx.enter_context(nc.semaphore(name))

    xz = sb("xz", [KP, NI * XZ])
    wt = sb("wt", [KP, VER, E])
    gam = sb("gam", [KP, VER, TOK])
    bet = sb("bet", [KP, VER, TOK])
    zwt = sb("zwt", [KP, ZT])
    npix = sb("npix", [KP, KP])
    ones = sb("ones", [KP, KP])
    ident = sb("ident", [KP, KP])
    selm = sb("selm", [KP, KP])
    cst = sb("cst", [KP, 5])
    col = sb("col", [KP, 12])
    tokb, lng, lnb, bv, bo = (col[:, i:i + 1] for i in range(5))
    bq, bk, psc = col[:, 5:7], col[:, 7:9], col[:, 9:11]
    wq = sb("wq", [KP, 2, KP])
    wk = sb("wk", [KP, 2, KP])
    wv = sb("wv", [KP, KP])
    wo = sb("wo", [KP, KP])
    wr = sb("wr", [KP, NEXP])

    gmean = sb("gmean", [KP, TOK])
    gbias = sb("gbias", [KP, TOK])
    qscale = sb("qscale", [KP, 2])
    qbias = sb("qbias", [KP, 2])
    kbias = sb("kbias", [KP, 2])
    qraw = sb("qraw", [KP, 6])
    selk = sb("selk", [KP, 2, KP])
    row1 = sb("row1", [1, 2, KP])
    obias = sb("obias", [KP, 1])
    mhalf = sb("mhalf", [KP, 4])

    zs = sb("zs", [KP, UN, ZT])
    part = sb("part", [KP, 4, 2])
    stat = sb("stat", [KP, 4, 2])
    ivar = sb("ivar", [KP, 4])
    istd = sb("istd", [KP, 4])
    inmr = sb("inmr", [KP, 4])
    tick = sb("tick", [1, 1])
    wrc = sb("wrc", [KP, NEXP])
    vtot = sb("vtot", [KP, 1])
    gx = sb("gx", [KP, 2, VER, TP])
    tb = sb("tb", [KP, TOK])
    yT = sb("yT", [KP, UN, TP])
    st6 = sb("st6", [HT, 2, 6])
    mv = sb("mv", [HT, 2, 2])
    ve = sb("ve", [HT, 2])
    rs = sb("rs", [HT, 2])
    x = sb("x", [HT, 2, E])
    xT = sb("xT", [KP, 2, TP])
    qT = sb("qT", [KP, 2, 2, TP])
    kT = sb("kT", [KP, 2, 2, 4, TP])
    ksq = sb("ksq", [KP, 2, TP])
    kbrow = sb("kbrow", [1, 2, KP])
    q2 = sb("q2", [KP, 2, TP])
    va = sb("va", [HT, 2, 2, HEADS, DH + 1])
    mp = sb("mp", [HT, 2, 4, 32])
    pT = sb("pT", [HT, 2, 4, 2, TP])
    oinv = sb("oinv", [HT, 2, HEADS])
    o = sb("o", [HT, 2, E])
    oT = sb("oT", [KP, TP])
    sT = sb("sT", [KP, TP])
    st6b = sb("st6b", [HT, 2, 6])
    mvb = sb("mvb", [HT, 2, 2])
    veb = sb("veb", [HT, 2])
    rsb = sb("rsb", [HT, 2])
    h2 = sb("h2", [HT, UN, 2, E])
    lg = sb("lg", [HT, UN, 2, NEXP])

    ring = [ctx.enter_context(nc.psum_tensor(f"ring{n}", [KP, 2, 512], F32)) for n in range(2)]
    bank = [ctx.enter_context(nc.psum_tensor(f"bank{i}", [KP, 512], F32)) for i in range(4, 8)]
    b4, b5, b6, b7 = bank

    s_c = sem("s_consts")
    s_ld = [sem(f"s_loaded{r}") for r in range(UN)]
    s_set = sem("s_setup")
    s_sps = sem("s_setup_psum")
    s_fill = sem("s_filled")
    s_zs = sem("s_zs")
    s_pt = sem("s_part")
    s_stp = sem("s_stat_psum")
    s_st = sem("s_stat")
    s_iv = sem("s_ivar")
    s_is = sem("s_istd")
    s_nm = sem("s_inmr")
    s_gx = sem("s_gx")
    s_cv = sem("s_conv")
    s_tb = sem("s_tb")
    s_y = sem("s_y")
    s_ht = sem("s_h_turned")
    s_hb = sem("s_h_stats")
    s_hr = sem("s_h_rstd")
    s_x = sem("s_x")
    s_xt = sem("s_x_turned")
    s_xT = sem("s_xT")
    s_q = sem("s_q_psum")
    s_qe = sem("s_q")
    s_k = sem("s_k_psum")
    s_sq = sem("s_ksq")
    s_kk = sem("s_k_whole")
    s_ke = sem("s_k")
    s_v = sem("s_v_psum")
    s_ve = sem("s_v")
    s_S = sem("s_scores")
    s_m = sem("s_max")
    s_mt = sem("s_max_turned")
    s_q2 = sem("s_q_less_max")
    s_ST = sem("s_scoresT")
    s_e = sem("s_exp")
    s_pv = sem("s_pv")
    s_oi = sem("s_oinv")
    s_on = sem("s_o")
    s_ot = sem("s_o_turned")
    s_oT = sem("s_oT")
    s_wo = sem("s_wo")
    s_s = sem("s_sum")
    s_sb = sem("s_s_turned")
    s_sn = sem("s_s_stats")
    s_sr = sem("s_s_rstd")
    s_h2 = sem("s_h2")
    s_out = [sem(f"s_stored{r}") for r in range(UN)]

    consts = [(wt, "w"), (gam, "gamma"), (bet, "beta"), (zwt, "zwt"), (npix, "npix"), (ones, "ones"),
              (ident, "ident"), (selm, "selm"), (cst, "cst"), (wr, "wr"), (wq, "wq"), (wk, "wk"), (wv, "wv"),
              (wo, "wo"), (row1, "row1")]
    columns = ("tok_b", "ln_g", "ln_b", "bv", "bo", "bq", "bk", "ps")
    NCONST = len(consts) + len(columns)
    NG = NI // UN

    def w(eng, s, v):
        if isinstance(v, int) and v <= 0:
            return
        eng.wait_ge(s, v)

    def pipeline(eng, body):
        body(-2, UN - 1)
        for r in range(UN):
            body(-1, r)
        with eng.Fori(0, NG - 2) as q:
            for r in range(UN):
                body(q, r)
        for q in (NG - 2, NG - 1):
            for r in range(UN):
                body(q, r)

    def stages(q, r):
        if not isinstance(q, int):
            return [True] * 5 + [r == UN - 1, r == 0]
        i = q * UN + r
        return [0 <= i + n < NI for n in range(5)] + [r == UN - 1 and q + 2 < NG, r == 0 and q + 1 < NG]

    block = ctx.enter_context(nc.Block())

    @block.sync
    def _(sp):
        at = 0
        for n in columns:
            sp.dma_start(col[:, at:at + A[n].shape[1]], A[n]).then_inc(s_c, 16)
            at += A[n].shape[1]

        def load(q, r):
            w(sp, s_ld[r], q * 16)
            at = (q * UN + r) * XZ
            sp.dma_start(xz[:, bass.ds(at, XZ)], A["xz"][:, bass.ds(at, XZ)]).then_inc(s_ld[r], 16)

        def store(q, r):
            first = (q * UN + r) * TOK
            sp.wait_ge(s_h2, q * UN + r + 1)
            for t, (a, n) in enumerate(((first, HT), (first + HT, HT - 1))):
                sp.dma_start(h2_dram[bass.ds(a, n), :], h2[0:n, r, t, :]).then_inc(s_out[r], 16)
                sp.dma_start(lg_dram[bass.ds(a, n), :], lg[0:n, r, t, :]).then_inc(s_out[r], 16)

        for r in range(UN):
            load(0, r)
        for t, n in consts:
            sp.dma_start(t[:], A[n]).then_inc(s_c, 16)
        for r in range(UN):
            load(1, r)
        with sp.Fori(0, NG - 2) as q:
            for r in range(UN):
                load(q + 2, r)
            for r in range(UN):
                store(q, r)
        for q in (NG - 2, NG - 1):
            for r in range(UN):
                store(q, r)
        for r in range(UN):
            sp.wait_ge(s_out[r], NG * 64)

    @block.gpsimd
    def _(pool):
        fills = ((gx[:, :, :, TOK:TP], 0.0), (yT[:, :, TOK:TP], 0.0), (mp[:], 0.0), (va[:, :, :, :, DH:DH + 1], 1.0),
                 (mhalf[:], -0.5), (kT[:], 0.0))
        assert len(fills) == FILLS
        for t, v in fills:
            nc.gpsimd.memset(t, v).then_inc(s_fill, 1)
        pool.wait_ge(s_fill, FILLS)
        pool.wait_ge(s_c, 16 * NCONST)

        def gamma(i, q, r):
            pool.wait_ge(s_ld[r], (q + 1) * 16)
            w(pool, s_cv, i - 1)
            o = gx[:, r % 2, :, 0:TOK].rearrange("p v (a b) -> p v a b", b=GRID)
            px = xz[:, bass.ds(i * XZ, TOK)].rearrange("p (a b) -> p a b", b=GRID)
            pz = xz[:, bass.ds(i * XZ + TOK, ZT)].rearrange("p (a b) -> p a b", b=ZG)
            gm = gam[:].rearrange("p v (a b) -> p v a b", b=GRID)
            nc.gpsimd.tensor_tensor(o[:, 0], px, gm[:, 0], ALU.mult)
            for v, (dy, dx) in enumerate(((1, 0), (1, 1), (0, 0), (0, 1))):
                ins = nc.gpsimd.tensor_tensor(o[:, v + 1], pz[:, dy:dy + GRID, dx:dx + GRID], gm[:, v + 1], ALU.mult)
            ins.then_inc(s_gx, 1)

        def body(q, r):
            last, att, proj, tok, more, sums, devs = stages(q, r)
            i = q * UN + r
            if devs:
                pool.wait_ge(s_iv, 2 * (q + 2))
                nc.gpsimd.tensor_tensor(istd[:], ivar[:], mhalf[:], ALU.pow).then_inc(s_is, 1)
            if tok:
                pool.wait_ge(s_hb, 3 * (i + 3) + 3)
                nc.gpsimd.tensor_tensor(rs[:], ve[:], mhalf[0:HT, 0:2], ALU.pow).then_inc(s_hr, 1)
            if last:
                pool.wait_ge(s_sn, 3 * i + 3)
                nc.gpsimd.tensor_tensor(rsb[:], veb[:], mhalf[0:HT, 0:2], ALU.pow).then_inc(s_sr, 1)
            if more:
                gamma(i + 4, q + 1, r)

        pipeline(pool, body)

    @block.tensor
    def _(pe):
        mm = nc.tensor.matmul
        pe.wait_ge(s_c, 16 * NCONST)
        for c, t in enumerate((wq[:, 0, :], wq[:, 1, :], wk[:, 0, :], wk[:, 1, :], wv[:])):
            mm(b4[:, c:c + 1], t, lnb, start=True, stop=True)
        for to, t in ((b5, gam), (b6, bet)):
            for v in range(VER):
                mm(to[:, 0:TOK], wt[:, v, :], t[:, v, :], start=(v == 0), stop=(v == VER - 1))
        mm(b7[:, 0:NEXP], ones[:], wr[:], start=True, stop=True).then_inc(s_sps, 1)
        pe.wait_ge(s_set, 3)
        mm(b4[:, 8:9], wo[:], vtot[:], start=True, stop=True).then_inc(s_sps, 1)
        pe.wait_ge(s_set, 5)
        for G in range(2):
            ins = nc.tensor.transpose(b5[0:1, G * KP:(G + 1) * KP], kbias[:, G:G + 1], ident[:])
        ins.then_inc(s_sps, 1)
        pe.wait_ge(s_set, 6)
        for G in range(2):
            ins = mm(b6[:, G * KP:(G + 1) * KP], row1[:, G, :], kbrow[:, G, :], start=True, stop=True)
        ins.then_inc(s_sps, 1)
        pe.wait_ge(s_set, SETUP)
        pe.wait_ge(s_fill, FILLS)

        def half(t):
            return slice(t * HT, t * HT + HT)

        def body(q, r):
            last, att, proj, tok, more, sums, devs = stages(q, r)
            i = q * UN + r
            a, b, c = i + 1, i + 2, i + 3

            def scoresT(n):
                G, t = n // 2, n % 2
                if n == 0:
                    pe.wait_ge(s_q2, a + 1)
                    w(pe, s_m, 4 * a + 3)
                elif n == 1:
                    w(pe, s_m, 4 * a + 4)
                else:
                    pe.wait_ge(s_e, 4 * a + n - 1)
                for g in range(4):
                    ins = mm(ring[n % 2][0:HT, g // 2, g % 2 * TP:g % 2 * TP + TP], kT[:, i_par(r, 1), G, g, half(t)],
                             q2[:, G, :], start=True, stop=True)
                ins.then_inc(s_ST, 1)

            def scores(n):
                G, t = n // 2, n % 2
                if n < 2:
                    w(pe, s_e, 4 * a + 3 + n if att else 0)
                else:
                    pe.wait_ge(s_m, 4 * b + n - 1)
                for g in range(4):
                    ins = mm(ring[n % 2][0:HT, g // 2, g % 2 * TP:g % 2 * TP + TOK], qT[:, i_par(r, 2), G, half(t)],
                             kT[:, i_par(r, 2), G, g, 0:TOK], start=True, stop=True)
                ins.then_inc(s_S, 1)

            def values(G):
                for t in range(2):
                    for h in range(4 * G, 4 * G + 4):
                        for k in range(2):
                            n = HT - k
                            at = (t * HEADS + h) * (DH + 1)
                            ins = mm(b5[0:HT, at:at + DH + 1], pT[0:n, G, h % 4, k, half(t)], va[0:n, i_par(r, 1), k, h, :],
                                     start=(k == 0), stop=(k == 1))
                return ins

            if last:
                pe.wait_ge(s_on, i + 1)
                w(pe, s_xT, min(i + 3, NI) if isinstance(i, int) else i + 3)
                for t in range(2):
                    ins = nc.tensor.transpose(b7[:, half(t)], o[:, t, :], ident[0:HT, 0:HT])
                ins.then_inc(s_ot, 1)
            if devs:
                pe.wait_ge(s_st, q + 2)
            if tok:
                pe.wait_ge(s_gx, c + 1)
                w(pe, s_h2, i)
                for v in range(VER):
                    ins = mm(b4[:, 0:TP], wt[:, v, :], gx[:, i_par(r, 3), v, :], start=(v == 0), stop=(v == VER - 1))
                ins.then_inc(s_cv, 1)
            if att:
                pe.wait_ge(s_m, 4 * a + 4)
                w(pe, s_on, a)
                pe.wait_ge(s_ve, a + 1)
                for t in range(2):
                    ins = nc.tensor.transpose(b5[:, half(t)], mp[:, t].rearrange("p g c -> p (g c)"), ident[0:HT, 0:HT])
                ins.then_inc(s_mt, 1)
            if last:
                pe.wait_ge(s_oT, i + 1)
                w(pe, s_ke, a + 1 if att else NI)
                mm(b6[:, 0:TP], wo[:], oT[:], start=True, stop=True).then_inc(s_wo, 1)
            if att:
                scoresT(0)
            if proj:
                pe.wait_ge(s_xT, b + 1)
                w(pe, s_q2, a + 1 if att else 0)
                for G in range(2):
                    ins = mm(b5[:, G * TP:G * TP + TP], wq[:, G, :], xT[:, i_par(r, 2), :], start=True, stop=True)
                ins.then_inc(s_q, 1)
            if tok:
                pe.wait_ge(s_y, c + 1)
                w(pe, s_oT, i + 1 if last else 0)
                for t in range(2):
                    ins = nc.tensor.transpose(b7[0:HT, t * E:t * E + E], yT[:, i_ring(r, 3), half(t)], ident[:])
                ins.then_inc(s_ht, 1)
            if att:
                scoresT(1)
            if proj:
                w(pe, s_s, i + 1 if last else 0)
                for G in range(2):
                    ins = mm(b6[:, G * TP:G * TP + TP], wk[:, G, :], xT[:, i_par(r, 2), :], start=(G == 0), stop=True,
                             skip_group_check=True)
                ins.then_inc(s_k, 1)
            if last:
                pe.wait_ge(s_s, i + 1)
                w(pe, s_y, c + 1 if tok else 0)
                for t in range(2):
                    nc.tensor.transpose(b4[0:HT, t * E:t * E + E], sT[:, half(t)], ident[:])
                for t in range(2):
                    ins = mm(b4[0:HT, 2 * E + t * NEXP:2 * E + (t + 1) * NEXP], sT[:, half(t)], wrc[:],
                             start=True, stop=True)
                ins.then_inc(s_sb, 1)
            if att:
                scoresT(2)
            if proj:
                pe.wait_ge(s_sq, b + 1)
                for G in range(2):
                    ins = mm(b6[:, G * TP:G * TP + TP], selk[:, G, :], ksq[:, G, :], start=False, stop=True,
                             skip_group_check=True)
                ins.then_inc(s_kk, 1)
                pe.wait_ge(s_qe, b + 1)
                for t in range(2):
                    ins = mm(b5[0:HT, t * E:t * E + E], xT[:, i_par(r, 2), half(t)], wv[:], start=True, stop=True)
                ins.then_inc(s_v, 1)
            if att:
                scoresT(3)
            if tok:
                pe.wait_ge(s_x, c + 1)
                for t in range(2):
                    ins = nc.tensor.transpose(b7[:, half(t)], x[:, t, :], ident[0:HT, 0:HT])
                ins.then_inc(s_xt, 1)
            if proj:
                pe.wait_ge(s_ke, b + 1)
                scores(0)
            if att:
                pe.wait_ge(s_e, 4 * a + 2)
                w(pe, s_ve, b + 1 if proj else 0)
                values(0)
            if proj:
                scores(1)
            if att:
                pe.wait_ge(s_e, 4 * a + 4)
                values(1).then_inc(s_pv, 1)
            if proj:
                scores(2)
                scores(3)
            if sums:
                w(pe, s_pt, q + 3)
                w(pe, s_h2, i + 1 if last else 0)
                mm(b4[:, 300:308], npix[:], part[:].rearrange("p a b -> p (a b)"), start=True, stop=True).then_inc(s_stp, 1)

        pipeline(pe, body)

    @block.scalar
    def _(act):
        act.wait_ge(s_set, SETUP)
        act.wait_ge(s_fill, FILLS)
        activation = nc.scalar.activation

        def body(q, r):
            last, att, proj, tok, more, sums, devs = stages(q, r)
            i = q * UN + r
            a, b, c = i + 1, i + 2, i + 3

            def exponentials(n):
                G, t = n // 2, n % 2
                act.wait_ge(s_ST, 4 * a + n + 1)
                activation(pT[:, G, :, t, :].rearrange("p (u g) c -> p u g c", u=2),
                           ring[n % 2][0:HT, :, 0:2 * TP].rearrange("p u (g c) -> p u g c", g=2), ACT.Exp).then_inc(s_e, 1)

            if last:
                act.wait_ge(s_ot, i + 1)
                activation(oT[:], b7[:, 0:TP], ACT.Copy).then_inc(s_oT, 1)
            if att:
                w(act, s_pv, a)
                exponentials(0)
            if proj:
                act.wait_ge(s_q, b + 1)
                for G in range(2):
                    ins = activation(qT[:, i_par(r, 2), G, :], b5[:, G * TP:G * TP + TP], ACT.Identity,
                                     bias=qbias[:, G:G + 1], scale=qscale[:, G:G + 1])
                ins.then_inc(s_qe, 1)
            if att:
                exponentials(1)
            if proj:
                act.wait_ge(s_k, b + 1)
                w(act, s_kk, b)
                for G in range(2):
                    ins = activation(ksq[:, G, :], b6[:, G * TP:G * TP + TP], ACT.Square, bias=kbias[:, G:G + 1])
                ins.then_inc(s_sq, 1)
            if att:
                exponentials(2)
            if proj:
                act.wait_ge(s_kk, b + 1)
                for g in range(4):
                    p = slice(32 * g, 32 * g + 32)
                    ins = activation(kT[p, i_par(r, 2), :, g, :],
                                     b6[p, 0:2 * TP].rearrange("p (t c) -> p t c", t=2), ACT.Copy)
                ins.then_inc(s_ke, 1)
                act.wait_ge(s_v, b + 1)
                w(act, s_pv, b - 1)
                activation(va[:, i_par(r, 2), :, :, 0:DH],
                           b5[0:HT, 0:2 * E].rearrange("p (t h d) -> p t h d", t=2, d=DH), ACT.Copy).then_inc(s_ve, 1)
            if att:
                exponentials(3)
            if tok:
                act.wait_ge(s_xt, c + 1)
                activation(xT[:, i_par(r, 3), :], b7[:, 0:TP], ACT.Copy).then_inc(s_xT, 1)

        pipeline(act, body)

    @block.vector
    def _(dve):
        V = nc.vector
        dve.wait_ge(s_c, 16 * NCONST)
        V.tensor_scalar(qscale[:], psc, cst[:, 1:2], cst[:, 0:1], ALU.mult, ALU.add)
        for G in range(2):
            V.tensor_scalar(selk[:, G, :], selm[:], psc[:, G:G + 1], -1.0, ALU.mult, ALU.mult)
        dve.wait_ge(s_sps, 1)
        V.tensor_tensor(qraw[:, 0:2], b4[:, 0:2], bq, ALU.add).then_inc(s_set, 1)
        V.tensor_tensor(qraw[:, 2:4], b4[:, 2:4], bk, ALU.add).then_inc(s_set, 1)
        V.tensor_tensor(vtot[:], b4[:, 4:5], bv, ALU.add).then_inc(s_set, 1)
        dve.wait_ge(s_set, 3)
        V.tensor_tensor(qraw[:, 4:6], qraw[:, 0:2], qscale[:], ALU.mult).then_inc(s_set, 1)
        V.tensor_tensor(kbias[:], qraw[:, 2:4], cst[:, 3:5], ALU.add)
        V.tensor_copy(gmean[:], b5[:, 0:TOK])
        V.tensor_scalar(gbias[:], b6[:, 0:TOK], tokb, None, ALU.add)
        V.tensor_tensor(wrc[:], wr[:], b7[:, 0:NEXP], ALU.subtract)
        for t in (wq[:, 0, :], wq[:, 1, :], wk[:, 0, :], wk[:, 1, :], wv[:]):
            V.tensor_scalar(t, t, lng, None, ALU.mult)
        dve.wait_ge(s_set, 4)
        V.tensor_scalar(qbias[:], qraw[:, 4:6], cst[:, 2:3], None, ALU.add)
        dve.wait_ge(s_sps, 2)
        V.tensor_tensor(obias[:], b4[:, 8:9], bo, ALU.add).then_inc(s_set, 1)
        dve.wait_ge(s_sps, 3)
        V.tensor_copy(kbrow[:].rearrange("p g c -> p (g c)"), b5[0:1, 0:2 * KP]).then_inc(s_set, 1)
        dve.wait_ge(s_sps, 4)
        V.tensor_tensor(selk[:].rearrange("p g c -> p (g c)"), selk[:].rearrange("p g c -> p (g c)"), b6[:, 0:2 * KP],
                        ALU.add).then_inc(s_set, 1)
        dve.wait_ge(s_set, SETUP)
        dve.wait_ge(s_fill, FILLS)

        def norm_stats(src, six, two, var, s, i):
            for t in range(2):
                ins = V.bn_stats(six[:, t, :], src[0:HT, t * E:t * E + E])
            ins.then_inc(s, 1)
            dve.wait_ge(s, 3 * i + 1)
            V.memset(tick[:], 0.0)
            for t in range(2):
                ins = V.bn_aggr(two[:, t, :], six[:, t, :])
            ins.then_inc(s, 1)
            dve.wait_ge(s, 3 * i + 2)
            V.tensor_scalar(var[:], two[:, :, 1], LN_EPS, None, ALU.add).then_inc(s, 1)

        def body(q, r):
            last, att, proj, tok, more, sums, devs = stages(q, r)
            i = q * UN + r
            a, b, c = i + 1, i + 2, i + 3
            if tok:
                k = (r + 3) % UN
                dve.wait_ge(s_nm, q + (2 if r >= 1 else 1))
                V.scalar_tensor_tensor(tb[:], gmean[:], inmr[:, k:k + 1], gbias[:], ALU.mult, ALU.add).then_inc(s_tb, 1)
                dve.wait_ge(s_cv, c + 1)
                dve.wait_ge(s_tb, c + 1)
                V.scalar_tensor_tensor(yT[:, k, 0:TOK], b4[:, 0:TOK], istd[:, k:k + 1], tb[:], ALU.mult,
                                       ALU.add).then_inc(s_y, 1)
            if devs:
                dve.wait_ge(s_st, q + 2)
                V.tensor_tensor(ivar[:], stat[:, :, 0], stat[:, :, 0], ALU.mult).then_inc(s_iv, 1)
                dve.wait_ge(s_iv, 2 * (q + 1) + 1)
                V.scalar_tensor_tensor(ivar[:], stat[:, :, 1], TOK_EPS, ivar[:], ALU.add, ALU.subtract).then_inc(s_iv, 1)
            if att:
                dve.wait_ge(s_mt, a + 1)
                V.tensor_tensor(q2[:], qT[:, i_par(r, 1)], b5[:, 0:TP].unsqueeze(1).to_broadcast([KP, 2, TP]),
                                ALU.add).then_inc(s_q2, 1)
            if last:
                dve.wait_ge(s_wo, i + 1)
                w(dve, s_sb, i)
                V.scalar_tensor_tensor(sT[:], b6[:, 0:TP], obias[:, 0:1], yT[:, r, :], ALU.add,
                                       ALU.add).then_inc(s_s, 1)
            if tok:
                dve.wait_ge(s_ht, c + 1)
                norm_stats(b7, st6, mv, ve, s_hb, c)
            if devs:
                dve.wait_ge(s_is, q + 2)
                V.scalar_tensor_tensor(inmr[:], stat[:, :, 0], -1.0, istd[:], ALU.mult, ALU.mult).then_inc(s_nm, 1)
            if last:
                dve.wait_ge(s_sb, i + 1)
                norm_stats(b4, st6b, mvb, veb, s_sn, i)
            if tok:
                dve.wait_ge(s_hr, c + 1)
                w(dve, s_xt, c)
                for t in range(2):
                    ins = V.tensor_scalar(x[:, t, :], b7[0:HT, t * E:t * E + E], mv[:, t, 0:1], rs[:, t:t + 1],
                                          ALU.subtract, ALU.mult)
                ins.then_inc(s_x, 1)
            if last:
                dve.wait_ge(s_sr, i + 1)
                w(dve, s_out[r], q * 64)
                V.tensor_tensor(lg[:, r], b4[0:HT, 2 * E:2 * E + 2 * NEXP].rearrange("p (t e) -> p t e", t=2),
                                rsb[:].unsqueeze(2).to_broadcast([HT, 2, NEXP]), ALU.mult)
                for t in range(2):
                    ins = V.tensor_scalar(h2[:, r, t, :], b4[0:HT, t * E:t * E + E], mvb[:, t, 0:1], rsb[:, t:t + 1],
                                          ALU.subtract, ALU.mult)
                ins.then_inc(s_h2, 1)
            if sums:
                at = (q + 2) * (UN * XZ)
                for n in range(UN):
                    dve.wait_ge(s_ld[n], (q + 3) * 16)
                z = [xz[:, bass.ds(at + n * XZ + TOK, ZT)] for n in range(UN)]
                for n in range(UN):
                    ins = V.scalar_tensor_tensor(zs[:, n, :], z[n], 1.0, zwt[:], ALU.mult, ALU.mult,
                                                 accum_out=part[:, n, 0:1])
                ins.then_inc(s_zs, 1)
                dve.wait_ge(s_zs, q + 3)
                for n in range(UN):
                    ins = V.scalar_tensor_tensor(zs[:, n, :], zs[:, n, :], 1.0, z[n], ALU.mult, ALU.mult,
                                                 accum_out=part[:, n, 1:2])
                ins.then_inc(s_pt, 1)

            def maxima(n):
                G, t = n // 2, n % 2
                dve.wait_ge(s_S, 4 * b + n + 1)
                if n == 0:
                    w(dve, s_mt, b)
                V.tensor_reduce(mp[:, t, :, 29 + G].rearrange("p (u g) -> p u g", u=2),
                                ring[n % 2][0:HT, :, 0:2 * TP].rearrange("p u (g c) -> p u g c", g=2)[:, :, :, 0:TOK],
                                AX.X, ALU.max, negate=True).then_inc(s_m, 1)

            if proj:
                maxima(0)
                maxima(1)
            if att:
                dve.wait_ge(s_pv, a + 1)
                ov = b5[0:HT, 0:2 * HEADS * (DH + 1)].rearrange("p (t h d) -> p t h d", t=2, d=DH + 1)
                V.reciprocal(oinv[:], ov[:, :, :, DH]).then_inc(s_oi, 1)
                dve.wait_ge(s_oi, a + 1)
                w(dve, s_ot, a)
                V.tensor_tensor(o[:].rearrange("p t (h d) -> p t h d", d=DH), ov[:, :, :, 0:DH],
                                oinv[:].unsqueeze(3).to_broadcast([HT, 2, HEADS, DH]), ALU.mult).then_inc(s_on, 1)
            if proj:
                maxima(2)
                maxima(3)
            if sums:
                dve.wait_ge(s_stp, q + 3)
                V.tensor_copy(stat[:].rearrange("p a b -> p (a b)"), b4[:, 300:308]).then_inc(s_st, 1)

        pipeline(dve, body)


def experts(nc, ctx, A, h2_dram, lg_dram, e_dram, t_dram, acc_dram, out):

    def sb(name, shape, dt=F32):
        return ctx.enter_context(nc.sbuf_tensor(name, shape, dt))

    def sem(name):
        return ctx.enter_context(nc.semaphore(name))

    W3 = NEXP * R
    TAB = 2 * R + 1
    NB = CAP // 128
    BITS = 30
    CT = 13
    NCH = R // CT
    ON_ACT = 8

    ident = sb("ident2", [128, 128])
    ones = sb("ones2", [R, R])
    tri = sb("tri", [R, R])
    blk = sb("blk", [128, 128])
    reset = sb("reset", [R, W3])
    slots = sb("slots", [R, CAP])
    slot1 = sb("slot1", [128, NB])
    iota = sb("iota", [128, R])
    rowbase = sb("rowbase", [R, 1])
    bits = sb("bits", [128, BITS], U32)
    b1 = sb("b1", [128, NEXP * 4])
    b2 = sb("b2", [128, NEXP * E])

    lrow = sb("lrow", [R, W3])
    pr = sb("pr", [R, NEXP, R])
    mx = sb("mx", [R, NEXP])
    gm = sb("gm", [NEXP, 1])
    dg = sb("dg", [NEXP, NEXP])
    mb = sb("mb", [R, NEXP])
    tot = sb("tot", [R, NEXP])
    rtot = sb("rtot", [R, NEXP])
    pe_ = sb("pe_", [128, CHUNK])
    ge = sb("ge", [128, CHUNK])
    cnt = sb("cnt", [128, 1])
    cand = sb("cand", [128, 1])
    pick = sb("pick", [128, 1])
    thr = sb("thr", [128, 1])
    tb = sb("thr_rows", [R, NEXP])
    gt = sb("gt", [R, NEXP, R])
    eq = sb("eq", [R, NEXP, R])
    run = sb("run", [R, NEXP, R])
    ng = sb("ng", [R, NEXP])
    te = sb("te", [R, NEXP])
    room = sb("room", [R, NEXP])
    start = sb("start", [R, NEXP])
    end = sb("end", [R, NEXP])
    tab = sb("tab", [R, NEXP * TAB])
    oh0 = sb("oh0", [R, CAP])
    oh = sb("oh", [R, CAP])
    tabs = sb("tabs", [128, NB, TAB])
    jk = sb("jk", [128, NB, R])
    loc = sb("loc", [128, NB])
    wgt = sb("wgt", [128, 2, NB])
    idx = sb("idx", [128, 2, NB], U32)
    xg = sb("xg", [128, 2, NB, E])
    xgT = sb("xgT", [128, 2, UNIT])
    w1 = sb("w1", [128, 2, FF])
    w2 = sb("w2", [128, 2, 4, E])
    hT = sb("hT", [128, 2, 4, UNIT])
    yb = sb("yb", [128, NBLK, E])
    yw = sb("yw", [128, 2, NBLK, E])
    fin = sb("fin", [R, 3, CT, E])
    fout = sb("fout", [R, 2, CT, E])
    f6 = sb("f6", [R, CT, 6])
    fmv = sb("fmv", [R, 2, CT, 2])
    fve = sb("fve", [R, CT])
    frs = sb("frs", [R, 2, CT])
    fnm = sb("fnm", [R, 2, CT])
    half = sb("half", [128, CT])
    b1e = sb("b1e", [128, 2, 4])

    def pb(name):
        return ctx.enter_context(nc.psum_tensor(name, [128, 512], F32))

    bI = [pb("bI0"), pb("bI1")]
    bX = pb("bX")
    bH = [pb("bH0"), pb("bH1"), pb("bH2")]
    bO = [pb("bO0"), pb("bO1")]

    s_c = sem("s2_consts")
    s_l = sem("s_logits")
    s_copy = sem("s_acc_copied")
    s_half = sem("s_half")
    s_d = sem("s_dve")
    s_pe = sem("s_routing_psum")
    s_sh = sem("s_shifted")
    s_ex = sem("s_exp2")
    s_est = sem("s_exp_stored")
    s_eld = sem("s_exp_loaded")
    s_cnt = sem("s_count")
    s_sum = sem("s_count_sum")
    s_cand = sem("s_cand")
    s_pick = sem("s_pick")
    s_thr = sem("s_thr")
    s_tst = sem("s_thr_stored")
    s_tld = sem("s_thr_loaded")
    s_tab = sem("s_table")
    s_o0 = sem("s_onehot_half")
    s_oh = sem("s_onehot")
    s_ix = sem("s_index_psum")
    s_ie = sem("s_index_copied")
    s_loc = sem("s_loc")
    s_idx = sem("s_idx")
    s_g = [[sem(f"s_gathered{p}{u}") for u in range(2)] for p in range(2)]
    s_w = [sem(f"s_weights{p}") for p in range(2)]
    s_xp = sem("s_xg_turned")
    s_xe = sem("s_xgT")
    s_h = sem("s_h_psum")
    s_held = sem("s_held")
    s_b1 = sem("s_b1")
    s_ge = sem("s_gelu")
    s_o = sem("s_o_psum")
    s_yb = sem("s_y_biased")
    s_yw = sem("s_y_weighted")
    s_sc = [sem(f"s_scattered{p}") for p in range(2)]
    s_fl = [sem(f"s_fin_loaded{n}") for n in range(3)]
    s_f6 = sem("s_fin_stats")
    s_fr = sem("s_fin_rstd")
    s_fn = sem("s_fin_nmr")
    s_fa = sem("s_fin_act")
    s_fv = sem("s_fin_dve")
    s_fs = [sem(f"s_fin_stored{n}") for n in range(2)]

    consts = [(ident, "ident"), (ones, "ones1"), (tri, "tri"), (blk, "blk"), (reset, "reset"), (slots, "slots"),
              (slot1, "slot1"), (iota, "iota"), (rowbase, "rowbase"), (bits, "bits"), (b1, "b1"), (b2, "b2")]

    def w(eng, s, v):
        if isinstance(v, int) and v <= 0:
            return
        eng.wait_ge(s, v)

    def pipeline(eng, body):
        body(-1, 1)
        for p in range(2):
            body(0, p)
        with eng.Fori(1, NEXP // 2 - 1) as q:
            for p in range(2):
                body(q, p)
        for p in range(2):
            body(NEXP // 2 - 1, p)

    def stages(q, p):
        if not isinstance(q, int):
            return True, True
        e = 2 * q + p
        return e >= 0, e + 1 < NEXP

    def rows(d):
        return d.rearrange("(p t) e -> p t e", p=R)

    block = ctx.enter_context(nc.Block())

    @block.sync
    def _(sp):
        sp.dma_start(lrow[:], lg_dram.rearrange("(p t) e -> p (t e)", p=R)).then_inc(s_l, 16)
        for t, n in consts:
            sp.dma_start(t[:], A[n]).then_inc(s_c, 16)

        def weights(q, p):
            e = 2 * q + p
            w(sp, s_o, 2 * (e - 1))
            sp.dma_start(w1[:, p, :], A["W1"][bass.ds(e, 1)].rearrange("e d f -> d (e f)")).then_inc(s_w[p], 16)
            sp.dma_start(w2[:, p], A["W2"][bass.ds(e, 1)].rearrange("e (c f) d -> f (e c) d", c=4)).then_inc(s_w[p], 16)

        weights(0, 0)
        weights(0, 1)
        sp.wait_ge(s_ex, 1)
        sp.dma_start(e_dram.rearrange("e (p t) -> p e t", p=R), pr[:]).then_inc(s_est, 16)
        sp.wait_ge(s_est, 16)
        sp.dma_start(pe_[:], e_dram.rearrange("e (c m) -> (e c) m", c=16)).then_inc(s_eld, 16)
        sp.dma_start(acc_dram, h2_dram).then_inc(s_copy, 16)
        sp.wait_ge(s_thr, BITS + 1)
        sp.dma_start(t_dram.rearrange("o e -> e o"), thr[0:128:16, :]).then_inc(s_tst, 16)
        sp.wait_ge(s_tst, 16)
        sp.dma_start(tb[:], t_dram.to_broadcast([R, NEXP])).then_inc(s_tld, 16)
        with sp.Fori(1, NEXP // 2) as q:
            for p in range(2):
                weights(q, p)
        for p in range(2):
            sp.wait_ge(s_sc[p], 16 * NBLK * NEXP)

        def store(n):
            sp.wait_ge(s_fa, n + 1)
            sp.wait_ge(s_fv, n + 1)
            sp.dma_start(rows(out)[:, n * CT:(n + 1) * CT, :], fout[:, n % 2]).then_inc(s_fs[n % 2], 16)

        for n in range(NCH):
            if n >= 3:
                sp.wait_ge(s_fa, n - 2)
                sp.wait_ge(s_fv, n - 2)
            sp.dma_start(fin[:, n % 3], rows(acc_dram)[:, n * CT:(n + 1) * CT, :]).then_inc(s_fl[n % 3], 16)
            if n >= 2:
                store(n - 2)
        store(NCH - 2)
        store(NCH - 1)
        for n in range(2):
            sp.wait_ge(s_fs[n], 16 * (NCH // 2))

    @block.gpsimd
    def _(pool):
        nc.gpsimd.memset(half[:], -0.5).then_inc(s_half, 1)
        pool.wait_ge(s_copy, 16)
        pool.wait_ge(s_half, 1)

        def held():
            pool.sem_inc(s_held, 1)

        def body(q, p):
            ffn, index = stages(q, p)
            e = 2 * q + p
            n = 1 - p
            if index:
                pool.wait_ge(s_idx, e + 2)
                w(pool, s_xp, 2 * e)
                held()
                for k in range(NB):
                    nc.gpsimd.indirect_dma_start(
                        out=xg[:, n, k, :], out_offset=None, in_=h2_dram,
                        in_offset=bass.IndirectOffsetOnAxis(ap=idx[:, n, k:k + 1], axis=0),
                    ).then_inc(s_g[n][k // NBLK], 16)
            if ffn:
                for u in range(2):
                    pool.wait_ge(s_yw, 2 * e + u + 1)
                    if u == 0:
                        for v in range(2):
                            w(pool, s_sc[v], 16 * NBLK * e)
                    held()
                    for k in range(NBLK):
                        nc.gpsimd.indirect_dma_start(
                            out=acc_dram, in_=yw[:, u, k, :], in_offset=None,
                            out_offset=bass.IndirectOffsetOnAxis(ap=idx[:, p, u * NBLK + k:u * NBLK + k + 1], axis=0),
                            compute_op=ALU.add,
                        ).then_inc(s_sc[u], 16)

        pipeline(pool, body)
        for n in range(NCH):
            pool.wait_ge(s_f6, 3 * n + 3)
            nc.gpsimd.tensor_tensor(frs[:, n % 2, :], fve[:], half[0:R, :], ALU.pow).then_inc(s_fr, 1)

    @block.tensor
    def _(pe):
        mm = nc.tensor.matmul
        pe.wait_ge(s_c, 16 * len(consts))
        pe.wait_ge(s_d, D_MAX)
        nc.tensor.transpose(bX[0:NEXP, 0:R], mx[:], ident[0:R, 0:R]).then_inc(s_pe, 1)
        pe.wait_ge(s_d, D_DIAG)
        mm(bX[0:R, 0:NEXP], ones[0:NEXP, :], dg[:], start=True, stop=True).then_inc(s_pe, 1)
        pe.wait_ge(s_d, D_TOT)
        mm(bX[0:R, 0:NEXP], ones[:], tot[:], start=True, stop=True).then_inc(s_pe, 1)
        with pe.Fori(0, BITS) as i:
            pe.wait_ge(s_cnt, i + 1)
            mm(bI[0][:, 0:1], blk[:], cnt[:], start=True, stop=True).then_inc(s_sum, 1)
        pe.wait_ge(s_d, D_TIES)
        mm(bX[0:R, 0:NEXP], ones[:], ng[:], start=True, stop=False)
        mm(bX[0:R, 0:NEXP], tri[:], te[:], start=False, stop=True).then_inc(s_pe, 1)
        pe.wait_ge(s_d, D_SEL)
        mm(bX[0:R, 0:NEXP], tri[:], te[:], start=True, stop=True).then_inc(s_pe, 1)
        pe.wait_ge(s_tab, 1)

        def body(q, p):
            ffn, index = stages(q, p)
            e = 2 * q + p

            def tables(k):
                if k == 0:
                    pe.wait_ge(s_oh, e + 2)
                w(pe, s_ie, 4 * (e + 1) + k - 1)
                for c in range(2):
                    at = (2 * k + c) * 128
                    ins = mm(bI[k % 2][:, c * TAB:(c + 1) * TAB], oh[:, at:at + 128], tab[:, bass.ds((e + 1) * TAB, TAB)],
                             start=True, stop=True)
                ins.then_inc(s_ix, 1)

            def layers(u):
                n = 2 * e + u
                pe.wait_ge(s_g[p][u], (q + 1) * 16 * NBLK)
                w(pe, s_xe, n)
                for k in range(NBLK):
                    ins = nc.tensor.transpose(bX[:, k * 128:(k + 1) * 128], xg[:, p, u * NBLK + k, :], ident[:])
                ins.then_inc(s_xp, 1)
                if u == 0:
                    pe.wait_ge(s_w[p], (q + 1) * 32)
                pe.wait_ge(s_xe, n + 1)
                for f in range(4):
                    if f % 3 == 0:
                        w(pe, s_ge, 4 * n + f // 3)
                    mm(bH[f % 3][:], w1[:, p, f * 128:(f + 1) * 128], xgT[:, u, :], start=True, stop=True).then_inc(s_h, 1)
                pe.wait_ge(s_ge, 4 * n + 4)
                w(pe, s_yb, n - 1)
                for k in range(NBLK):
                    for f in range(4):
                        ins = mm(bO[u][:, k * E:(k + 1) * E], hT[:, u, f, k * 128:(k + 1) * 128], w2[:, p, f, :],
                                 start=(f == 0), stop=(f == 3))
                ins.then_inc(s_o, 1)

            if ffn:
                layers(0)
            if index:
                for k in range(NB // 2):
                    tables(k)
            if ffn:
                layers(1)

        pipeline(pe, body)

    @block.scalar
    def _(act):
        activation = nc.scalar.activation
        act.wait_ge(s_sh, 1)
        activation(pr[:], pr[:], ACT.Exp).then_inc(s_ex, 1)
        act.wait_ge(s_c, 16 * len(consts))

        def body(q, p):
            ffn, index = stages(q, p)
            e = 2 * q + p

            def gelus(u):
                n = 2 * e + u
                if u == 0:
                    activation(b1e[:, p, :], b1[:, bass.ds(e * 4, 4)], ACT.Copy).then_inc(s_b1, 1)
                    act.wait_ge(s_b1, e + 1)
                for f in range(4):
                    act.wait_ge(s_h, 4 * n + f + 1)
                    if f == 0:
                        w(act, s_o, n - 1)
                    activation(hT[:, u, f, :], bH[f % 3][:], ACT.Gelu,
                               bias=b1e[:, p, f:f + 1]).then_inc(s_ge, 1)

            if ffn:
                gelus(0)
            if index:
                for k in range(NB // 2):
                    act.wait_ge(s_ix, 4 * (e + 1) + k + 1)
                    if k == 0:
                        w(act, s_idx, e + 1)
                    activation(tabs[:, 2 * k:2 * k + 2, :].rearrange("p k c -> p (k c)"), bI[k % 2][:, 0:2 * TAB],
                               ACT.Copy).then_inc(s_ie, 1)
            if ffn:
                gelus(1)

        pipeline(act, body)
        for n in range(NCH):
            act.wait_ge(s_fn, n + 1)
            if n >= 2:
                act.wait_ge(s_fs[n % 2], 16 * (n // 2))
            for t in range(ON_ACT):
                ins = activation(fout[:, n % 2, t, :], fin[:, n % 3, t, :], ACT.Identity, bias=fnm[:, n % 2, t:t + 1],
                                 scale=frs[:, n % 2, t:t + 1])
            ins.then_inc(s_fa, 1)

    @block.vector
    def _(dve):
        V = nc.vector
        done = [0]

        def link(ins):
            done[0] += 1
            ins.then_inc(s_d, 1)
            dve.wait_ge(s_d, done[0])

        def over(t):
            return t[:].unsqueeze(2).to_broadcast([R, NEXP, R])

        def flat(t):
            return t[:].rearrange("p e t -> p (e t)")

        dve.wait_ge(s_l, 16)
        link(V.tensor_copy(pr[:], lrow[:].rearrange("p (t e) -> p e t", e=NEXP)))
        link(V.tensor_reduce(mx[:], pr[:], AX.X, ALU.max))
        assert done[0] == D_MAX
        dve.wait_ge(s_pe, 1)
        link(V.tensor_reduce(gm[:], bX[0:NEXP, 0:R], AX.X, ALU.max))
        dve.wait_ge(s_c, 16 * len(consts))
        link(V.tensor_scalar(dg[:], ident[0:NEXP, 0:NEXP], gm[:, 0:1], None, ALU.mult))
        assert done[0] == D_DIAG
        dve.wait_ge(s_pe, 2)
        link(V.tensor_copy(mb[:], bX[0:R, 0:NEXP]))
        V.tensor_tensor(pr[:], pr[:], over(mb), ALU.subtract).then_inc(s_sh, 1)
        dve.wait_ge(s_ex, 1)
        link(V.tensor_reduce(tot[:], pr[:], AX.X, ALU.add))
        assert done[0] == D_TOT
        dve.wait_ge(s_pe, 3)
        link(V.reciprocal(rtot[:], bX[0:R, 0:NEXP]))
        link(V.tensor_tensor(tab[:].rearrange("p (e c) -> p e c", c=TAB)[:, :, R:2 * R], pr[:], over(rtot), ALU.mult))
        V.tensor_copy(tab[:].rearrange("p (e c) -> p e c", c=TAB)[:, :, 2 * R],
                      rowbase[:, 0:1].to_broadcast([R, NEXP]))

        V.memset(thr[:], 0.0).then_inc(s_thr, 1)
        dve.wait_ge(s_eld, 16)
        with dve.Fori(0, BITS) as i:
            dve.wait_ge(s_thr, i + 1)
            V.tensor_tensor(cand[:].bitcast(U32), thr[:].bitcast(U32), bits[:, bass.ds(i, 1)],
                            ALU.bitwise_or).then_inc(s_cand, 1)
            dve.wait_ge(s_cand, i + 1)
            V.tensor_scalar(ge[:], pe_[:], cand[:, 0:1], 0.0, ALU.is_ge, ALU.add, accum_out=cnt[:]).then_inc(s_cnt, 1)
            dve.wait_ge(s_sum, i + 1)
            V.scalar_tensor_tensor(pick[:], bI[0][:, 0:1], CAP - 0.5, cand[:], ALU.is_ge, ALU.mult).then_inc(s_pick, 1)
            dve.wait_ge(s_pick, i + 1)
            V.tensor_tensor(thr[:], thr[:], pick[:], ALU.max).then_inc(s_thr, 1)

        dve.wait_ge(s_tld, 16)
        V.tensor_tensor(gt[:], pr[:], over(tb), ALU.is_gt)
        link(V.tensor_tensor(eq[:], pr[:], over(tb), ALU.is_equal))
        V.tensor_reduce(ng[:], gt[:], AX.X, ALU.add)
        link(V.tensor_tensor_scan(flat(run), reset[:], flat(eq), 0.0, ALU.mult, ALU.add))
        link(V.tensor_copy(te[:], run[:, :, R - 1]))
        assert done[0] == D_TIES
        dve.wait_ge(s_pe, 4)
        link(V.tensor_scalar(room[:], bX[0:R, 0:NEXP], -1.0, float(CAP), ALU.mult, ALU.add))
        link(V.tensor_tensor(run[:], run[:], over(room), ALU.is_le))
        link(V.tensor_tensor(run[:], run[:], eq[:], ALU.mult))
        link(V.tensor_tensor(gt[:], gt[:], run[:], ALU.add))
        link(V.tensor_tensor_scan(flat(run), reset[:], flat(gt), 0.0, ALU.mult, ALU.add))
        link(V.tensor_copy(te[:], run[:, :, R - 1]))
        assert done[0] == D_SEL
        dve.wait_ge(s_pe, 5)
        link(V.tensor_copy(start[:], bX[0:R, 0:NEXP]))
        V.tensor_tensor(end[:], start[:], te[:], ALU.add)
        link(V.tensor_tensor(run[:], run[:], over(start), ALU.add))
        V.tensor_tensor(tab[:].rearrange("p (e c) -> p e c", c=TAB)[:, :, 0:R], run[:], gt[:], ALU.mult).then_inc(s_tab, 1)
        dve.wait_ge(s_tab, 1)

        def body(q, p):
            ffn, index = stages(q, p)
            e = 2 * q + p
            n = 1 - p

            def onehot():
                w(dve, s_ix, 4 * (e + 1))
                V.tensor_scalar(oh0[:], slots[:], start[:, bass.ds(e + 1, 1)], None, ALU.is_ge).then_inc(s_o0, 1)
                dve.wait_ge(s_o0, e + 2)
                V.scalar_tensor_tensor(oh[:], slots[:], end[:, bass.ds(e + 1, 1)], oh0[:], ALU.is_lt,
                                       ALU.mult).then_inc(s_oh, 1)

            def numbers():
                for k in range(NB):
                    if k % 2 == 0:
                        dve.wait_ge(s_ie, 4 * (e + 1) + k // 2 + 1)
                    if k == 0:
                        for v in range(2):
                            w(dve, s_sc[v], 16 * NBLK * e)
                        w(dve, s_idx, e + 1)
                    V.scalar_tensor_tensor(jk[:, k, :], tabs[:, k, 0:R], slot1[:, k:k + 1], iota[:], ALU.is_equal,
                                           ALU.mult, accum_out=loc[:, k:k + 1])
                    ins = V.scalar_tensor_tensor(tabs[:, k, R:2 * R], tabs[:, k, 0:R], slot1[:, k:k + 1],
                                                 tabs[:, k, R:2 * R], ALU.is_equal, ALU.mult,
                                                 accum_out=wgt[:, n, k:k + 1])
                ins.then_inc(s_loc, 1)
                dve.wait_ge(s_loc, e + 2)
                V.tensor_tensor(idx[:, n, :], loc[:], tabs[:, :, 2 * R], ALU.add).then_inc(s_idx, 1)

            def turned(u):
                m = 2 * e + u
                dve.wait_ge(s_xp, m + 1)
                w(dve, s_h, 4 * (m - 1))
                V.tensor_copy(xgT[:, u, :], bX[:]).then_inc(s_xe, 1)

            def weighted(u):
                m = 2 * e + u
                dve.wait_ge(s_o, m + 1)
                w(dve, s_yw, m)
                V.tensor_tensor(yb[:], bO[u][:].rearrange("p (k c) -> p k c", c=E),
                                b2[:, bass.ds(e * E, E)].unsqueeze(1).to_broadcast([128, NBLK, E]),
                                ALU.add).then_inc(s_yb, 1)
                dve.wait_ge(s_yb, m + 1)
                w(dve, s_sc[u], 16 * NBLK * e)
                V.tensor_tensor(yw[:, u], yb[:], wgt[:, p, u * NBLK:(u + 1) * NBLK].unsqueeze(2).to_broadcast([128, NBLK, E]),
                                ALU.mult).then_inc(s_yw, 1)

            if index:
                onehot()
            if ffn:
                turned(0)
                weighted(0)
            if index:
                numbers()
            if ffn:
                turned(1)
                weighted(1)

        pipeline(dve, body)
        for n in range(NCH):
            dve.wait_ge(s_fl[n % 3], 16 * (n // 3 + 1))
            if n >= 2:
                dve.wait_ge(s_fa, n - 1)
            for t in range(CT):
                ins = V.bn_stats(f6[:, t, :], fin[:, n % 3, t, :])
            ins.then_inc(s_f6, 1)
            dve.wait_ge(s_f6, 3 * n + 1)
            for t in range(CT):
                ins = V.bn_aggr(fmv[:, n % 2, t, :], f6[:, t, :])
            ins.then_inc(s_f6, 1)
            dve.wait_ge(s_f6, 3 * n + 2)
            V.tensor_scalar(fve[:], fmv[:, n % 2, :, 1], LN_EPS, None, ALU.add).then_inc(s_f6, 1)
            dve.wait_ge(s_fr, n + 1)
            V.scalar_tensor_tensor(fnm[:, n % 2, :], fmv[:, n % 2, :, 0], -1.0, frs[:, n % 2, :], ALU.mult,
                                   ALU.mult).then_inc(s_fn, 1)
            if n >= 2:
                dve.wait_ge(s_fs[n % 2], 16 * (n // 2))
            for t in range(ON_ACT, CT):
                ins = V.tensor_scalar(fout[:, n % 2, t, :], fin[:, n % 3, t, :], fmv[:, n % 2, t, 0:1],
                                      frs[:, n % 2, t:t + 1], ALU.subtract, ALU.mult)
            ins.then_inc(s_fv, 1)


D_MAX, D_DIAG, D_TOT, D_TIES, D_SEL = 2, 4, 6, 11, 17


def program(nc, A, out):
    h2_dram = nc.dram_tensor("h2_rows", [NTOK, E], F32, kind=A["kind"]).ap()
    lg_dram = nc.dram_tensor("logit_rows", [NTOK, NEXP], F32, kind=A["kind"]).ap()
    e_dram = nc.dram_tensor("exp_rows", [NEXP, NTOK], F32, kind="Internal").ap()
    t_dram = nc.dram_tensor("thresholds", [1, NEXP], F32, kind="Internal").ap()
    acc_dram = nc.dram_tensor("acc_rows", [NTOK, E], F32, kind=A["kind"]).ap()
    with ExitStack() as ctx:
        tower_tokens(nc, ctx, A, h2_dram, lg_dram)
    with ExitStack() as ctx:
        experts(nc, ctx, A, h2_dram, lg_dram, e_dram, t_dram, acc_dram, out)


def layouts(i):
    f = {k: np.asarray(v) for k, v in i.items()}
    x = f["x"]
    plain = x.reshape(NI, CH, GRID, PATCH, GRID, PATCH).transpose(1, 3, 5, 0, 2, 4).reshape(KP, NI, TOK)
    pad = np.pad(x, ((0, 0), (0, 0), (SHIFT, SHIFT), (SHIFT, SHIFT)))
    shifted = pad.reshape(NI, CH, ZG, PATCH, ZG, PATCH).transpose(1, 3, 5, 0, 2, 4).reshape(KP, NI, ZT)

    def patches(g):
        return g.reshape(VER, CH, GRID, PATCH, GRID, PATCH).transpose(1, 3, 5, 0, 2, 4).reshape(KP, VER, TOK)

    def heads(scalar, point):
        o = np.zeros(scalar.shape[:-1] + (HEADS, 32), scalar.dtype)
        o[..., 0:DH] = scalar.reshape(scalar.shape[:-1] + (HEADS, DH))
        o[..., DH:DH + PP] = point.reshape(point.shape[:-1] + (HEADS, PP))
        return o.reshape(scalar.shape[:-1] + (2, KP))

    def column(v):
        return v.reshape(-1, 1)

    wo = f["L0_attn_wo"]
    edge = np.full(ZG, 2.0)
    edge[[0, -1]] = 1.0
    row = np.arange(KP) % 32
    cst = np.stack([0.25 * (row < DH), 2.0 * ((row >= DH) & (row < DH + PP)), row == 28, row == 29, row == 30], 1)
    selm = np.zeros((KP, KP))
    for p in range(KP):
        if DH <= row[p] < DH + PP:
            selm[p, p - row[p] + 28] = 1.0
    c = lambda a: np.ascontiguousarray(a, np.float32)
    return {
        "xz": np.concatenate([plain, shifted], 2).reshape(KP, NI * XZ),
        "w": np.ascontiguousarray(f["L0_tok_W"].reshape(E, VER, KP).transpose(2, 1, 0)),
        "gamma": patches(f["L0_tok_gamma"]), "beta": patches(f["L0_tok_beta"]),
        "zwt": c(np.broadcast_to((1.0 + np.outer(edge, edge)).reshape(1, ZT), (KP, ZT))),
        "npix": c(np.full((KP, KP), 1.0 / NPIX)), "ones": c(np.full((KP, KP), 1.0 / E)),
        "ident": c(np.eye(KP)), "selm": c(selm), "cst": c(cst), "wr": f["L0_ffn_Wr"],
        "tok_b": column(f["L0_tok_b"]), "ln_g": column(f["L0_attn_ln_g"]), "ln_b": column(f["L0_attn_ln_b"]),
        "bv": column(f["L0_attn_bv"]), "bo": column(f["L0_attn_bo"]),
        "bq": heads(f["L0_attn_bq"], f["L0_attn_bqp"]).T, "bk": heads(f["L0_attn_bk"], f["L0_attn_bkp"]).T,
        "ps": np.repeat(f["L0_attn_pscale"].reshape(2, 4).T, 32, 0),
        "wq": heads(f["L0_attn_wq"], f["L0_attn_wqp"]), "wk": heads(f["L0_attn_wk"], f["L0_attn_wkp"]),
        "wv": f["L0_attn_wv"], "wo": wo,
        "row1": c(np.stack([np.arange(KP) == 29, np.arange(KP) == 30])[None]),
        "ones1": c(np.ones((R, R))), "tri": c(np.triu(np.ones((R, R)), 1)),
        "blk": c(np.kron(np.eye(NEXP), np.ones((16, 16)))),
        "reset": c(np.broadcast_to((np.arange(NEXP * R) % R != 0)[None], (R, NEXP * R))),
        "slots": c(np.broadcast_to(np.arange(CAP)[None], (R, CAP))),
        "slot1": c(1 + np.arange(128)[:, None] + 128 * np.arange(CAP // 128)[None]),
        "iota": c(np.broadcast_to(np.arange(R)[None], (128, R))),
        "rowbase": c(R * np.arange(R)[:, None]),
        "bits": np.broadcast_to((1 << np.arange(29, -1, -1, dtype=np.uint32))[None], (128, 30)),
        "b1": f["L0_ffn_b1"].reshape(NEXP * 4, 128).T,
        "b2": np.broadcast_to(f["L0_ffn_b2"].reshape(1, NEXP * E), (128, NEXP * E)),
        "W1": f["L0_ffn_W1"], "W2": f["L0_ffn_W2"],
    }


def kernel(**inputs):
    import concourse.bacc as _bacc
    from concourse.bass_utils import run_bass_kernel_spmd as _run

    nc = _bacc.Bacc("TRN2", target_bir_lowering=False, num_devices=1)
    arrays, A = {}, {"kind": KIND}
    for name, a in layouts(inputs).items():
        a = np.ascontiguousarray(a)
        arrays[f"in_{name}"] = a
        A[name] = nc.dram_tensor(f"in_{name}", a.shape, mybir.dt.from_np(a.dtype), kind="ExternalInput").ap()
    out = nc.dram_tensor("out_tokens", [NTOK, E], F32, kind="ExternalOutput").ap()
    program(nc, A, out)
    r = _run(nc, [arrays], core_ids=[0])
    return r.results[0]["out_tokens"].reshape(NI, TOK, E)
```

```python
from contextlib import ExitStack

import numpy as np

import concourse.bass as bass
from concourse import mybir

ALU = mybir.AluOpType
ACT = mybir.ActivationFunctionType
F32 = mybir.dt.float32
F32R = mybir.dt.float32r
U32 = mybir.dt.uint32
U16 = mybir.dt.uint16
AX = mybir.AxisListType

NI, CH, SIDE, SHIFT, PATCH = 64, 2, 104, 4, 8
GRID = SIDE // PATCH
TOK = GRID * GRID
ZG = GRID + 1
ZT = ZG * ZG
XZ = TOK + ZT
VER = 5
KP = CH * PATCH * PATCH
E = 128
HEADS, DH, PP = 8, 16, 12
HT = (TOK + 1) // 2
TP = 2 * HT
NTOK = NI * TOK
UN = 4
NEXP, FF, CAP = 8, 512, 1024
R = 104
TOK_EPS, LN_EPS = 1e-7, 1e-5
NPIX = 10 * SIDE * SIDE
CHUNK = NTOK // 16
UNIT = 512
NBLK = UNIT // 128
KIND = "Internal"


SETUP = 8
FILLS = 10
MAX_ROW = 96
ONE_ROW = MAX_ROW + 2 * HEADS


PACK = {"columns": 12, "wq": 2 * KP, "wk": 2 * KP, "wv": KP, "wo": KP, "wr": NEXP, "ident": KP, "selm": KP, "cst": 5,
        "qcst": 64, "ps8": HEADS, "zwt": ZT}
TOKPACK = {"w": VER * E, "gamma": VER * TOK, "beta": VER * TOK}


def i_par(r, ahead):
    return (r + ahead) % 2


def i_ring(r, ahead):
    return (r + ahead) % UN


def tower_tokens(nc, ctx, A, h2_dram, lg_dram):

    def sb(name, shape, dt=F32):
        return ctx.enter_context(nc.sbuf_tensor(name, shape, dt))

    def sem(name):
        return ctx.enter_context(nc.semaphore(name))

    xz = sb("xz", [KP, NI * XZ])
    pack = sb("pack", [KP, sum(PACK.values())])
    tokpack = sb("tokpack", [KP, sum(TOKPACK.values())])

    def part(tile, columns, name):
        at = 0
        for n, width in columns.items():
            if n == name:
                return tile[:, at:at + width]
            at += width

    wt, gam, bet = (part(tokpack, TOKPACK, n).rearrange("p (v c) -> p v c", v=VER) for n in ("w", "gamma", "beta"))
    wq, wk = (part(pack, PACK, n).rearrange("p (g c) -> p g c", g=2) for n in ("wq", "wk"))
    wv, wo, wr, ident, selm, cst, qcst, ps8, zwt, col = (
        part(pack, PACK, n) for n in ("wv", "wo", "wr", "ident", "selm", "cst", "qcst", "ps8", "zwt", "columns"))
    npix = sb("npix", [KP, KP])
    ones = sb("ones", [KP, KP])
    tokb, lng, lnb, bv, bo = (col[:, i:i + 1] for i in range(5))
    bq, bk, psc = col[:, 5:7], col[:, 7:9], col[:, 9:11]

    gmean = sb("gmean", [KP, TOK])
    gbias = sb("gbias", [KP, TOK])
    qscale = sb("qscale", [KP, 2])
    qbias = sb("qbias", [KP, 2])
    kbias = sb("kbias", [KP, 2])
    qraw = sb("qraw", [KP, 6])
    selk = sb("selk", [KP, 2, KP])
    row1 = sb("row1", [1, 2, KP])
    obias = sb("obias", [KP, 1])
    mhalf = sb("mhalf", [KP, 4])

    zs = sb("zs", [KP, UN, ZT])
    part = sb("part", [KP, 4, 2])
    stat = sb("stat", [KP, 4, 2])
    ivar = sb("ivar", [KP, 4])
    istd = sb("istd", [KP, 4])
    inmr = sb("inmr", [KP, 4])
    tick = sb("tick", [1, 1])
    wrc = sb("wrc", [KP, NEXP])
    vtot = sb("vtot", [KP, 1])
    gx = sb("gx", [KP, 2, VER, TP])
    tb = sb("tb", [KP, TOK])
    yT = sb("yT", [KP, UN, TP])
    st6 = sb("st6", [HT, 4, 6])
    mv = sb("mv", [HT, 4, 2])
    ve = sb("ve", [HT, 4])
    rs = sb("rs", [HT, 4])
    x = sb("x", [HT, 2, E])
    xT = sb("xT", [KP, 2, TP])
    spread = sb("spread", [KP, 4, 4, KP], F32R)
    qmul = sb("qmul", [KP, 2 * KP])
    qhi = sb("qhi", [KP, 2, TP], F32R)
    qlo = sb("qlo", [KP, 2, TP], F32R)
    khi = sb("khi", [KP, 2, TP], F32R)
    klo = sb("klo", [KP, 2, TP], F32R)
    qop = sb("qop", [KP, 2, 4, 2 * TP], F32R)
    kop = sb("kop", [KP, 2, 4, 2 * TP], F32R)
    ksq = sb("ksq", [KP, 2, TP])
    kbrow = sb("kbrow", [1, 2, KP])
    va = sb("va", [HT, 2, 2, HEADS, DH + 1])
    mx = sb("smax", [HT, 2, HEADS])
    mhi = sb("mhi", [HT, 2, HEADS], F32R)
    mp = sb("mp", [HT, 2, KP])
    pT = sb("pT", [HT, 2, 4, 2, TP])
    oinv = sb("oinv", [HT, 2, HEADS])
    o = sb("o", [HT, 2, E])
    oT = sb("oT", [KP, TP])
    sT = sb("sT", [KP, TP])
    h2 = sb("h2", [HT, UN, 2, E])
    lraw = sb("lraw", [HT, 2 * NEXP])
    lg = sb("lg", [HT, UN, 2, NEXP])

    ring = [ctx.enter_context(nc.psum_tensor(f"ring{n}", [KP, 2, 512], F32)) for n in range(2)]
    bank = [ctx.enter_context(nc.psum_tensor(f"bank{i}", [KP, 512], F32)) for i in range(4, 8)]
    b4, b5, b6, b7 = bank

    s_c = sem("s_consts")
    s_ct = sem("s_token_consts")
    s_ld = [sem(f"s_loaded{r}") for r in range(UN)]
    s_set = sem("s_setup")
    s_sps = sem("s_setup_psum")
    s_fill = sem("s_filled")
    s_zs = sem("s_zs")
    s_pt = sem("s_part")
    s_stp = sem("s_stat_psum")
    s_st = sem("s_stat")
    s_iv = sem("s_ivar")
    s_is = sem("s_istd")
    s_nm = sem("s_inmr")
    s_gx = sem("s_gx")
    s_cv = sem("s_conv")
    s_tb = sem("s_tb")
    s_y = sem("s_y")
    s_ht = sem("s_h_turned")
    s_nb = sem("s_norm_stats")
    s_nr = sem("s_norm_rstd")
    s_x = sem("s_x")
    s_xt = sem("s_x_turned")
    s_xT = sem("s_xT")
    s_q = sem("s_q_psum")
    s_qh = sem("s_q_high")
    s_ql = sem("s_q_low")
    s_rq = sem("s_q_spread")
    s_qc = sem("s_q_operand")
    s_rk = sem("s_k_spread")
    s_kc = sem("s_k_operand")
    s_k = sem("s_k_psum")
    s_sq = sem("s_ksq")
    s_kk = sem("s_k_whole")
    s_kh = sem("s_k_high")
    s_kl = sem("s_k_low")
    s_v = sem("s_v_psum")
    s_ve = sem("s_v")
    s_S = sem("s_scores")
    s_m = sem("s_max")
    s_mh = sem("s_max_high")
    s_ms = sem("s_max_split")
    s_mt = sem("s_max_turned")
    s_q2 = sem("s_q_less_max")
    s_ST = sem("s_scoresT")
    s_e = sem("s_exp")
    s_pv = sem("s_pv")
    s_oi = sem("s_oinv")
    s_on = sem("s_o")
    s_ot = sem("s_o_turned")
    s_oT = sem("s_oT")
    s_wo = sem("s_wo")
    s_s = sem("s_sum")
    s_sb = sem("s_s_turned")
    s_lr = sem("s_logits_raw")
    s_h2 = sem("s_h2")
    s_out = [sem(f"s_stored{r}") for r in range(UN)]

    NG = NI // UN

    def w(eng, s, v):
        if isinstance(v, int) and v <= 0:
            return
        eng.wait_ge(s, v)

    def pipeline(eng, body):
        body(-2, UN - 1)
        for r in range(UN):
            body(-1, r)
        with eng.Fori(0, NG - 3) as q:
            for r in range(UN):
                body(q, r)
        for q in range(NG - 3, NG):
            for r in range(UN):
                body(q, r)

    def stages(q, r):
        if not isinstance(q, int):
            return [True] * 6 + [True, r == UN - 1]
        i = q * UN + r
        return [0 <= i + n < NI for n in range(6)] + [i + 9 < NI, r == UN - 1 and q + 2 < NG]

    block = ctx.enter_context(nc.Block())

    @block.sync
    def _(sp):
        sp.dma_start(pack[:], A["pack"]).then_inc(s_c, 16)
        sp.dma_start(row1[:], A["row1"]).then_inc(s_c, 16)

        def load(q, r):
            w(sp, s_ld[r], q * 16)
            at = (q * UN + r) * XZ
            sp.dma_start(xz[:, bass.ds(at, XZ)], A["xz"][:, bass.ds(at, XZ)]).then_inc(s_ld[r], 16)

        def store(q, r):
            first = (q * UN + r) * TOK
            sp.wait_ge(s_h2, q * UN + r + 1)
            for t, (a, n) in enumerate(((first, HT), (first + HT, HT - 1))):
                sp.dma_start(h2_dram[bass.ds(a, n), :], h2[0:n, r, t, :]).then_inc(s_out[r], 16)
                sp.dma_start(lg_dram[bass.ds(a, n), :], lg[0:n, r, t, :]).then_inc(s_out[r], 16)

        load(0, 0)
        sp.dma_start(tokpack[:], A["tokpack"]).then_inc(s_ct, 16)
        for r in range(1, UN):
            load(0, r)
        for q in (1, 2):
            for r in range(UN):
                load(q, r)
        with sp.Fori(0, NG - 3) as q:
            for r in range(UN):
                load(q + 3, r)
            for r in range(UN):
                store(q, r)
        for q in range(NG - 3, NG):
            for r in range(UN):
                store(q, r)
        for r in range(UN):
            sp.wait_ge(s_out[r], NG * 64)

    @block.gpsimd
    def _(pool):
        fills = ((gx[:, :, :, TOK:TP], 0.0), (yT[:, :, TOK:TP], 0.0), (mp[:, :, 0:MAX_ROW], 0.0), (mp[:, :, MAX_ROW:KP], 1.0), (va[:, :, :, :, DH:DH + 1], 1.0),
                 (mhalf[:], -0.5), (mv[:], 1.0), (ones[:], 1.0 / E), (npix[:], 1.0 / NPIX),
                 (spread[:].bitcast(F32), 0.0))
        assert len(fills) == FILLS
        for t, v in fills:
            nc.gpsimd.memset(t, v).then_inc(s_fill, 1)
        pool.wait_ge(s_fill, FILLS)
        pool.wait_ge(s_ct, 16)

        def gamma(i, q, r):
            pool.wait_ge(s_ld[r], (q + 1) * 16)
            w(pool, s_cv, i - 1)
            o = gx[:, r % 2, :, 0:TOK].rearrange("p v (a b) -> p v a b", b=GRID)
            px = xz[:, bass.ds(i * XZ, TOK)].rearrange("p (a b) -> p a b", b=GRID)
            pz = xz[:, bass.ds(i * XZ + TOK, ZT)].rearrange("p (a b) -> p a b", b=ZG)
            gm = gam[:].rearrange("p v (a b) -> p v a b", b=GRID)
            nc.gpsimd.tensor_tensor(o[:, 0], px, gm[:, 0], ALU.mult)
            for v, (dy, dx) in enumerate(((1, 0), (1, 1), (0, 0), (0, 1))):
                ins = nc.gpsimd.tensor_tensor(o[:, v + 1], pz[:, dy:dy + GRID, dx:dx + GRID], gm[:, v + 1], ALU.mult)
            ins.then_inc(s_gx, 1)

        def body(q, r):
            last, att, score, proj, tok, more, sums, devs = stages(q, r)
            i = q * UN + r
            if more:
                gamma(i + 5, q + 1 + (r + 1) // UN, (r + 1) % UN)
            if tok or last:
                pool.wait_ge(s_nb, 3 * (i + 4) + 3)
                nc.gpsimd.tensor_tensor(rs[:], ve[:], mhalf[0:HT, :], ALU.pow).then_inc(s_nr, 1)
            if devs:
                pool.wait_ge(s_iv, 2 * (q + 3))
                nc.gpsimd.tensor_tensor(istd[:], ivar[:], mhalf[:], ALU.pow).then_inc(s_is, 1)

        pipeline(pool, body)

    @block.tensor
    def _(pe):
        mm = nc.tensor.matmul
        pe.wait_ge(s_c, 32)
        pe.wait_ge(s_fill, FILLS)
        for c, t in enumerate((wq[:, 0, :], wq[:, 1, :], wk[:, 0, :], wk[:, 1, :], wv[:])):
            mm(b4[:, c:c + 1], t, lnb, start=True, stop=True)
        mm(b7[:, 0:NEXP], ones[:], wr[:], start=True, stop=True).then_inc(s_sps, 1)
        pe.wait_ge(s_set, 3)
        mm(b4[:, 8:9], wo[:], vtot[:], start=True, stop=True).then_inc(s_sps, 1)
        pe.wait_ge(s_set, 6)
        for G in range(2):
            ins = nc.tensor.transpose(b5[0:1, G * KP:(G + 1) * KP], kbias[:, G:G + 1], ident[:])
        ins.then_inc(s_sps, 1)
        pe.wait_ge(s_set, 7)
        for G in range(2):
            ins = mm(b6[:, G * KP:(G + 1) * KP], row1[:, G, :], kbrow[:, G, :], start=True, stop=True)
        ins.then_inc(s_sps, 1)
        pe.wait_ge(s_ct, 16)
        for to, t in ((b5, gam), (b7, bet)):
            for v in range(VER):
                ins = mm(to[:, 0:TOK], wt[:, v, :], t[:, v, :], start=(v == 0), stop=(v == VER - 1))
        ins.then_inc(s_sps, 1)
        pe.wait_ge(s_set, SETUP)

        def half(t):
            return slice(t * HT, t * HT + HT)

        def body(q, r):
            last, att, score, proj, tok, more, sums, devs = stages(q, r)
            i = q * UN + r
            a, b, p, c = i + 1, i + 2, i + 3, i + 4

            def scoresT(n):
                G, t = n // 2, n % 2
                if n == 0:
                    pe.wait_ge(s_q2, a + 1)
                if n < 2:
                    pe.wait_ge(s_kc, 2 * p - 1 + n if not isinstance(p, int) else min(2 * p - 1 + n, 2 * NI))
                elif score:
                    pe.wait_ge(s_m, 4 * b + n - 1)
                else:
                    pe.wait_ge(s_e, 4 * a + n - 1)
                for g in range(4):
                    ins = mm(ring[n % 2][0:HT, g // 2, g % 2 * TP:g % 2 * TP + TP],
                             kop[:, i_par(r, 1), g, G * TP + t * HT:G * TP + t * HT + HT],
                             qop[:, i_par(r, 1), g, G * TP:G * TP + TP], start=True, stop=True)
                ins.then_inc(s_ST, 1)

            def scores(n):
                G, t = n // 2, n % 2
                if n == 0:
                    pe.wait_ge(s_kc, 2 * b + 2)
                if att:
                    pe.wait_ge(s_e, 4 * a + n + 1)
                elif n >= 2:
                    pe.wait_ge(s_m, 4 * b + n - 1)
                for g in range(4):
                    ins = mm(ring[n % 2][0:HT, g // 2, g % 2 * TP:g % 2 * TP + TP],
                             qop[:, i_par(r, 2), g, G * TP + t * HT:G * TP + t * HT + HT],
                             kop[:, i_par(r, 2), g, G * TP:G * TP + TP], start=True, stop=True)
                ins.then_inc(s_S, 1)

            def to_operand(n, done, first, high, low):
                for u in range(2):
                    for k, part in enumerate((high, low)):
                        ins = mm(ring[n % 2][:, u, 0:2 * TP], spread[:, first + k, 2 * n + u, :],
                                 part[:].rearrange("p g c -> p (g c)"), start=(k == 0), stop=(k == 1))
                ins.then_inc(done, 1)

            def convolution(par, versions):
                for v in versions:
                    ins = mm(b4[:, 0:TP], wt[:, v, :], gx[:, par, v, :], start=(v == 0), stop=(v == VER - 1))
                return ins

            def spread_q(n):
                if n == 0:
                    pe.wait_ge(s_ql, p + 1)
                if score:
                    pe.wait_ge(s_m, 4 * b + n + 3)
                to_operand(n, s_rq, 0, qhi, qlo)

            def spread_k(n):
                if n == 0:
                    pe.wait_ge(s_kl, p + 1)
                pe.wait_ge(s_qc, 2 * p + n + 1)
                to_operand(n, s_rk, 2, khi, klo)

            def values(G, t):
                for h in range(4 * G, 4 * G + 4):
                    for k in range(2):
                        n = HT - k
                        at = (t * HEADS + h) * (DH + 1)
                        ins = mm(b5[0:HT, at:at + DH + 1], pT[0:n, G, h % 4, k, half(t)], va[0:n, i_par(r, 1), k, h, :],
                                 start=(k == 0), stop=(k == 1))
                return ins

            if att:
                scoresT(0)
                scoresT(1)
            if tok:
                convolution(i_par(r, 4), (3,))
            if score:
                w(pe, *((s_on, i + 1) if last else (s_ql, p)))
                for t in range(2):
                    ins = mm(b5[0:HT, t * E:t * E + E], xT[:, i_par(r, 2), half(t)], wv[:], start=True, stop=True)
                ins.then_inc(s_v, 1)
            if last:
                pe.wait_ge(s_on, i + 1)
                w(pe, s_xT, min(c, NI) if isinstance(i, int) else c)
                for t in range(2):
                    ins = nc.tensor.transpose(b7[:, half(t)], o[:, t, :], ident[0:HT, 0:HT])
                ins.then_inc(s_ot, 1)
            if tok:
                convolution(i_par(r, 4), (4,)).then_inc(s_cv, 1)
            if score:
                scores(0)
            if last:
                pe.wait_ge(s_oT, i + 1)
                mm(b6[:, 0:TP], wo[:], oT[:], start=True, stop=True).then_inc(s_wo, 1)
            if proj:
                pe.wait_ge(s_xT, p + 1)
                w(pe, *((s_ve, b + 1) if score else (s_ql, p)))
                for G in range(2):
                    ins = mm(b5[:, G * TP:G * TP + TP], wq[:, G, :], xT[:, i_par(r, 3), :], start=True, stop=True)
                ins.then_inc(s_q, 1)
            if score:
                scores(1)
            if proj:
                w(pe, *((s_s, i + 1) if last else (s_kl, p)))
                for G in range(2):
                    ins = mm(b6[:, G * TP:G * TP + TP], wk[:, G, :], xT[:, i_par(r, 3), :], start=(G == 0), stop=True,
                             skip_group_check=True)
                ins.then_inc(s_k, 1)
            if tok:
                pe.wait_ge(s_y, c + 1)
                w(pe, *((s_oT, i + 1) if last else (s_xT, c)))
                for t in range(2):
                    ins = nc.tensor.transpose(b7[0:HT, t * E:t * E + E], yT[:, i_ring(r, 4), half(t)], ident[:])
                ins.then_inc(s_ht, 1)
            if devs:
                pe.wait_ge(s_pt, UN * (q + 3))
                w(pe, s_lr, i)
                mm(b4[:, 2 * NEXP:2 * NEXP + 8], npix[:], part[:].rearrange("p a b -> p (a b)"), start=True, stop=True).then_inc(s_stp, 1)
            if last:
                pe.wait_ge(s_s, i + 1)
                w(pe, s_y, c + 1 if tok else 0)
                w(pe, s_lr, i)
                for t in range(2):
                    nc.tensor.transpose(b7[0:HT, (2 + t) * E:(3 + t) * E], sT[:, half(t)], ident[:])
                for t in range(2):
                    ins = mm(b4[0:HT, t * NEXP:(t + 1) * NEXP], sT[:, half(t)], wrc[:],
                             start=True, stop=True)
                ins.then_inc(s_sb, 1)
            if att:
                scoresT(2)
            if proj:
                pe.wait_ge(s_sq, p + 1)
                for G in range(2):
                    ins = mm(b6[:, G * TP:G * TP + TP], selk[:, G, :], ksq[:, G, :], start=False, stop=True,
                             skip_group_check=True)
                ins.then_inc(s_kk, 1)
            if att:
                scoresT(3)
            if att:
                pe.wait_ge(s_e, 4 * a + 2)
                if proj:
                    pe.wait_ge(s_ql, p + 1)
                elif score:
                    pe.wait_ge(s_ve, b + 1)
                values(0, 0)
            if score:
                scores(2)
                scores(3)
            if att:
                values(0, 1).then_inc(s_pv, 1)
            if more:
                pe.wait_ge(s_gx, c + 2)
                w(pe, *((s_lr, i + 1) if last else (s_y, c + 1)))
                if devs:
                    pe.wait_ge(s_st, q + 3)
                convolution(i_par(r, 5), range(0, 3))
            if proj:
                spread_q(0)
                spread_q(1)
            if att:
                pe.wait_ge(s_e, 4 * a + 4)
                values(1, 0)
            if tok:
                pe.wait_ge(s_x, c + 1)
                w(pe, s_h2, i + 1 if last else 0)
                for t in range(2):
                    ins = nc.tensor.transpose(b7[:, half(t)], x[:, t, :], ident[0:HT, 0:HT])
                ins.then_inc(s_xt, 1)
            if score:
                pe.wait_ge(s_ms, b + 1)
                w(pe, s_kl, p + 1 if proj else 0)
                for t in range(2):
                    ins = nc.tensor.transpose(b6[:, half(t)], mp[:, t, :], ident[0:HT, 0:HT])
                ins.then_inc(s_mt, 1)
            if proj:
                spread_k(0)
                spread_k(1)
            if att:
                values(1, 1).then_inc(s_pv, 1)

        pipeline(pe, body)

    @block.scalar
    def _(act):
        act.wait_ge(s_set, SETUP)
        act.wait_ge(s_fill, FILLS)
        activation = nc.scalar.activation

        def body(q, r):
            last, att, score, proj, tok, more, sums, devs = stages(q, r)
            i = q * UN + r
            a, b, p, c = i + 1, i + 2, i + 3, i + 4

            def exponentials(n):
                G, t = n // 2, n % 2
                act.wait_ge(s_ST, 4 * a + n + 1)
                w(act, s_pv, 2 * a - 1 + G)
                activation(pT[:, G, :, t, :].rearrange("p (u g) c -> p u g c", u=2),
                           ring[n % 2][0:HT, :, 0:2 * TP].rearrange("p u (g c) -> p u g c", g=2), ACT.Exp).then_inc(s_e, 1)

            def operand(to, spread_done, copied, n):
                act.wait_ge(spread_done, 2 * p + n + 1)
                activation(to[:, i_par(r, 3), 2 * n:2 * n + 2, :], ring[n % 2][:, :, 0:2 * TP], ACT.Copy).then_inc(copied, 1)

            if att:
                exponentials(0)
            if last:
                act.wait_ge(s_ot, i + 1)
                activation(oT[:], b7[:, 0:TP], ACT.Copy).then_inc(s_oT, 1)
            if att:
                exponentials(1)
            if proj:
                act.wait_ge(s_q, p + 1)
                w(act, s_rq, 2 * p)
                for G in range(2):
                    ins = activation(qhi[:, G, :], b5[:, G * TP:G * TP + TP], ACT.Identity, bias=qbias[:, G:G + 1])
                ins.then_inc(s_qh, 1)
                act.wait_ge(s_k, p + 1)
                w(act, s_kk, p)
                for G in range(2):
                    ins = activation(ksq[:, G, :], b6[:, G * TP:G * TP + TP], ACT.Square, bias=kbias[:, G:G + 1])
                ins.then_inc(s_sq, 1)
            if last:
                act.wait_ge(s_sb, i + 1)
                w(act, s_h2, i)
                activation(lraw[:], b4[0:HT, 0:2 * NEXP], ACT.Copy).then_inc(s_lr, 1)
            if devs:
                act.wait_ge(s_stp, q + 3)
                activation(stat[:].rearrange("p a b -> p (a b)"), b4[:, 2 * NEXP:2 * NEXP + 8], ACT.Copy).then_inc(s_st, 1)
            if att:
                exponentials(2)
                exponentials(3)
            if proj:
                act.wait_ge(s_kk, p + 1)
                w(act, s_rk, 2 * p)
                activation(khi[:], b6[:, 0:2 * TP].rearrange("p (g c) -> p g c", g=2), ACT.Copy).then_inc(s_kh, 1)
                operand(qop, s_rq, s_qc, 0)
                operand(qop, s_rq, s_qc, 1)
            if tok:
                act.wait_ge(s_xt, c + 1)
                activation(xT[:, i_par(r, 4), :], b7[:, 0:TP], ACT.Copy).then_inc(s_xT, 1)
            if proj:
                operand(kop, s_rk, s_kc, 0)
                operand(kop, s_rk, s_kc, 1)

        pipeline(act, body)

    @block.vector
    def _(dve):
        V = nc.vector
        dve.wait_ge(s_c, 32)
        dve.wait_ge(s_fill, FILLS)
        V.tensor_scalar(qscale[:], psc, cst[:, 1:2], cst[:, 0:1], ALU.mult, ALU.add)

        def by_head(t):
            return t.rearrange("p (h c) -> p h c", c=32)

        def for_all(c):
            return qcst[:, c * 32:c * 32 + 32].unsqueeze(1).to_broadcast([KP, HEADS, 32])

        V.tensor_tensor(by_head(qmul[:]), ps8.unsqueeze(2).to_broadcast([KP, HEADS, 32]), for_all(1), ALU.mult)
        for G in range(2):
            V.tensor_scalar(selk[:, G, :], selm[:], psc[:, G:G + 1], -1.0, ALU.mult, ALU.mult)
        dve.wait_ge(s_sps, 1)
        V.tensor_tensor(qraw[:, 0:2], b4[:, 0:2], bq, ALU.add).then_inc(s_set, 1)
        V.tensor_tensor(qraw[:, 2:4], b4[:, 2:4], bk, ALU.add).then_inc(s_set, 1)
        V.tensor_tensor(vtot[:], b4[:, 4:5], bv, ALU.add).then_inc(s_set, 1)
        dve.wait_ge(s_set, 3)
        V.tensor_tensor(qraw[:, 4:6], qraw[:, 0:2], qscale[:], ALU.mult).then_inc(s_set, 1)
        V.tensor_tensor(kbias[:], qraw[:, 2:4], cst[:, 3:5], ALU.add)
        V.tensor_tensor(wrc[:], wr[:], b7[:, 0:NEXP], ALU.subtract)
        for t in (wk[:, 0, :], wk[:, 1, :], wv[:]):
            V.tensor_scalar(t, t, lng, None, ALU.mult)
        dve.wait_ge(s_set, 4)
        V.tensor_tensor(by_head(qmul[:]), by_head(qmul[:]), for_all(0), ALU.add).then_inc(s_set, 1)
        dve.wait_ge(s_set, 5)
        V.scalar_tensor_tensor(wq[:].rearrange("p g c -> p (g c)"), wq[:].rearrange("p g c -> p (g c)"), lng, qmul[:],
                               ALU.mult, ALU.mult)
        V.tensor_scalar(qbias[:], qraw[:, 4:6], cst[:, 2:3], None, ALU.add)
        dve.wait_ge(s_sps, 2)
        V.tensor_tensor(obias[:], b4[:, 8:9], bo, ALU.add).then_inc(s_set, 1)
        dve.wait_ge(s_sps, 3)
        V.tensor_copy(kbrow[:].rearrange("p g c -> p (g c)"), b5[0:1, 0:2 * KP]).then_inc(s_set, 1)
        dve.wait_ge(s_sps, 4)
        V.tensor_tensor(selk[:].rearrange("p g c -> p (g c)"), selk[:].rearrange("p g c -> p (g c)"), b6[:, 0:2 * KP],
                        ALU.add)
        for which, blocks in ((0, (0, 1)), (1, (2,)), (2, (0, 2)), (3, (1,))):
            for n in blocks:
                V.tensor_copy(spread[:, which, :, 32 * n:32 * n + DH + PP],
                              ident.rearrange("p (g c) -> p g c", c=32)[:, :, 0:DH + PP])
        flat = spread[:].rearrange("p a g c -> p (a g c)")
        for which, at in ((0, ONE_ROW), (0, ONE_ROW + 1), (2, ONE_ROW), (3, ONE_ROW + 1)):
            V.tensor_copy(spread[:, which, :, at:at + 1], ident.rearrange("p (g c) -> p g c", c=32)[:, :, 28:29])
        for G in range(2):
            for low in range(2):
                at = 2 * 4 * KP + MAX_ROW + HEADS * low + 4 * G
                ins = V.tensor_copy(flat[:, at:at + 3 * (KP + 1) + 1:KP + 1], ident[:, 29 + G:29 + G + 97:32])
        dve.wait_ge(s_sps, 5)
        V.tensor_copy(gmean[:], b5[:, 0:TOK])
        V.tensor_scalar(gbias[:], b7[:, 0:TOK], tokb, None, ALU.add).then_inc(s_set, 1)
        dve.wait_ge(s_set, SETUP)

        def norm_stats(tok, last, step):
            which = [n for n in range(4) if (tok if n < 2 else last)]
            for n in which:
                ins = V.bn_stats(st6[:, n, :], b7[0:HT, n * E:(n + 1) * E])
            ins.then_inc(s_nb, 1)
            dve.wait_ge(s_nb, 3 * step + 1)
            V.memset(tick[:], 0.0)
            for n in which:
                ins = V.bn_aggr(mv[:, n, :], st6[:, n, :])
            ins.then_inc(s_nb, 1)
            dve.wait_ge(s_nb, 3 * step + 2)
            V.tensor_scalar(ve[:], mv[:, :, 1], LN_EPS, None, ALU.add).then_inc(s_nb, 1)

        def body(q, r):
            last, att, score, proj, tok, more, sums, devs = stages(q, r)
            i = q * UN + r
            a, b, p, c = i + 1, i + 2, i + 3, i + 4
            first = isinstance(q, int) and q == -2

            def pixel_sums(j, n):
                z = xz[:, bass.ds(j * XZ + TOK, ZT)]
                dve.wait_ge(s_ld[n], (q + (n == 0) + 3) * 16 if not first else 16 * (1 + j // UN))
                V.scalar_tensor_tensor(zs[:, n, :], z, 1.0, zwt[:], ALU.mult, ALU.mult,
                                       accum_out=part[:, n, 0:1]).then_inc(s_zs, 1)
                dve.wait_ge(s_zs, j + 1)
                V.scalar_tensor_tensor(zs[:, n, :], zs[:, n, :], 1.0, z, ALU.mult, ALU.mult,
                                       accum_out=part[:, n, 1:2]).then_inc(s_pt, 1)

            def maxima(n):
                G, t = n // 2, n % 2
                dve.wait_ge(s_S, 4 * b + n + 1)
                V.tensor_reduce(mx[:, t, 4 * G:4 * G + 4].rearrange("p (u g) -> p u g", u=2),
                                ring[n % 2][0:HT, :, 0:2 * TP].rearrange("p u (g c) -> p u g c", g=2)[:, :, :, 0:TOK],
                                AX.X, ALU.max, negate=True).then_inc(s_m, 1)

            if first:
                for n in range(UN):
                    pixel_sums(n, n)
            if score:
                dve.wait_ge(s_v, b + 1)
                w(dve, s_pv, 2 * (b - 1))
                V.tensor_copy(va[:, i_par(r, 2), :, :, 0:DH],
                              b5[0:HT, 0:2 * E].rearrange("p (t h d) -> p t h d", t=2, d=DH)).then_inc(s_ve, 1)
            if tok:
                dve.wait_ge(s_nm, q + 2)
                V.scalar_tensor_tensor(tb[:], gmean[:], inmr[:, r:r + 1], gbias[:], ALU.mult, ALU.add).then_inc(s_tb, 1)
            if last:
                dve.wait_ge(s_wo, i + 1)
                w(dve, s_sb, i)
                V.scalar_tensor_tensor(sT[:], b6[:, 0:TP], obias[:, 0:1], yT[:, r, :], ALU.add,
                                       ALU.add).then_inc(s_s, 1)
            if tok:
                dve.wait_ge(s_cv, c + 1)
                dve.wait_ge(s_tb, c + 1)
                w(dve, s_s, i + 1 if last else 0)
                V.scalar_tensor_tensor(yT[:, i_ring(r, 4), 0:TOK], b4[:, 0:TOK], istd[:, r:r + 1], tb[:], ALU.mult,
                                       ALU.add).then_inc(s_y, 1)
            if score:
                maxima(0)
                maxima(1)
            if proj:
                dve.wait_ge(s_qh, p + 1)
                for G in range(2):
                    ins = V.scalar_tensor_tensor(qlo[:, G, :], b5[:, G * TP:G * TP + TP], qbias[:, G:G + 1], qhi[:, G, :],
                                                 ALU.add, ALU.subtract)
                ins.then_inc(s_ql, 1)
            if tok:
                dve.wait_ge(s_ht, c + 1)
            if last:
                dve.wait_ge(s_sb, i + 1)
            if tok or last:
                norm_stats(tok, last, i + 4)
            if devs:
                dve.wait_ge(s_st, q + 3)
                V.tensor_tensor(ivar[:], stat[:, :, 0], stat[:, :, 0], ALU.mult).then_inc(s_iv, 1)
                dve.wait_ge(s_iv, 2 * (q + 2) + 1)
                V.scalar_tensor_tensor(ivar[:], stat[:, :, 1], TOK_EPS, ivar[:], ALU.add, ALU.subtract).then_inc(s_iv, 1)
            if score:
                maxima(2)
                maxima(3)
            if proj:
                dve.wait_ge(s_kh, p + 1)
                V.tensor_tensor(klo[:], b6[:, 0:2 * TP].rearrange("p (g c) -> p g c", g=2), khi[:],
                                ALU.subtract).then_inc(s_kl, 1)
            if tok:
                dve.wait_ge(s_nr, c + 1)
                w(dve, s_xt, c)
                for t in range(2):
                    ins = V.tensor_scalar(x[:, t, :], b7[0:HT, t * E:t * E + E], mv[:, t, 0:1], rs[:, t:t + 1],
                                          ALU.subtract, ALU.mult)
                ins.then_inc(s_x, 1)
            if last:
                dve.wait_ge(s_nr, i + 5)
                dve.wait_ge(s_lr, i + 1)
                w(dve, s_out[r], q * 64)
                V.tensor_tensor(lg[:, r], lraw[:].rearrange("p (t e) -> p t e", t=2),
                                rs[:, 2:4].unsqueeze(2).to_broadcast([HT, 2, NEXP]), ALU.mult)
                for t in range(2):
                    ins = V.tensor_scalar(h2[:, r, t, :], b7[0:HT, (2 + t) * E:(3 + t) * E], mv[:, 2 + t, 0:1], rs[:, 2 + t:3 + t],
                                          ALU.subtract, ALU.mult)
                ins.then_inc(s_h2, 1)
            if score:
                dve.wait_ge(s_m, 4 * b + 4)
                V.tensor_copy(mhi[:], mx[:]).then_inc(s_mh, 1)
                dve.wait_ge(s_mh, b + 1)
                w(dve, s_mt, b)
                V.tensor_copy(mp[:, :, MAX_ROW:MAX_ROW + HEADS], mhi[:])
                V.tensor_tensor(mp[:, :, MAX_ROW + HEADS:ONE_ROW], mx[:], mhi[:], ALU.subtract).then_inc(s_ms, 1)
            if score:
                dve.wait_ge(s_mt, b + 1)
                V.tensor_copy(qop[MAX_ROW:KP, i_par(r, 2)].rearrange("p g (k c) -> p (g k) c", k=2),
                              b6[MAX_ROW:KP, 0:TP].unsqueeze(1).to_broadcast([KP - MAX_ROW, HEADS, TP])).then_inc(s_q2, 1)
            if att:
                dve.wait_ge(s_pv, 2 * a + 2)
                ov = b5[0:HT, 0:2 * HEADS * (DH + 1)].rearrange("p (t h d) -> p t h d", t=2, d=DH + 1)
                V.reciprocal(oinv[:], ov[:, :, :, DH]).then_inc(s_oi, 1)
                dve.wait_ge(s_oi, a + 1)
                w(dve, s_ot, a)
                V.tensor_tensor(o[:].rearrange("p t (h d) -> p t h d", d=DH), ov[:, :, :, 0:DH],
                                oinv[:].unsqueeze(3).to_broadcast([HT, 2, HEADS, DH]), ALU.mult).then_inc(s_on, 1)
            if devs:
                dve.wait_ge(s_is, q + 3)
                V.scalar_tensor_tensor(inmr[:], stat[:, :, 0], -1.0, istd[:], ALU.mult, ALU.mult).then_inc(s_nm, 1)
            if sums:
                pixel_sums(i + 9, (r + 1) % UN)

        pipeline(dve, body)


def experts(nc, ctx, A, h2_dram, lg_dram, e_dram, acc_dram, out):

    def sb(name, shape, dt=F32):
        return ctx.enter_context(nc.sbuf_tensor(name, shape, dt))

    def sem(name):
        return ctx.enter_context(nc.semaphore(name))

    W3 = NEXP * R
    TAB = 2 * R + 1
    NB = CAP // 128
    HI_ROUNDS, LO_ROUNDS = 7, 8
    ROUNDS = HI_ROUNDS + LO_ROUNDS
    FR = NTOK // 128
    REST = NTOK - 128 * FR
    CT = 12
    NCH = FR // CT
    ON_ACT, ON_POOL = 10, 1

    ident = sb("ident2", [128, 128])
    ones = sb("ones2", [128, R])
    owner = sb("owner", [128, NEXP])
    halves = sb("halves", [128, 2, NEXP])
    tri = sb("tri", [R, R])
    blk = sb("blk", [128, 128])
    reset = sb("reset", [R, W3])
    slots = sb("slots", [R, CAP])
    slot1 = sb("slot1", [128, NB])
    iota = sb("iota", [128, R])
    rowbase = sb("rowbase", [R, 1])
    steps = sb("steps", [128, (ROUNDS + 1) * 6])
    b1 = sb("b1", [128, NEXP * 4])
    b2 = sb("b2", [128, NEXP * E])

    lrow = sb("lrow", [R, W3])
    pr = sb("pr", [R, NEXP, R])
    mx = sb("mx", [R, NEXP])
    gm = sb("gm", [NEXP, 1])
    dg = sb("dg", [NEXP, NEXP])
    mb = sb("mb", [R, NEXP])
    tot = sb("tot", [R, NEXP])
    rtot = sb("rtot", [R, NEXP])
    pe_ = sb("pe_", [128, CHUNK])
    key = sb("key", [128, 2, CHUNK], U16)
    low = sb("low", [128, CHUNK], U16)
    ge = sb("ge", [128, 3, CHUNK], U16)
    cnt = sb("cnt", [128, 3])
    cand = sb("cand", [128, 3])
    inc = sb("inc", [128, 1])
    base = sb("base", [128, 1])
    need = sb("need", [128, 1])
    junk = sb("junk", [128, 3])
    tb = sb("thr_rows", [R, NEXP])
    gt = sb("gt", [R, NEXP, R])
    eq = sb("eq", [R, NEXP, R])
    run = sb("run", [R, NEXP, R])
    ng = sb("ng", [R, NEXP])
    te = sb("te", [R, NEXP])
    room = sb("room", [R, NEXP])
    start = sb("start", [R, NEXP])
    end = sb("end", [R, NEXP])
    tab = sb("tab", [R, NEXP * TAB])
    oh0 = sb("oh0", [R, CAP])
    oh = sb("oh", [R, CAP])
    tabs = sb("tabs", [128, NB, TAB])
    jk = sb("jk", [128, NB, R])
    loc = sb("loc", [128, NB])
    wgt = sb("wgt", [128, 2, NB])
    idx = sb("idx", [128, 2, NB], U32)
    swgt = sb("swgt", [128, NBLK])
    sidx = sb("sidx", [128, 2, NBLK], U32)
    xg = sb("xg", [128, 2, NB, E])
    xgT = sb("xgT", [128, 2, UNIT])
    w1 = sb("w1", [128, 2, FF])
    w2 = sb("w2", [128, 2, 4, E])
    hT = sb("hT", [128, 2, 4, UNIT])
    yb = sb("yb", [128, NBLK, E])
    yw = sb("yw", [128, 2, NBLK, E])
    fin = sb("fin", [128, 4, CT + 1, E])
    fout = sb("fout", [128, 3, CT + 1, E])
    f6 = sb("f6", [128, CT + 1, 6])
    fmv = sb("fmv", [128, 3, CT + 1, 2])
    fve = sb("fve", [128, 3, CT + 1])
    frs = sb("frs", [128, 3, CT + 1])
    fnm = sb("fnm", [128, 3, CT + 1])
    half = sb("half", [128, CT + 1])
    b1e = sb("b1e", [128, 2, 4])

    def pb(name):
        return ctx.enter_context(nc.psum_tensor(name, [128, 512], F32))

    bI = [pb("bI0"), pb("bI1")]
    bX = pb("bX")
    bH = [pb("bH0"), pb("bH1"), pb("bH2")]
    bO = [pb("bO0"), pb("bO1")]

    s_cs = sem("s_search_consts")
    s_c = sem("s2_consts")
    s_l = sem("s_logits")
    s_copy = sem("s_acc_copied")
    s_half = sem("s_half")
    s_d = sem("s_dve")
    s_pe = sem("s_routing_psum")
    s_sh = sem("s_shifted")
    s_ex = sem("s_exp2")
    s_est = sem("s_exp_stored")
    s_eld = sem("s_exp_loaded")
    s_cnt = sem("s_count")
    s_sum = sem("s_count_sum")
    s_cand = sem("s_cand")
    s_inc = sem("s_inc")
    s_base = sem("s_base")
    s_thr = sem("s_thr")
    s_tld = sem("s_thr_psum")
    s_tab = sem("s_table")
    s_o0 = sem("s_onehot_half")
    s_oh = sem("s_onehot")
    s_ix = sem("s_index_psum")
    s_ie = sem("s_index_copied")
    s_loc = sem("s_loc")
    s_idx = sem("s_idx")
    s_g = [[sem(f"s_gathered{p}{u}") for u in range(2)] for p in range(2)]
    s_w = [sem(f"s_weights{p}") for p in range(2)]
    s_xp = sem("s_xg_turned")
    s_xe = sem("s_xgT")
    s_h = sem("s_h_psum")
    s_held = sem("s_held")
    s_b1 = sem("s_b1")
    s_side = sem("s_side")
    s_ge = sem("s_gelu")
    s_o = sem("s_o_psum")
    s_yb = sem("s_y_biased")
    s_yw = sem("s_y_weighted")
    s_sc = [sem(f"s_scattered{p}") for p in range(2)]
    s_fl = [sem(f"s_fin_loaded{n}") for n in range(4)]
    s_f6 = sem("s_fin_stats")
    s_fr = sem("s_fin_rstd")
    s_fn = sem("s_fin_nmr")
    s_fa = sem("s_fin_act")
    s_fp = sem("s_fin_pool")
    s_fv = sem("s_fin_dve")
    s_fs = [sem(f"s_fin_stored{n}") for n in range(3)]

    consts = [(tri, "tri"), (reset, "reset"), (slots, "slots"),
              (slot1, "slot1"), (iota, "iota"), (b1, "b1"), (b2, "b2")]
    search_consts = [(ident, "ident"), (rowbase, "rowbase"), (blk, "blk"), (steps, "steps"), (owner, "owner")]

    def w(eng, s, v):
        if isinstance(v, int) and v <= 0:
            return
        eng.wait_ge(s, v)

    def pipeline(eng, body):
        body(-1, 1)
        for p in range(2):
            body(0, p)
        with eng.Fori(1, NEXP // 2 - 1) as q:
            for p in range(2):
                body(q, p)
        for p in range(2):
            body(NEXP // 2 - 1, p)
        body(NEXP // 2, 0)

    def stages(q, p, u):
        if not isinstance(q, int):
            return [True] * 4
        e = 2 * q + p
        n = 2 * e + u
        return [0 <= n < 2 * NEXP, 0 <= n - 1 < 2 * NEXP, 0 <= n + 1 < 2 * NEXP, 0 <= e + 1 + u < NEXP]

    def piece(d, n):
        return d[0:128 * FR, :].rearrange("(p t) e -> p t e", p=128)[:, n * CT:(n + 1) * CT, :]

    def tokens(n):
        return [(128, t) for t in range(CT)] + ([(REST, CT)] if n == NCH - 1 else [])

    block = ctx.enter_context(nc.Block())

    @block.sync
    def _(sp):
        sp.dma_start(lrow[:], lg_dram.rearrange("(p t) e -> p (t e)", p=R)).then_inc(s_l, 16)
        for t, n in search_consts:
            sp.dma_start(t[:], A[n]).then_inc(s_cs, 16)
        for t, n in consts:
            sp.dma_start(t[:], A[n]).then_inc(s_c, 16)

        def weights(q, p):
            e = 2 * q + p
            w(sp, s_o, 2 * (e - 1))
            sp.dma_start(w1[:, p, :], A["W1"][bass.ds(e, 1)].rearrange("e d f -> d (e f)")).then_inc(s_w[p], 16)
            sp.dma_start(w2[:, p], A["W2"][bass.ds(e, 1)].rearrange("e (c f) d -> f (e c) d", c=4)).then_inc(s_w[p], 16)

        weights(0, 0)
        weights(0, 1)
        sp.wait_ge(s_ex, 1)
        sp.dma_start(e_dram.rearrange("e (p t) -> p e t", p=R), pr[:]).then_inc(s_est, 16)
        sp.wait_ge(s_est, 16)
        sp.dma_start(pe_[:], e_dram.rearrange("e (c m) -> (e c) m", c=16)).then_inc(s_eld, 16)
        sp.dma_start(acc_dram, h2_dram).then_inc(s_copy, 16)
        with sp.Fori(1, NEXP // 2) as q:
            for p in range(2):
                weights(q, p)
        for p in range(2):
            sp.wait_ge(s_sc[p], 16 * NBLK * NEXP)

        def normed(n):
            for s in (s_fa, s_fp, s_fv):
                sp.wait_ge(s, n + 1)

        def store(n):
            normed(n)
            sp.dma_start(piece(out, n), fout[:, n % 3, 0:CT]).then_inc(s_fs[n % 3], 16)

        for n in range(NCH):
            if n >= 4:
                normed(n - 4)
            sp.dma_start(fin[:, n % 4, 0:CT], piece(acc_dram, n)).then_inc(s_fl[n % 4], 16)
            if n == NCH - 1:
                sp.dma_start(fin[0:REST, n % 4, CT], acc_dram[128 * FR:NTOK, :]).then_inc(s_fl[n % 4], 16)
            if n >= 3:
                store(n - 3)
        for n in range(NCH - 3, NCH):
            store(n)
        sp.dma_start(out[128 * FR:NTOK, :], fout[0:REST, (NCH - 1) % 3, CT]).then_inc(s_fs[(NCH - 1) % 3], 16)
        for k in range(3):
            sp.wait_ge(s_fs[k], 16 * (len(range(k, NCH, 3)) + (k == (NCH - 1) % 3)))

    @block.gpsimd
    def _(pool):
        nc.gpsimd.memset(half[:], -0.5).then_inc(s_half, 1)
        nc.gpsimd.memset(fve[:], 1.0).then_inc(s_half, 1)
        nc.gpsimd.memset(ones[:], 1.0).then_inc(s_half, 1)
        pool.wait_ge(s_copy, 16)
        pool.wait_ge(s_half, 3)

        def held():
            pool.sem_inc(s_held, 1)

        def gather(q, p):
            e = 2 * q + p
            pool.wait_ge(s_idx, e + 2)
            w(pool, s_xp, 2 * e)
            held()
            for k in range(NB):
                nc.gpsimd.indirect_dma_start(
                    out=xg[:, 1 - p, k, :], out_offset=None, in_=h2_dram,
                    in_offset=bass.IndirectOffsetOnAxis(ap=idx[:, 1 - p, k:k + 1], axis=0),
                ).then_inc(s_g[1 - p][k // NBLK], 16)

        def body(q, p):
            e = 2 * q + p
            for u in range(2):
                first, second, turn, index = stages(q, p, u)
                if u == 0 and index:
                    gather(q, p)
                if second:
                    pool.wait_ge(s_yw, 2 * e + u)
                    if u == 1:
                        for v in range(2):
                            w(pool, s_sc[v], 16 * NBLK * e)
                    held()
                    for k in range(NBLK):
                        nc.gpsimd.indirect_dma_start(
                            out=acc_dram, in_=yw[:, 1 - u, k, :], in_offset=None,
                            out_offset=bass.IndirectOffsetOnAxis(ap=sidx[:, 1 - u, k:k + 1], axis=0),
                            compute_op=ALU.add,
                        ).then_inc(s_sc[1 - u], 16)

        pipeline(pool, body)
        for n in range(NCH):
            pool.wait_ge(s_f6, 3 * n + 3)
            nc.gpsimd.tensor_tensor(frs[:, n % 3, :], fve[:, n % 3, :], half[:], ALU.pow).then_inc(s_fr, 1)
            pool.wait_ge(s_fr, n + 1)
            if n >= 3:
                pool.wait_ge(s_fs[n % 3], 16 * (n // 3))
            for t in range(ON_ACT, ON_ACT + ON_POOL):
                ins = nc.gpsimd.tensor_scalar(fout[:, n % 3, t, :], fin[:, n % 4, t, :], fmv[:, n % 3, t, 0:1],
                                              frs[:, n % 3, t:t + 1], ALU.subtract, ALU.mult)
            ins.then_inc(s_fp, 1)

    @block.tensor
    def _(pe):
        mm = nc.tensor.matmul
        pe.wait_ge(s_cs, 16 * len(search_consts))
        pe.wait_ge(s_half, 3)
        pe.wait_ge(s_d, D_MAX)
        nc.tensor.transpose(bX[0:NEXP, 0:R], mx[:], ident[0:R, 0:R]).then_inc(s_pe, 1)
        pe.wait_ge(s_d, D_DIAG)
        mm(bX[0:R, 0:NEXP], ones[0:NEXP, :], dg[:], start=True, stop=True).then_inc(s_pe, 1)
        pe.wait_ge(s_d, D_TOT)
        mm(bX[0:R, 0:NEXP], ones[0:R, :], tot[:], start=True, stop=True).then_inc(s_pe, 1)
        def totals(i, n):
            pe.wait_ge(s_cnt, i + 1)
            mm(bI[0][:, 0:n], blk[:], cnt[:, 0:n], start=True, stop=True).then_inc(s_sum, 1)

        with pe.Fori(0, HI_ROUNDS) as i:
            totals(i, 3)
        totals(HI_ROUNDS, 1)
        with pe.Fori(HI_ROUNDS + 1, ROUNDS + 1) as i:
            totals(i, 3)
        pe.wait_ge(s_thr, 1)
        mm(bX[0:R, 0:2 * NEXP], ones[:], halves[:].rearrange("p a e -> p (a e)"), start=True, stop=True).then_inc(s_tld, 1)
        pe.wait_ge(s_d, D_TIES)
        pe.wait_ge(s_c, 16 * len(consts))
        mm(bX[0:R, 0:NEXP], ones[0:R, :], ng[:], start=True, stop=False)
        mm(bX[0:R, 0:NEXP], tri[:], te[:], start=False, stop=True).then_inc(s_pe, 1)
        pe.wait_ge(s_d, D_SEL)
        mm(bX[0:R, 0:NEXP], tri[:], te[:], start=True, stop=True).then_inc(s_pe, 1)
        pe.wait_ge(s_tab, 1)

        def body(q, p):
            e = 2 * q + p

            def tables(k):
                if k == 0:
                    pe.wait_ge(s_oh, e + 2)
                w(pe, s_ie, 4 * (e + 1) + k - 1)
                for c in range(2):
                    at = (2 * k + c) * 128
                    ins = mm(bI[k % 2][:, c * TAB:(c + 1) * TAB], oh[:, at:at + 128], tab[:, bass.ds((e + 1) * TAB, TAB)],
                             start=True, stop=True)
                ins.then_inc(s_ix, 1)

            def turned(u):
                n = 2 * e + u + 1
                if u == 0:
                    par, seen = p, q + 1
                else:
                    par, seen = 1 - p, q + p + 1
                pe.wait_ge(s_g[par][1 - u], seen * 16 * NBLK)
                w(pe, s_xe, n)
                for k in range(NBLK):
                    ins = nc.tensor.transpose(bX[:, k * 128:(k + 1) * 128], xg[:, par, (1 - u) * NBLK + k, :], ident[:])
                ins.then_inc(s_xp, 1)

            def layer1(u, f):
                n = 2 * e + u
                if f == 0:
                    if u == 0:
                        pe.wait_ge(s_w[p], (q + 1) * 32)
                    pe.wait_ge(s_xe, n + 1)
                if f % 3 == 0:
                    w(pe, s_ge, 4 * n + f // 3)
                mm(bH[f % 3][:], w1[:, p, f * 128:(f + 1) * 128], xgT[:, u, :], start=True, stop=True).then_inc(s_h, 1)

            def layer2(u, k):
                n = 2 * e + u - 1
                par = p if u == 1 else 1 - p
                if k == 0:
                    pe.wait_ge(s_ge, 4 * n + 4)
                    w(pe, s_yb, n - 1)
                for f in range(4):
                    ins = mm(bO[1 - u][:, k * E:(k + 1) * E], hT[:, 1 - u, f, k * 128:(k + 1) * 128], w2[:, par, f, :],
                             start=(f == 0), stop=(f == 3))
                if k == NBLK - 1:
                    ins.then_inc(s_o, 1)

            for u in range(2):
                first, second, turn, index = stages(q, p, u)
                index = index and u == 0
                if index:
                    tables(0)
                    tables(1)
                for k in range(4):
                    if first:
                        layer1(u, k)
                    if index and k < 2:
                        tables(2 + k)
                    if second:
                        layer2(u, k)
                    if turn and k == 2:
                        turned(u)

        pipeline(pe, body)

    @block.scalar
    def _(act):
        activation = nc.scalar.activation
        act.wait_ge(s_sh, 1)
        activation(pr[:], pr[:], ACT.Exp).then_inc(s_ex, 1)
        act.wait_ge(s_c, 16 * len(consts))

        def body(q, p):
            e = 2 * q + p

            def gelu(u, f):
                n = 2 * e + u
                if u == 0 and f == 0:
                    activation(b1e[:, p, :], b1[:, bass.ds(e * 4, 4)], ACT.Copy).then_inc(s_b1, 1)
                    act.wait_ge(s_b1, e + 1)
                act.wait_ge(s_h, 4 * n + f + 1)
                if f == 0:
                    w(act, s_o, n - 1)
                activation(hT[:, u, f, :], bH[f % 3][:], ACT.Gelu,
                           bias=b1e[:, p, f:f + 1]).then_inc(s_ge, 1)

            def tables(k):
                act.wait_ge(s_ix, 4 * (e + 1) + k + 1)
                if k == 0:
                    w(act, s_idx, e + 1)
                activation(tabs[:, 2 * k:2 * k + 2, :].rearrange("p k c -> p (k c)"), bI[k % 2][:, 0:2 * TAB],
                           ACT.Copy).then_inc(s_ie, 1)

            for u in range(2):
                first, second, turn, index = stages(q, p, u)
                index = index and u == 0
                if index:
                    tables(0)
                    tables(1)
                for k in range(4):
                    if first:
                        gelu(u, k)
                    if index and k < 2:
                        tables(2 + k)

        pipeline(act, body)
        for n in range(NCH):
            act.wait_ge(s_fn, n + 1)
            if n >= 3:
                act.wait_ge(s_fs[n % 3], 16 * (n // 3))
            for t in range(ON_ACT):
                ins = activation(fout[:, n % 3, t, :], fin[:, n % 4, t, :], ACT.Identity, bias=fnm[:, n % 3, t:t + 1],
                                 scale=frs[:, n % 3, t:t + 1])
            ins.then_inc(s_fa, 1)

    @block.vector
    def _(dve):
        V = nc.vector
        done = [0]

        def link(ins):
            done[0] += 1
            ins.then_inc(s_d, 1)
            dve.wait_ge(s_d, done[0])

        def over(t):
            return t[:].unsqueeze(2).to_broadcast([R, NEXP, R])

        def flat(t):
            return t[:].rearrange("p e t -> p (e t)")

        dve.wait_ge(s_l, 16)
        raw = lrow[:].rearrange("p (t e) -> p e t", e=NEXP)
        link(V.tensor_reduce(mx[:], raw, AX.X, ALU.max))
        assert done[0] == D_MAX
        dve.wait_ge(s_pe, 1)
        link(V.tensor_reduce(gm[:], bX[0:NEXP, 0:R], AX.X, ALU.max))
        dve.wait_ge(s_cs, 16 * len(search_consts))
        link(V.tensor_scalar(dg[:], ident[0:NEXP, 0:NEXP], gm[:, 0:1], None, ALU.mult))
        assert done[0] == D_DIAG
        dve.wait_ge(s_pe, 2)
        link(V.tensor_copy(mb[:], bX[0:R, 0:NEXP]))
        V.tensor_tensor(pr[:], raw, over(mb), ALU.subtract).then_inc(s_sh, 1)
        dve.wait_ge(s_ex, 1)
        link(V.tensor_reduce(tot[:], pr[:], AX.X, ALU.add))
        assert done[0] == D_TOT
        dve.wait_ge(s_pe, 3)
        link(V.reciprocal(rtot[:], bX[0:R, 0:NEXP]))
        link(V.tensor_tensor(tab[:].rearrange("p (e c) -> p e c", c=TAB)[:, :, R:2 * R], pr[:], over(rtot), ALU.mult))
        V.tensor_copy(tab[:].rearrange("p (e c) -> p e c", c=TAB)[:, :, 2 * R],
                      rowbase[:, 0:1].to_broadcast([R, NEXP]))

        dve.wait_ge(s_eld, 16)
        V.tensor_copy(key[:], pe_[:].bitcast(U16).rearrange("p (n k) -> p k n", k=2))
        V.memset(base[:], 0.0)
        V.memset(need[:], CAP - 0.5)
        link(V.tensor_copy(cand[:], steps[:, 3:6]))

        def count(keys, n):
            for j in range(n):
                ins = V.tensor_scalar(ge[:, j, :], keys, cand[:, j:j + 1], 0.0, ALU.is_ge, ALU.add, accum_out=cnt[:, j:j + 1])
            ins.then_inc(s_cnt, 1)

        def search(i, r, keys):
            dve.wait_ge(s_cand, r)
            count(keys, 3)
            dve.wait_ge(s_sum, i + 1)
            V.scalar_tensor_tensor(junk[:], bI[0][:, 0:3], need[:, 0:1], steps[:, bass.ds(r * 6, 3)], ALU.is_ge,
                                   ALU.mult, accum_out=inc[:]).then_inc(s_inc, 1)
            dve.wait_ge(s_inc, r + 1)
            V.scalar_tensor_tensor(cand[:], steps[:, bass.ds(r * 6 + 9, 3)], inc[:, 0:1],
                                   base[:, 0:1].to_broadcast([128, 3]), ALU.add, ALU.add).then_inc(s_cand, 1)
            dve.wait_ge(s_cand, r + 1)
            V.tensor_tensor(base[:], base[:], inc[:], ALU.add).then_inc(s_base, 1)

        search(0, 0, key[:, 1, :])
        with dve.Fori(1, HI_ROUNDS) as i:
            search(i, i, key[:, 1, :])
        dve.wait_ge(s_base, HI_ROUNDS)
        V.tensor_scalar(halves[:, 1, :], owner[:], base[:, 0:1], None, ALU.mult)
        V.scalar_tensor_tensor(low[:], key[:, 1, :], base[:, 0:1], key[:, 0, :], ALU.is_equal, ALU.mult)
        link(V.tensor_scalar(cand[:, 0:1], base[:], 1.0, None, ALU.add))
        count(key[:, 1, :], 1)
        dve.wait_ge(s_sum, HI_ROUNDS + 1)
        V.tensor_scalar(need[:], bI[0][:, 0:1], -1.0, CAP - 0.5, ALU.mult, ALU.add)
        V.memset(base[:], 0.0)
        link(V.tensor_copy(cand[:], steps[:, HI_ROUNDS * 6 + 3:HI_ROUNDS * 6 + 6]))
        with dve.Fori(HI_ROUNDS, ROUNDS) as i:
            search(i + 1, i, low[:])
        dve.wait_ge(s_base, ROUNDS)
        V.tensor_scalar(halves[:, 0, :], owner[:], base[:, 0:1], None, ALU.mult).then_inc(s_thr, 1)

        dve.wait_ge(s_tld, 1)
        link(V.tensor_copy(tb[:].bitcast(U16).rearrange("p (e a) -> p a e", a=2),
                           bX[0:R, 0:2 * NEXP].rearrange("p (a e) -> p a e", a=2)))
        dve.wait_ge(s_c, 16 * len(consts))
        V.tensor_tensor(gt[:], pr[:], over(tb), ALU.is_gt)
        link(V.tensor_tensor(eq[:], pr[:], over(tb), ALU.is_equal))
        V.tensor_reduce(ng[:], gt[:], AX.X, ALU.add)
        link(V.tensor_tensor_scan(flat(run), reset[:], flat(eq), 0.0, ALU.mult, ALU.add))
        link(V.tensor_copy(te[:], run[:, :, R - 1]))
        assert done[0] == D_TIES
        dve.wait_ge(s_pe, 4)
        link(V.tensor_scalar(room[:], bX[0:R, 0:NEXP], -1.0, float(CAP), ALU.mult, ALU.add))
        link(V.tensor_tensor(run[:], run[:], over(room), ALU.is_le))
        link(V.tensor_tensor(run[:], run[:], eq[:], ALU.mult))
        link(V.tensor_tensor(gt[:], gt[:], run[:], ALU.add))
        link(V.tensor_tensor_scan(flat(run), reset[:], flat(gt), 0.0, ALU.mult, ALU.add))
        link(V.tensor_copy(te[:], run[:, :, R - 1]))
        assert done[0] == D_SEL
        dve.wait_ge(s_pe, 5)
        link(V.tensor_copy(start[:], bX[0:R, 0:NEXP]))
        V.tensor_tensor(end[:], start[:], te[:], ALU.add)
        link(V.tensor_tensor(run[:], run[:], over(start), ALU.add))
        V.tensor_tensor(tab[:].rearrange("p (e c) -> p e c", c=TAB)[:, :, 0:R], run[:], gt[:], ALU.mult).then_inc(s_tab, 1)
        dve.wait_ge(s_tab, 1)

        def onehot(x):
            w(dve, s_ix, 4 * x)
            V.tensor_scalar(oh0[:], slots[:], start[:, bass.ds(x, 1)], None, ALU.is_ge).then_inc(s_o0, 1)
            dve.wait_ge(s_o0, x + 1)
            V.scalar_tensor_tensor(oh[:], slots[:], end[:, bass.ds(x, 1)], oh0[:], ALU.is_lt,
                                   ALU.mult).then_inc(s_oh, 1)

        def body(q, p):
            e = 2 * q + p
            n = 1 - p

            def numbers():
                if not isinstance(e, int) or e >= 1:
                    w(dve, s_sc[1], 16 * NBLK * (e - 1))
                    V.tensor_copy(sidx[:, 1, :], idx[:, n, NBLK:NB])
                    V.tensor_copy(swgt[:], wgt[:, n, NBLK:NB]).then_inc(s_side, 1)
                    dve.wait_ge(s_side, e)
                for k in range(NB):
                    if k % 2 == 0:
                        dve.wait_ge(s_ie, 4 * (e + 1) + k // 2 + 1)
                    if k == 0:
                        w(dve, s_idx, e + 1)
                    V.scalar_tensor_tensor(jk[:, k, :], tabs[:, k, 0:R], slot1[:, k:k + 1], iota[:], ALU.is_equal,
                                           ALU.mult, accum_out=loc[:, k:k + 1])
                    ins = V.scalar_tensor_tensor(tabs[:, k, R:2 * R], tabs[:, k, 0:R], slot1[:, k:k + 1],
                                                 tabs[:, k, R:2 * R], ALU.is_equal, ALU.mult,
                                                 accum_out=wgt[:, n, k:k + 1])
                ins.then_inc(s_loc, 1)
                dve.wait_ge(s_loc, e + 2)
                V.tensor_tensor(idx[:, n, :], loc[:], tabs[:, :, 2 * R], ALU.add).then_inc(s_idx, 1)

            def turned(u):
                m = 2 * e + u + 1
                dve.wait_ge(s_xp, m + 1)
                w(dve, s_h, 4 * (m - 1))
                V.tensor_copy(xgT[:, 1 - u, :], bX[:]).then_inc(s_xe, 1)

            def weighted(u):
                m = 2 * e + u - 1
                x = e if u == 1 else e - 1
                dve.wait_ge(s_o, m + 1)
                w(dve, s_yw, m)
                V.tensor_tensor(yb[:], bO[1 - u][:].rearrange("p (k c) -> p k c", c=E),
                                b2[:, bass.ds(x * E, E)].unsqueeze(1).to_broadcast([128, NBLK, E]),
                                ALU.add).then_inc(s_yb, 1)
                dve.wait_ge(s_yb, m + 1)
                w(dve, s_sc[1 - u], 16 * NBLK * x)
                if u == 1:
                    V.tensor_copy(sidx[:, 0, :], idx[:, p, 0:NBLK])
                    by = wgt[:, p, 0:NBLK]
                else:
                    if isinstance(e, int) and e + 1 >= NEXP:
                        V.tensor_copy(sidx[:, 1, :], idx[:, n, NBLK:NB])
                        by = wgt[:, n, NBLK:NB]
                    else:
                        by = swgt[:]
                V.tensor_tensor(yw[:, 1 - u], yb[:], by.unsqueeze(2).to_broadcast([128, NBLK, E]),
                                ALU.mult).then_inc(s_yw, 1)

            for u in range(2):
                first, second, turn, index = stages(q, p, u)
                if u == 0 and index:
                    numbers()
                if u == 1 and index:
                    onehot(e + 2)
                if turn:
                    turned(u)
                if second:
                    weighted(u)

        onehot(0)
        pipeline(dve, body)
        dve.wait_ge(s_half, 2)

        def stats(n):
            dve.wait_ge(s_fl[n % 4], 16 * (n // 4 + 1 + (n == NCH - 1)))
            for p, t in tokens(n):
                ins = V.bn_stats(f6[0:p, t, :], fin[0:p, n % 4, t, :])
            ins.then_inc(s_f6, 1)
            if n >= 3:
                dve.wait_ge(s_fa, n - 2)
                dve.wait_ge(s_fp, n - 2)
                dve.wait_ge(s_fv, n - 2)
            dve.wait_ge(s_f6, 3 * n + 1)
            for p, t in tokens(n):
                ins = V.bn_aggr(fmv[0:p, n % 3, t, :], f6[0:p, t, :])
            ins.then_inc(s_f6, 1)
            dve.wait_ge(s_f6, 3 * n + 2)
            if n == NCH - 1:
                V.tensor_scalar(fve[0:REST, n % 3, CT:CT + 1], fmv[0:REST, n % 3, CT:CT + 1, 1], LN_EPS, None, ALU.add)
            V.tensor_scalar(fve[:, n % 3, 0:CT], fmv[:, n % 3, 0:CT, 1], LN_EPS, None, ALU.add).then_inc(s_f6, 1)

        stats(0)
        for n in range(NCH):
            if n + 1 < NCH:
                stats(n + 1)
            dve.wait_ge(s_fr, n + 1)
            V.scalar_tensor_tensor(fnm[:, n % 3, 0:CT], fmv[:, n % 3, 0:CT, 0], -1.0, frs[:, n % 3, 0:CT], ALU.mult,
                                   ALU.mult).then_inc(s_fn, 1)
            if n >= 3:
                dve.wait_ge(s_fs[n % 3], 16 * (n // 3))
            for p, t in tokens(n)[ON_ACT + ON_POOL:]:
                ins = V.tensor_scalar(fout[0:p, n % 3, t, :], fin[0:p, n % 4, t, :], fmv[0:p, n % 3, t, 0:1],
                                      frs[0:p, n % 3, t:t + 1], ALU.subtract, ALU.mult)
            ins.then_inc(s_fv, 1)


D_MAX, D_DIAG, D_TOT, D_TIES, D_SEL = 1, 3, 5, 14, 20


def program(nc, A, out):
    h2_dram = nc.dram_tensor("h2_rows", [NTOK, E], F32, kind=A["kind"]).ap()
    lg_dram = nc.dram_tensor("logit_rows", [NTOK, NEXP], F32, kind=A["kind"]).ap()
    e_dram = nc.dram_tensor("exp_rows", [NEXP, NTOK], F32, kind="Internal").ap()
    acc_dram = nc.dram_tensor("acc_rows", [NTOK, E], F32, kind=A["kind"]).ap()
    with ExitStack() as ctx:
        tower_tokens(nc, ctx, A, h2_dram, lg_dram)
    with ExitStack() as ctx:
        experts(nc, ctx, A, h2_dram, lg_dram, e_dram, acc_dram, out)


def layouts(i):
    f = {k: np.asarray(v) for k, v in i.items()}
    x = f["x"]
    plain = x.reshape(NI, CH, GRID, PATCH, GRID, PATCH).transpose(1, 3, 5, 0, 2, 4).reshape(KP, NI, TOK)
    pad = np.pad(x, ((0, 0), (0, 0), (SHIFT, SHIFT), (SHIFT, SHIFT)))
    shifted = pad.reshape(NI, CH, ZG, PATCH, ZG, PATCH).transpose(1, 3, 5, 0, 2, 4).reshape(KP, NI, ZT)

    def patches(g):
        return g.reshape(VER, CH, GRID, PATCH, GRID, PATCH).transpose(1, 3, 5, 0, 2, 4).reshape(KP, VER, TOK)

    def heads(scalar, point):
        o = np.zeros(scalar.shape[:-1] + (HEADS, 32), scalar.dtype)
        o[..., 0:DH] = scalar.reshape(scalar.shape[:-1] + (HEADS, DH))
        o[..., DH:DH + PP] = point.reshape(point.shape[:-1] + (HEADS, PP))
        return o.reshape(scalar.shape[:-1] + (2, KP))

    def column(v):
        return v.reshape(-1, 1)

    edge = np.full(ZG, 2.0)
    edge[[0, -1]] = 1.0
    row = np.arange(KP) % 32
    cst = np.stack([0.25 * (row < DH), 2.0 * ((row >= DH) & (row < DH + PP)), row == 28, row == 29, row == 30], 1)
    selm = np.zeros((KP, KP))
    for p in range(KP):
        if DH <= row[p] < DH + PP:
            selm[p, p - row[p] + 28] = 1.0
    small = {
        "columns": np.concatenate([
            column(f["L0_tok_b"]), column(f["L0_attn_ln_g"]), column(f["L0_attn_ln_b"]), column(f["L0_attn_bv"]),
            column(f["L0_attn_bo"]), heads(f["L0_attn_bq"], f["L0_attn_bqp"]).T,
            heads(f["L0_attn_bk"], f["L0_attn_bkp"]).T, np.repeat(f["L0_attn_pscale"].reshape(2, 4).T, 32, 0),
            np.zeros((KP, 1), np.float32)], 1),
        "wq": heads(f["L0_attn_wq"], f["L0_attn_wqp"]), "wk": heads(f["L0_attn_wk"], f["L0_attn_wkp"]),
        "wv": f["L0_attn_wv"], "wo": f["L0_attn_wo"], "wr": f["L0_ffn_Wr"], "ident": np.eye(KP), "selm": selm, "cst": cst,
        "qcst": np.broadcast_to(np.concatenate([cst[:32, 0], cst[:32, 1]])[None], (KP, 64)),
        "ps8": np.broadcast_to(f["L0_attn_pscale"][None], (KP, HEADS)),
        "zwt": np.broadcast_to((1.0 + np.outer(edge, edge)).reshape(1, ZT), (KP, ZT)),
    }
    token = {"w": f["L0_tok_W"].reshape(E, VER, KP).transpose(2, 1, 0), "gamma": patches(f["L0_tok_gamma"]),
             "beta": patches(f["L0_tok_beta"])}

    def packed(widths, arrays):
        return np.concatenate([np.asarray(arrays[n], np.float32).reshape(KP, width) for n, width in widths.items()], 1)

    step = np.concatenate([4.0 ** np.arange(6, -1, -1), 4.0 ** np.arange(7, -1, -1), [0.0]])
    steps = step[:, None] * np.array([1, 1, 1, 1, 2, 3])
    c = lambda a: np.ascontiguousarray(a, np.float32)
    return {
        "xz": np.concatenate([plain, shifted], 2).reshape(KP, NI * XZ),
        "pack": packed(PACK, small), "tokpack": packed(TOKPACK, token),
        "row1": c(np.stack([np.arange(KP) == 29, np.arange(KP) == 30])[None]),
        "ident": c(np.eye(KP)), "tri": c(np.triu(np.ones((R, R)), 1)),
        "blk": c(np.kron(np.eye(NEXP), np.ones((16, 16)))),
        "reset": c(np.broadcast_to((np.arange(NEXP * R) % R != 0)[None], (R, NEXP * R))),
        "slots": c(np.broadcast_to(np.arange(CAP)[None], (R, CAP))),
        "slot1": c(1 + np.arange(128)[:, None] + 128 * np.arange(CAP // 128)[None]),
        "iota": c(np.broadcast_to(np.arange(R)[None], (128, R))),
        "rowbase": c(R * np.arange(R)[:, None]),
        "owner": c(np.kron(np.eye(NEXP), np.eye(16)[:, 0:1])),
        "steps": c(np.broadcast_to(steps.reshape(1, -1), (128, steps.size))),
        "b1": f["L0_ffn_b1"].reshape(NEXP * 4, 128).T,
        "b2": np.broadcast_to(f["L0_ffn_b2"].reshape(1, NEXP * E), (128, NEXP * E)),
        "W1": f["L0_ffn_W1"], "W2": f["L0_ffn_W2"],
    }


def kernel(**inputs):
    import concourse.bacc as _bacc
    from concourse.bass_utils import run_bass_kernel_spmd as _run

    nc = _bacc.Bacc("TRN2", target_bir_lowering=False, num_devices=1)
    arrays, A = {}, {"kind": KIND}
    for name, a in layouts(inputs).items():
        a = np.ascontiguousarray(a)
        arrays[f"in_{name}"] = a
        A[name] = nc.dram_tensor(f"in_{name}", a.shape, mybir.dt.from_np(a.dtype), kind="ExternalInput").ap()
    out = nc.dram_tensor("out_tokens", [NTOK, E], F32, kind="ExternalOutput").ap()
    program(nc, A, out)
    r = _run(nc, [arrays], core_ids=[0])
    return r.results[0]["out_tokens"].reshape(NI, TOK, E)
```
